# Optimizing a Trainium2 kernel written in Bass

```python
import numpy as np
import jax
import jax.numpy as jnp

def _softmax(x, axis=-1):
    return jax.nn.softmax(x, axis=axis)

def _gelu(x):
    return jax.nn.gelu(x, approximate=True)

def _silu(x):
    return jax.nn.silu(x)

def _sigmoid(x):
    return jax.nn.sigmoid(x)

def _layernorm(x, axis=-1, eps=1e-05):
    m = jnp.mean(x, axis=axis, keepdims=True)
    v = jnp.var(x, axis=axis, keepdims=True)
    return (x - m) / jnp.sqrt(v + eps)

def _scatter_add(tgt, idx, src, axis=0):
    return tgt.at[idx].add(src)

def _segment_sum(src, seg, n):
    return jax.ops.segment_sum(src, seg, n)
kernel_name = 'mk_hybrid_d2_jaxref_r8_ac4a48'

def setup_inputs(seed: int=0):
    np.random.seed(seed)
    _w = jnp.asarray

    def _L0_attn_a_setup():
        import jax, jax.numpy as jnp
        import numpy as np
        import math
        EMB = 128
        HEADS = 16
        W_STD = 0.02
        key = jax.random.key(seed)
        kx, kk, kq, kv, ku = jax.random.split(key, 5)
        b, t, e = (2, 256, EMB)
        x = jax.random.normal(kx, (b, t, e), dtype=jnp.float32)
        Wk = jax.random.normal(kk, (e, e), dtype=jnp.float32) * W_STD
        Wq = jax.random.normal(kq, (e, e), dtype=jnp.float32) * W_STD
        lim = 1.0 / math.sqrt(e)
        Wv = jax.random.uniform(kv, (e, e), dtype=jnp.float32, minval=-lim, maxval=lim)
        Wu = jax.random.uniform(ku, (e, e), dtype=jnp.float32, minval=-lim, maxval=lim)
        bu = jnp.zeros((e,), dtype=jnp.float32)
        return {'x': x, 'Wk': Wk, 'Wq': Wq, 'Wv': Wv, 'Wu': Wu, 'bu': bu}
    _L0_attn_a_in = _L0_attn_a_setup()

    def _L0_attn_b_setup():
        import jax, jax.numpy as jnp
        import numpy as np
        D_MODEL = 128
        D_STATE = 16
        D_CONV = 4
        EXPAND = 2
        D_INNER = EXPAND * D_MODEL
        DT_RANK = (D_MODEL + 15) // 16
        BATCH, SEQ_LEN = (2, 256)
        LN_EPS = 1e-05

        def _silu(v):
            return v * jax.nn.sigmoid(v)

        def _selective_scan(x, delta, A, B, C, Dp):
            b, L, d_inner = x.shape
            d_state = A.shape[1]
            xT = jnp.swapaxes(x, 0, 1)
            dT = jnp.swapaxes(delta, 0, 1)
            BT = jnp.swapaxes(B, 0, 1)
            CT = jnp.swapaxes(C, 0, 1)

            def step(h, inp):
                x_t, d_t, B_t, C_t = inp
                dA = jnp.exp(d_t[:, :, None] * A[None, :, :])
                h = dA * h + (d_t * x_t)[:, :, None] * B_t[:, None, :]
                y_t = jnp.einsum('bds,bs->bd', h, C_t)
                return (h, y_t)
            h0 = jnp.zeros((b, d_inner, d_state), x.dtype)
            _, yT = jax.lax.scan(step, h0, (xT, dT, BT, CT))
            y = jnp.swapaxes(yT, 0, 1)
            return y + x * Dp[None, None, :]
        if __name__ == '__main__':
            out = reference(**setup_inputs())
            print(out.shape, out.dtype)
        key = jax.random.key(seed)
        ks = jax.random.split(key, 10)
        s = lambda n: 1.0 / np.sqrt(n)
        x = jax.random.normal(ks[0], (BATCH, SEQ_LEN, D_MODEL), dtype=jnp.float32)
        norm_g = jnp.ones((D_MODEL,), jnp.float32)
        norm_b = jnp.zeros((D_MODEL,), jnp.float32)
        in_proj_w = jax.random.normal(ks[1], (2 * D_INNER, D_MODEL), jnp.float32) * s(D_MODEL)
        conv_w = jax.random.normal(ks[2], (D_INNER, D_CONV), jnp.float32) * s(D_CONV)
        conv_b = jax.random.normal(ks[3], (D_INNER,), jnp.float32) * 0.02
        x_proj_w = jax.random.normal(ks[4], (DT_RANK + 2 * D_STATE, D_INNER), jnp.float32) * s(D_INNER)
        dt_proj_w = jax.random.normal(ks[5], (D_INNER, DT_RANK), jnp.float32) * s(DT_RANK)
        dt_proj_b = jax.random.normal(ks[6], (D_INNER,), jnp.float32) * 0.02
        log_A = jnp.broadcast_to(jnp.log(jnp.arange(1, D_STATE + 1, dtype=jnp.float32))[None, :], (D_INNER, D_STATE))
        Dp = jnp.ones((D_INNER,), jnp.float32)
        out_proj_w = jax.random.normal(ks[7], (D_MODEL, D_INNER), jnp.float32) * s(D_INNER)
        return {'x': x, 'norm_g': norm_g, 'norm_b': norm_b, 'in_proj_w': in_proj_w, 'conv_w': conv_w, 'conv_b': conv_b, 'x_proj_w': x_proj_w, 'dt_proj_w': dt_proj_w, 'dt_proj_b': dt_proj_b, 'log_A': log_A, 'Dp': Dp, 'out_proj_w': out_proj_w}
    _L0_attn_b_in = _L0_attn_b_setup()

    def _L0_ffn_setup():
        import jax, jax.numpy as jnp
        import numpy as np
        TOP_K = 2
        key = jax.random.key(seed)
        k1, k2, k3, k4 = jax.random.split(key, 4)
        B, T, D, H, E = (2, 256, 128, 256, 8)
        x = jax.random.normal(k1, (B, T, D), dtype=jnp.float32)
        w12 = jax.random.normal(k2, (E, 2 * H, D), dtype=jnp.float32) * D ** (-0.5)
        w3 = jax.random.normal(k3, (E, D, H), dtype=jnp.float32) * H ** (-0.5)
        gate_w = jax.random.normal(k4, (E, D), dtype=jnp.float32) * D ** (-0.5)
        return {'x': x, 'w12': w12, 'w3': w3, 'gate_w': gate_w}
    _L0_ffn_in = _L0_ffn_setup()

    def _L1_attn_a_setup():
        import jax, jax.numpy as jnp
        import numpy as np
        B, N, D_IN, D_OUT, HEADS = (4, 512, 128, 128, 16)
        D_HEAD = D_OUT // HEADS
        key = jax.random.key(seed)
        ks = jax.random.split(key, 5)
        x = jax.random.normal(ks[0], (B, N, D_IN), dtype=jnp.float32)
        s_in = 1.0 / np.sqrt(D_IN)
        s_out = 1.0 / np.sqrt(D_OUT)
        Wq = jax.random.normal(ks[1], (D_IN, D_OUT), dtype=jnp.float32) * s_in
        Wk = jax.random.normal(ks[2], (D_IN, D_OUT), dtype=jnp.float32) * s_in
        Wv = jax.random.normal(ks[3], (D_IN, D_OUT), dtype=jnp.float32) * s_in
        Wo = jax.random.normal(ks[4], (D_OUT, D_OUT), dtype=jnp.float32) * s_out
        bo = jnp.zeros((D_OUT,), dtype=jnp.float32)
        return {'x': x, 'Wq': Wq, 'Wk': Wk, 'Wv': Wv, 'Wo': Wo, 'bo': bo}
    _L1_attn_a_in = _L1_attn_a_setup()

    def _L1_attn_b_setup():
        import jax, jax.numpy as jnp
        import numpy as np
        B, N, E, D = (2, 512, 128, 128)
        H = E // D
        LN_EPS = 1e-05

        def _gla_scan(q, k, v, g):

            def step(S, inp):
                qt, kt, vt, gt = inp
                S = jnp.exp(gt)[..., None] * S + kt[..., None] * vt[..., None, :]
                ot = jnp.einsum('bhd,bhde->bhe', qt, S)
                return (S, ot)
            xs = tuple((jnp.moveaxis(a, 2, 0) for a in (q, k, v, g)))
            S0 = jnp.zeros(q.shape[:2] + (q.shape[-1], v.shape[-1]), q.dtype)
            _, o = jax.lax.scan(step, S0, xs)
            return jnp.moveaxis(o, 0, 2)
        key = jax.random.key(seed)
        ks = jax.random.split(key, 6)
        s = 0.02
        return {'x': jax.random.normal(ks[0], (B, N, E), jnp.float32), 'W_in': jax.random.normal(ks[1], (3 * E, E), jnp.float32) * s, 'W_out': jax.random.normal(ks[2], (E, E), jnp.float32) * s, 'W_g1': jax.random.normal(ks[3], (D, E), jnp.float32) * s, 'W_g2': jax.random.normal(ks[4], (E, D), jnp.float32) * s, 'ln_w': jnp.ones((E,), jnp.float32)}
    _L1_attn_b_in = _L1_attn_b_setup()

    def _L1_ffn_setup():
        import jax, jax.numpy as jnp
        import numpy as np
        HIDDEN = 128
        INTER = 64
        N_EXPERTS = 16
        N_GROUP = 4
        TOPK_GROUP = 2
        TOP_K = 4
        SCALING = 2.5

        def _gate(x_flat, gate_w, e_bias):
            logits = x_flat @ gate_w.T
            scores = jax.nn.sigmoid(logits)
            scores_for_choice = scores + e_bias[None, :]
            T = x_flat.shape[0]
            per_group = N_EXPERTS // N_GROUP
            grouped = scores_for_choice.reshape(T, N_GROUP, per_group)
            top2, _ = jax.lax.top_k(grouped, 2)
            group_scores = top2.sum(-1)
            _, group_idx = jax.lax.top_k(group_scores, TOPK_GROUP)
            group_mask = jax.nn.one_hot(group_idx, N_GROUP, dtype=jnp.float32).sum(1) > 0
            score_mask = jnp.repeat(group_mask, per_group, axis=-1)
            tmp_scores = jnp.where(score_mask, scores_for_choice, 0.0)
            _, topk_idx = jax.lax.top_k(tmp_scores, TOP_K)
            topk_weight = jnp.take_along_axis(scores, topk_idx, axis=1)
            topk_weight = topk_weight / (topk_weight.sum(-1, keepdims=True) + 1e-20)
            topk_weight = topk_weight * SCALING
            return (topk_idx, topk_weight)
        key = jax.random.key(seed)
        ks = jax.random.split(key, 8)
        B, S = (2, 256)
        hidden_states = jax.random.normal(ks[0], (B, S, HIDDEN), dtype=jnp.float32)
        gate_w = jax.random.normal(ks[1], (N_EXPERTS, HIDDEN), dtype=jnp.float32) * 0.02
        e_bias = jnp.zeros((N_EXPERTS,), dtype=jnp.float32)
        gate_proj = jax.random.normal(ks[2], (N_EXPERTS, INTER, HIDDEN), dtype=jnp.float32) * 0.02
        up_proj = jax.random.normal(ks[3], (N_EXPERTS, INTER, HIDDEN), dtype=jnp.float32) * 0.02
        down_proj = jax.random.normal(ks[4], (N_EXPERTS, HIDDEN, INTER), dtype=jnp.float32) * 0.02
        shared_gate_w = jax.random.normal(ks[5], (INTER, HIDDEN), dtype=jnp.float32) * 0.02
        shared_up_w = jax.random.normal(ks[6], (INTER, HIDDEN), dtype=jnp.float32) * 0.02
        shared_down_w = jax.random.normal(ks[7], (HIDDEN, INTER), dtype=jnp.float32) * 0.02
        return {'hidden_states': hidden_states, 'gate_w': gate_w, 'e_bias': e_bias, 'gate_proj': gate_proj, 'up_proj': up_proj, 'down_proj': down_proj, 'shared_gate_w': shared_gate_w, 'shared_up_w': shared_up_w, 'shared_down_w': shared_down_w}
    _L1_ffn_in = _L1_ffn_setup()
    _d = {'L0_attn_a_x': _L0_attn_a_in['x'], 'L0_attn_a_Wk': _L0_attn_a_in['Wk'], 'L0_attn_a_Wq': _L0_attn_a_in['Wq'], 'L0_attn_a_Wv': _L0_attn_a_in['Wv'], 'L0_attn_a_Wu': _L0_attn_a_in['Wu'], 'L0_attn_a_bu': _L0_attn_a_in['bu'], 'L0_attn_b_norm_g': _L0_attn_b_in['norm_g'], 'L0_attn_b_norm_b': _L0_attn_b_in['norm_b'], 'L0_attn_b_in_proj_w': _L0_attn_b_in['in_proj_w'], 'L0_attn_b_conv_w': _L0_attn_b_in['conv_w'], 'L0_attn_b_conv_b': _L0_attn_b_in['conv_b'], 'L0_attn_b_x_proj_w': _L0_attn_b_in['x_proj_w'], 'L0_attn_b_dt_proj_w': _L0_attn_b_in['dt_proj_w'], 'L0_attn_b_dt_proj_b': _L0_attn_b_in['dt_proj_b'], 'L0_attn_b_log_A': _L0_attn_b_in['log_A'], 'L0_attn_b_Dp': _L0_attn_b_in['Dp'], 'L0_attn_b_out_proj_w': _L0_attn_b_in['out_proj_w'], 'L0_ffn_w12': _L0_ffn_in['w12'], 'L0_ffn_w3': _L0_ffn_in['w3'], 'L0_ffn_gate_w': _L0_ffn_in['gate_w'], 'L1_attn_a_Wq': _L1_attn_a_in['Wq'], 'L1_attn_a_Wk': _L1_attn_a_in['Wk'], 'L1_attn_a_Wv': _L1_attn_a_in['Wv'], 'L1_attn_a_Wo': _L1_attn_a_in['Wo'], 'L1_attn_a_bo': _L1_attn_a_in['bo'], 'L1_attn_b_W_in': _L1_attn_b_in['W_in'], 'L1_attn_b_W_out': _L1_attn_b_in['W_out'], 'L1_attn_b_W_g1': _L1_attn_b_in['W_g1'], 'L1_attn_b_W_g2': _L1_attn_b_in['W_g2'], 'L1_attn_b_ln_w': _L1_attn_b_in['ln_w'], 'L1_ffn_gate_w': _L1_ffn_in['gate_w'], 'L1_ffn_e_bias': _L1_ffn_in['e_bias'], 'L1_ffn_gate_proj': _L1_ffn_in['gate_proj'], 'L1_ffn_up_proj': _L1_ffn_in['up_proj'], 'L1_ffn_down_proj': _L1_ffn_in['down_proj'], 'L1_ffn_shared_gate_w': _L1_ffn_in['shared_gate_w'], 'L1_ffn_shared_up_w': _L1_ffn_in['shared_up_w'], 'L1_ffn_shared_down_w': _L1_ffn_in['shared_down_w']}
    _x0 = _d['L0_attn_a_x']
    _d['L0_attn_a_x'] = jax.random.normal(jax.random.fold_in(jax.random.key(seed), 1), (1, 2048, 128), dtype=_x0.dtype)
    del _x0
    return _d

def reference(L0_attn_a_x, L0_attn_a_Wk, L0_attn_a_Wq, L0_attn_a_Wv, L0_attn_a_Wu, L0_attn_a_bu, L0_attn_b_norm_g, L0_attn_b_norm_b, L0_attn_b_in_proj_w, L0_attn_b_conv_w, L0_attn_b_conv_b, L0_attn_b_x_proj_w, L0_attn_b_dt_proj_w, L0_attn_b_dt_proj_b, L0_attn_b_log_A, L0_attn_b_Dp, L0_attn_b_out_proj_w, L0_ffn_w12, L0_ffn_w3, L0_ffn_gate_w, L1_attn_a_Wq, L1_attn_a_Wk, L1_attn_a_Wv, L1_attn_a_Wo, L1_attn_a_bo, L1_attn_b_W_in, L1_attn_b_W_out, L1_attn_b_W_g1, L1_attn_b_W_g2, L1_attn_b_ln_w, L1_ffn_gate_w, L1_ffn_e_bias, L1_ffn_gate_proj, L1_ffn_up_proj, L1_ffn_down_proj, L1_ffn_shared_gate_w, L1_ffn_shared_up_w, L1_ffn_shared_down_w):

    def _L0_attn_a_ref(x, Wk, Wq, Wv, Wu, bu):
        import jax, jax.numpy as jnp
        import numpy as np
        import math
        EMB = 128
        HEADS = 16
        W_STD = 0.02
        b, t, e = x.shape
        h = HEADS
        s = e // h
        scale = 1.0 / math.sqrt(s)
        keys = x @ jnp.triu(Wk).T
        queries = x @ jnp.tril(Wq).T
        values = x @ Wv.T
        keys = keys.reshape(b, t, h, s)
        queries = queries.reshape(b, t, h, s)
        values = values.reshape(b, t, h, s)
        dot = jnp.einsum('bqhs,bkhs->bhqk', queries, keys) * scale
        att = jax.nn.softmax(dot, axis=-1)
        out = jnp.einsum('bhqk,bkhs->bqhs', att, values).reshape(b, t, e)
        return out @ Wu.T + bu

    def _L0_attn_b_ref(x, norm_g, norm_b, in_proj_w, conv_w, conv_b, x_proj_w, dt_proj_w, dt_proj_b, log_A, Dp, out_proj_w):
        import jax, jax.numpy as jnp
        import numpy as np
        D_MODEL = 128
        D_STATE = 16
        D_CONV = 4
        EXPAND = 2
        D_INNER = EXPAND * D_MODEL
        DT_RANK = (D_MODEL + 15) // 16
        BATCH, SEQ_LEN = (2, 256)
        LN_EPS = 1e-05

        def _silu(v):
            return v * jax.nn.sigmoid(v)

        def _selective_scan(x, delta, A, B, C, Dp):
            b, L, d_inner = x.shape
            d_state = A.shape[1]
            xT = jnp.swapaxes(x, 0, 1)
            dT = jnp.swapaxes(delta, 0, 1)
            BT = jnp.swapaxes(B, 0, 1)
            CT = jnp.swapaxes(C, 0, 1)

            def step(h, inp):
                x_t, d_t, B_t, C_t = inp
                dA = jnp.exp(d_t[:, :, None] * A[None, :, :])
                h = dA * h + (d_t * x_t)[:, :, None] * B_t[:, None, :]
                y_t = jnp.einsum('bds,bs->bd', h, C_t)
                return (h, y_t)
            h0 = jnp.zeros((b, d_inner, d_state), x.dtype)
            _, yT = jax.lax.scan(step, h0, (xT, dT, BT, CT))
            y = jnp.swapaxes(yT, 0, 1)
            return y + x * Dp[None, None, :]
        if __name__ == '__main__':
            out = reference(**setup_inputs())
            print(out.shape, out.dtype)
        residual = x
        mu = jnp.mean(x, axis=-1, keepdims=True)
        var = jnp.mean((x - mu) ** 2, axis=-1, keepdims=True)
        xn = (x - mu) * jax.lax.rsqrt(var + LN_EPS) * norm_g + norm_b
        xz = jnp.einsum('bld,ed->ble', xn, in_proj_w)
        x_ssm, z = jnp.split(xz, 2, axis=-1)
        L = x.shape[1]
        xpad = jnp.pad(x_ssm, ((0, 0), (D_CONV - 1, 0), (0, 0)))
        conv = sum((xpad[:, k:k + L, :] * conv_w[None, None, :, k] for k in range(D_CONV))) + conv_b
        x_ssm = _silu(conv)
        xp = jnp.einsum('bld,ed->ble', x_ssm, x_proj_w)
        dt, B, C = jnp.split(xp, [DT_RANK, DT_RANK + D_STATE], axis=-1)
        delta = jax.nn.softplus(jnp.einsum('blr,dr->bld', dt, dt_proj_w) + dt_proj_b)
        A = -jnp.exp(log_A)
        y = _selective_scan(x_ssm, delta, A, B, C, Dp)
        y = y * _silu(z)
        out = jnp.einsum('ble,de->bld', y, out_proj_w)
        return out + residual

    def _L0_ffn_ref(x, w12, w3, gate_w):
        import jax, jax.numpy as jnp
        import numpy as np
        TOP_K = 2
        E = gate_w.shape[0]
        H = w3.shape[-1]
        scores = jnp.einsum('btd,ed->bte', x, gate_w)
        topk_scores, topk_idx = jax.lax.top_k(scores, TOP_K)
        topk_probs = jax.nn.softmax(topk_scores, axis=-1)
        total_probs = jnp.sum(jax.nn.one_hot(topk_idx, E, dtype=topk_probs.dtype) * topk_probs[..., None], axis=-2)
        h12 = jnp.einsum('btd,ehd->bteh', x, w12)
        h1, h2 = (h12[..., :H], h12[..., H:])
        hidden = jax.nn.silu(h1) * h2
        expert_out = jnp.einsum('bteh,edh->bted', hidden, w3)
        y = jnp.sum(total_probs[..., None] * expert_out, axis=-2)
        return y

    def _L1_attn_a_ref(x, Wq, Wk, Wv, Wo, bo):
        import jax, jax.numpy as jnp
        import numpy as np
        B, N, D_IN, D_OUT, HEADS = (4, 512, 128, 128, 16)
        D_HEAD = D_OUT // HEADS
        q = jax.nn.softmax(jnp.einsum('bni,io->bno', x, Wq), axis=-1)
        k = jax.nn.softmax(jnp.einsum('bni,io->bno', x, Wk), axis=-2)
        v = jnp.einsum('bni,io->bno', x, Wv)
        scale = 1.0 / np.sqrt(D_HEAD).astype(np.float32)
        ctx = jnp.einsum('bnd,bne->bde', k, v) * scale
        y = jnp.einsum('bnd,bde->bne', q, ctx) / jnp.float32(D_OUT)
        return jnp.einsum('bnd,de->bne', y, Wo) + bo

    def _L1_attn_b_ref(x, W_in, W_out, W_g1, W_g2, ln_w):
        import jax, jax.numpy as jnp
        import numpy as np
        B, N, E, D = (2, 512, 128, 128)
        H = E // D
        LN_EPS = 1e-05

        def _gla_scan(q, k, v, g):

            def step(S, inp):
                qt, kt, vt, gt = inp
                S = jnp.exp(gt)[..., None] * S + kt[..., None] * vt[..., None, :]
                ot = jnp.einsum('bhd,bhde->bhe', qt, S)
                return (S, ot)
            xs = tuple((jnp.moveaxis(a, 2, 0) for a in (q, k, v, g)))
            S0 = jnp.zeros(q.shape[:2] + (q.shape[-1], v.shape[-1]), q.dtype)
            _, o = jax.lax.scan(step, S0, xs)
            return jnp.moveaxis(o, 0, 2)
        b, n, e = x.shape
        u = x @ W_in.T
        v, q, lg = jnp.split(u, 3, axis=-1)
        q = jax.nn.silu(q)
        f = jax.nn.sigmoid(lg)
        k = 1.0 - f
        g = jax.nn.log_sigmoid(lg)

        def tohead(a):
            return a.reshape(b, n, H, D).transpose(0, 2, 1, 3)
        o = _gla_scan(tohead(q), tohead(k), tohead(v), tohead(g))
        o = o.transpose(0, 2, 1, 3).reshape(b, n, e)
        gate = jax.nn.sigmoid(x @ W_g1.T @ W_g2.T)
        o = o * gate
        mu = jnp.mean(o, axis=-1, keepdims=True)
        var = jnp.var(o, axis=-1, keepdims=True)
        o = (o - mu) * jax.lax.rsqrt(var + LN_EPS) * ln_w
        return o @ W_out.T

    def _L1_ffn_ref(hidden_states, gate_w, e_bias, gate_proj, up_proj, down_proj, shared_gate_w, shared_up_w, shared_down_w):
        import jax, jax.numpy as jnp
        import numpy as np
        HIDDEN = 128
        INTER = 64
        N_EXPERTS = 16
        N_GROUP = 4
        TOPK_GROUP = 2
        TOP_K = 4
        SCALING = 2.5

        def _gate(x_flat, gate_w, e_bias):
            logits = x_flat @ gate_w.T
            scores = jax.nn.sigmoid(logits)
            scores_for_choice = scores + e_bias[None, :]
            T = x_flat.shape[0]
            per_group = N_EXPERTS // N_GROUP
            grouped = scores_for_choice.reshape(T, N_GROUP, per_group)
            top2, _ = jax.lax.top_k(grouped, 2)
            group_scores = top2.sum(-1)
            _, group_idx = jax.lax.top_k(group_scores, TOPK_GROUP)
            group_mask = jax.nn.one_hot(group_idx, N_GROUP, dtype=jnp.float32).sum(1) > 0
            score_mask = jnp.repeat(group_mask, per_group, axis=-1)
            tmp_scores = jnp.where(score_mask, scores_for_choice, 0.0)
            _, topk_idx = jax.lax.top_k(tmp_scores, TOP_K)
            topk_weight = jnp.take_along_axis(scores, topk_idx, axis=1)
            topk_weight = topk_weight / (topk_weight.sum(-1, keepdims=True) + 1e-20)
            topk_weight = topk_weight * SCALING
            return (topk_idx, topk_weight)
        B, S, H = hidden_states.shape
        x = hidden_states.reshape(-1, H)
        T = x.shape[0]
        topk_idx, topk_weight = _gate(x, gate_w, e_bias)
        g = jnp.einsum('th,eih->eti', x, gate_proj)
        u = jnp.einsum('th,eih->eti', x, up_proj)
        inter = jax.nn.silu(g) * u
        expert_out = jnp.einsum('eti,ehi->eth', inter, down_proj)
        sel = expert_out[topk_idx, jnp.arange(T)[:, None]]
        y = jnp.einsum('tkh,tk->th', sel, topk_weight)
        y = y.reshape(B, S, H)
        sg = hidden_states @ shared_gate_w.T
        su = hidden_states @ shared_up_w.T
        shared_out = jax.nn.silu(sg) * su @ shared_down_w.T
        return y + shared_out
    x = L0_attn_a_x
    x = x + _L0_attn_a_ref(_layernorm(x, axis=-1), L0_attn_a_Wk, L0_attn_a_Wq, L0_attn_a_Wv, L0_attn_a_Wu, L0_attn_a_bu)
    x = x + _L0_ffn_ref(_layernorm(x, axis=-1), L0_ffn_w12, L0_ffn_w3, L0_ffn_gate_w)
    x = x + _L0_attn_b_ref(_layernorm(x, axis=-1), L0_attn_b_norm_g, L0_attn_b_norm_b, L0_attn_b_in_proj_w, L0_attn_b_conv_w, L0_attn_b_conv_b, L0_attn_b_x_proj_w, L0_attn_b_dt_proj_w, L0_attn_b_dt_proj_b, L0_attn_b_log_A, L0_attn_b_Dp, L0_attn_b_out_proj_w)
    x = x + _L0_ffn_ref(_layernorm(x, axis=-1), L0_ffn_w12, L0_ffn_w3, L0_ffn_gate_w)
    x = x + _L1_attn_a_ref(_layernorm(x, axis=-1), L1_attn_a_Wq, L1_attn_a_Wk, L1_attn_a_Wv, L1_attn_a_Wo, L1_attn_a_bo)
    x = x + _L1_ffn_ref(_layernorm(x, axis=-1), L1_ffn_gate_w, L1_ffn_e_bias, L1_ffn_gate_proj, L1_ffn_up_proj, L1_ffn_down_proj, L1_ffn_shared_gate_w, L1_ffn_shared_up_w, L1_ffn_shared_down_w)
    x = x + _L1_attn_b_ref(_layernorm(x, axis=-1), L1_attn_b_W_in, L1_attn_b_W_out, L1_attn_b_W_g1, L1_attn_b_W_g2, L1_attn_b_ln_w)
    x = x + _L1_ffn_ref(_layernorm(x, axis=-1), L1_ffn_gate_w, L1_ffn_e_bias, L1_ffn_gate_proj, L1_ffn_up_proj, L1_ffn_down_proj, L1_ffn_shared_gate_w, L1_ffn_shared_up_w, L1_ffn_shared_down_w)
    return x

_drawn_inputs = setup_inputs


def setup_inputs(seed=0):
    import zlib

    import numpy as np

    out = dict(_drawn_inputs(seed))
    spreads = {'L0_attn_a_bu': (0.0, 0.1),
     'L0_attn_b_norm_g': (1.0, 0.2),
     'L0_attn_b_norm_b': (0.0, 0.1),
     'L0_attn_b_Dp': (1.0, 0.2),
     'L1_attn_a_bo': (0.0, 0.1),
     'L1_attn_b_ln_w': (1.0, 0.6),
     'L1_ffn_e_bias': (0.0, 0.8)}
    factors = {'L0_attn_a_Wk': 8.0,
     'L0_attn_a_Wq': 5.364,
     'L0_attn_b_conv_b': 3.921,
     'L0_attn_b_dt_proj_b': 7.891,
     'L1_attn_a_Wq': 8.0,
     'L1_attn_a_Wk': 8.0,
     'L1_attn_a_Wv': 8.0,
     'L1_attn_a_Wo': 8.0,
     'L1_attn_b_W_g1': 8.0,
     'L1_attn_b_W_g2': 8.0,
     'L1_ffn_gate_w': 8.0,
     'L1_ffn_gate_proj': 8.0,
     'L1_ffn_up_proj': 8.0,
     'L1_ffn_down_proj': 8.0,
     'L1_ffn_shared_gate_w': 8.0,
     'L1_ffn_shared_up_w': 8.0,
     'L1_ffn_shared_down_w': 8.0}
    for name, (base, spread) in spreads.items():
        noise = np.random.default_rng([zlib.crc32(name.encode()), seed]).standard_normal(out[name].shape)
        drawn = base * np.exp(spread * noise) if base else spread * noise
        out[name] = jnp.asarray(drawn.astype(out[name].dtype))
    for name, factor in factors.items():
        out[name] = (out[name] * factor).astype(out[name].dtype)
    return out
```

```python
from contextlib import ExitStack

import numpy as np

import concourse.bass as bass
from concourse import mybir

ALU = mybir.AluOpType
ACT = mybir.ActivationFunctionType
F32 = mybir.dt.float32
BF16 = mybir.dt.bfloat16
U32 = mybir.dt.uint32
AX_X = mybir.AxisListType.X

P = 128
T = 2048
NT = T // P
CH = 512
NC_ = T // CH
TPC = CH // P
EPS = 1e-5

HEADS = 16
HD = P // HEADS
E0, H0, TOP0 = 8, 256, 2
DI, DS, DCONV, DTR = 256, 16, 4, 8
ND = DI // P
E1, I1, GROUPS, TOPG, TOP1 = 16, 64, 4, 2, 4
SCALING = 2.5
LEVELS = 7


class Line:

    def __init__(self, sem):
        self.sem, self.n = sem, 0

    def mark(self, ins):
        self.n += 1
        ins.then_inc(self.sem, 1)

    def wait(self, eng):
        eng.wait_ge(self.sem, self.n)

    def after(self, eng, ins):
        self.mark(ins)
        self.wait(eng)


class Core:

    def __init__(self, nc, ctx):
        self.nc, self.ctx = nc, ctx
        self.w = {}
        self.stage_sems = []
        self.dve_line = Line(self.sem("dve_line"))
        self.act_line = Line(self.sem("act_line"))
        self.pool_line = Line(self.sem("pool_line"))

    def sem(self, name):
        self.stage_sems.append(self.nc.alloc_semaphore(name=name))
        return self.stage_sems[-1]

    def run_stage(self, build, *args):
        self.stage_sems = []
        build(self, *args)
        self.nc.all_engine_barrier()
        self.nc.clear_and_free_semaphores(self.stage_sems)
        self.nc.all_engine_barrier()

    def sb(self, name, shape, dt=F32):
        return self.ctx.enter_context(self.nc.sbuf_tensor(name, shape, dt))


def tile_of(a, t):
    return a[:, t * P:(t + 1) * P]


class LayerNorm:

    def __init__(self, core, ctx, name, src, out, outT, gain=None, shift=None, banks=(0, 1)):
        nc = core.nc
        self.core, self.src, self.out, self.outT = core, src, out, outT
        self.gain, self.shift, self.banks = gain, shift, banks

        def sb(n, shape):
            return ctx.enter_context(nc.sbuf_tensor(f"{name}_{n}", shape, F32))

        self.stats = sb("stats", [P, NT, 6])
        self.mv = sb("mv", [P, NT, 2])
        self.veps = sb("veps", [P, NT])
        self.lnv = sb("lnv", [P, NT])
        self.r0 = sb("r0", [P, NT])
        self.r2 = sb("r2", [P, NT])
        self.rstd = sb("rstd", [P, NT])
        self.var_ready = core.sem(f"{name}_var_ready")
        self.guess_ready = core.sem(f"{name}_guess_ready")
        self.normed = core.sem(f"{name}_normed")
        self.turned = core.sem(f"{name}_turned")
        self.T_ready = core.sem(f"{name}_T_ready")

    def vector(self, dve):
        nc, line = self.core.nc, self.core.dve_line
        for t in range(NT):
            line.mark(nc.vector.bn_stats(self.stats[:, t, :], self.src[:, t, :]))
        line.wait(dve)
        for t in range(NT):
            line.mark(nc.vector.bn_aggr(self.mv[:, t, :], self.stats[:, t, :]))
        line.wait(dve)
        nc.vector.tensor_scalar(self.veps[:], self.mv[:, :, 1], EPS, None, ALU.add).then_inc(self.var_ready, 1)
        dve.wait_ge(self.guess_ready, 2)
        line.after(dve, nc.vector.tensor_tensor(self.r2[:], self.r0[:], self.r0[:], ALU.mult))
        line.after(dve, nc.vector.tensor_tensor(self.r2[:], self.r2[:], self.veps[:], ALU.mult))
        line.after(dve, nc.vector.tensor_scalar(self.r2[:], self.r2[:], -0.5, 1.5, ALU.mult, ALU.add))
        line.after(dve, nc.vector.tensor_tensor(self.rstd[:], self.r0[:], self.r2[:], ALU.mult))
        for t in range(NT):
            nc.vector.tensor_scalar(self.out[:, t, :], self.src[:, t, :], self.mv[:, t, 0:1], self.rstd[:, t:t + 1],
                                    ALU.subtract, ALU.mult).then_inc(self.normed, 1)

    def scalar(self, act):
        nc = self.core.nc
        act.wait_ge(self.var_ready, 1)
        nc.scalar.activation(self.lnv[:], self.veps[:], ACT.Ln).then_inc(self.guess_ready, 1)
        act.wait_ge(self.guess_ready, 1)
        nc.scalar.activation(self.r0[:], self.lnv[:], ACT.Exp, scale=-0.5).then_inc(self.guess_ready, 1)
        if self.outT is None:
            return
        for c in range(NC_):
            act.wait_ge(self.turned, c + 1)
            bank = self.core.ps[:, self.banks[c % 2], :]
            dst = self.outT[:, c * CH:(c + 1) * CH]
            if self.gain is None:
                nc.scalar.copy(dst, bank).then_inc(self.T_ready, 1)
            elif self.shift is None:
                nc.scalar.activation(dst, bank, ACT.Identity, scale=self.gain).then_inc(self.T_ready, 1)
            else:
                nc.scalar.activation(dst, bank, ACT.Identity, bias=self.shift, scale=self.gain).then_inc(self.T_ready, 1)

    def tensor(self, pe):
        nc, core = self.core.nc, self.core
        for c in range(NC_):
            if c >= 2:
                pe.wait_ge(self.T_ready, c - 1)
            for k in range(TPC):
                pe.wait_ge(self.normed, c * TPC + k + 1)
                last = nc.tensor.transpose(core.ps[:, self.banks[c % 2], k * P:(k + 1) * P],
                                           self.out[:, c * TPC + k, :], core.ident[:])
            last.then_inc(self.turned, 1)


def softmax_attention(core):
    nc, w = core.nc, core.w
    SCALE = float(HD) ** -0.5
    NPART, KROWS = 3, 6 * HD
    ROWS = KROWS + NPART
    QPARTS = ((0, 3), (0, 2), (0, 1))
    KPARTS = (0, 0, 0, 1, 1, 2)
    RING = 4
    LAG_S = NT + 3
    LAG_V = LAG_S + 2
    NBUF = 3
    BODY = NBUF * NT
    LOOPED = (HEADS - 1) // NBUF
    S_BANK, O_BANK = 4, 6
    with ExitStack() as ctx:
        def sb(name, shape, dt=F32):
            return ctx.enter_context(nc.sbuf_tensor(name, shape, dt))

        xn, xnT = core.xn, core.xnT
        ln = LayerNorm(core, ctx, "ln_a", core.x, xn, xnT)
        v_all = sb("v_all", [P, NT, P])
        v_head = [sb(f"v_head{i}", [P, NT, HD + 1]) for i in range(NBUF)]
        qst = [sb(f"q_stack{i}", [P, T], BF16) for i in range(NBUF)]
        kst = [sb(f"k_stack{i}", [P, T], BF16) for i in range(NBUF)]
        ones = sb("ones", [NPART, T], BF16)
        probs = sb("probs", [P, RING, T])
        mx = sb("row_max", [P, NT, 2])
        neg_max = sb("neg_max", [P, 32])
        nmT = sb("neg_maxT", [P, 32])
        nm_rest = sb("neg_max_rest", [P, 32])
        nm_parts = sb("neg_max_parts", [P, NPART, 32], BF16)
        o_sb = sb("o_sb", [P, CH])
        whole = sb("whole", [P, T])
        parts = sb("parts", [P, 2, NPART, T], BF16)
        den = sb("den", [P, HEADS * T // P])
        rden = sb("rden", [P, HEADS * T // P])
        att_raw = probs[:, 0, :]
        rden_rows = probs[:, 1, :]
        attT = probs[:, 2, :]
        qd = nc.dram_tensor("q_parts_dram", (HEADS, NPART, HD, T), BF16).ap()
        kd = nc.dram_tensor("k_parts_dram", (HEADS, NPART, HD, T), BF16).ap()
        md = [nc.dram_tensor(f"max_dram{i}", (NPART, T), BF16).ap() for i in range(NBUF)]
        od = nc.dram_tensor("o_dram", (HEADS, HD + 1, T), F32).ap()
        rd = nc.dram_tensor("rden_dram", (HEADS, T), F32).ap()

        proj = core.sem("a_proj")
        proj_used = core.sem("a_proj_used")
        whole_done = core.sem("a_whole")
        split_done = core.sem("a_split")
        parts_stored = core.sem("a_parts_stored")
        masked = core.sem("a_masked")
        ones_set = core.sem("a_ones")
        ones_placed = core.sem("a_ones_placed")
        stacked = [core.sem(f"a_stacked{i}") for i in range(NBUF)]
        p1_done = core.sem("a_pass1_scores")
        max_done = core.sem("a_max_done")
        nm_line = core.sem("a_nm_line")
        nm_ready = core.sem("a_nm_ready")
        m_stored = core.sem("a_max_stored")
        m_loaded = [core.sem(f"a_max_loaded{i}") for i in range(NBUF)]
        v_staged = core.sem("a_v_staged")
        s_done = core.sem("a_scores")
        exp_done = core.sem("a_exp")
        pv_done = core.sem("a_pv")
        evacuated = core.sem("a_evacuated")
        o_stored = core.sem("a_o_stored")
        den_loaded = core.sem("a_den_loaded")
        rden_ready = core.sem("a_rden_ready")
        rden_stored = core.sem("a_rden_stored")
        fin_loaded = core.sem("a_fin_loaded")
        att_ready = core.sem("a_att_ready")
        out_done = core.sem("a_out_done")
        bias_added = core.sem("a_bias_added")

        block = ctx.enter_context(nc.Block())
        STACK = 16 * (len(QPARTS) + len(KPARTS))

        @block.sync
        def _(sp):
            for which, dram in enumerate((qd, kd)):
                sp.wait_ge(split_done, 5 * (which + 1))
                for p in range(NPART):
                    sp.dma_start(dram[:, p].rearrange("h s t -> h s t"),
                                 parts[:, which, p, :]).then_inc(parts_stored, 16)
            sp.wait_ge(parts_stored, 16 * 2 * NPART)
            sp.wait_ge(ones_set, 3 * NBUF + 1)
            for buf in range(NBUF):
                sp.dma_start(kst[buf][KROWS:ROWS, :], ones[:]).then_inc(ones_placed, 16)

            def load_stack(head, par):
                row = 0
                for first, n in QPARTS:
                    sp.dma_start(qst[par][row:row + n * HD, :],
                                 qd[head, first:first + n].rearrange("p s t -> (p s) t")).then_inc(stacked[par], 16)
                    row += n * HD
                for i, part in enumerate(KPARTS):
                    sp.dma_start(kst[par][i * HD:(i + 1) * HD, :], kd[head, part]).then_inc(stacked[par], 16)

            def store_max(head, par):
                sp.wait_ge(nm_ready, head + 1)
                for b in range(P // 32):
                    sp.dma_start(md[par].rearrange("p (j b i) -> b j p i", b=P // 32, i=32)[b],
                                   nm_parts[32 * b:32 * b + NT, :, :]).then_inc(m_stored, 16)
                sp.wait_ge(m_stored, (head + 1) * 64)
                sp.dma_start(qst[par][KROWS:ROWS, :], md[par]).then_inc(m_loaded[par], 16)

            def store_o(head):
                sp.wait_ge(evacuated, head + 1)
                for c in range(NC_):
                    sp.dma_start(od[head, :, c * CH:(c + 1) * CH],
                                   o_sb[32 * c:32 * c + HD + 1, :]).then_inc(o_stored, 16)

            for head in range(NBUF):
                load_stack(head, head)
            for head in range(NBUF - 1):
                store_max(head, head)
            store_o(0)
            with sp.Fori(1, LOOPED) as j:
                for par in range(NBUF):
                    sp.wait_ge(s_done, j * (4 * BODY) + (par + 1 - NBUF) * 4 * NT)
                    load_stack(j * NBUF + par, par)
                    store_max(j * NBUF + (par - 1), (par - 1) % NBUF)
                    store_o(j * NBUF + (par - 2))
            sp.wait_ge(s_done, (HEADS - NBUF) * 4 * NT)
            load_stack(HEADS - 1, (HEADS - 1) % NBUF)
            store_max(HEADS - 2, (HEADS - 2) % NBUF)
            store_o(HEADS - 3)
            store_max(HEADS - 1, (HEADS - 1) % NBUF)
            for head in (HEADS - 2, HEADS - 1):
                store_o(head)
            sp.wait_ge(o_stored, 64 * HEADS)
            sp.dma_start(den[:], od[:, HD, :].rearrange("h (k n) -> h k n", k=P // HEADS)).then_inc(den_loaded, 16)
            for h in range(HEADS):
                sp.dma_start(att_raw[HD * h:HD * (h + 1), :], od[h, 0:HD, :]).then_inc(fin_loaded, 16)
            sp.wait_ge(rden_ready, 1)
            sp.dma_start(rd.rearrange("h (k n) -> h k n", k=P // HEADS), rden[:]).then_inc(rden_stored, 16)
            sp.wait_ge(rden_stored, 16)
            for h in range(HEADS):
                sp.dma_start(rden_rows[HD * h:HD * (h + 1), :],
                             rd[h:h + 1, :].to_broadcast([HD, T])).then_inc(fin_loaded, 16)

        @block.gpsimd
        def _(pool):
            core.loaded(pool, "Wq0", "Wk0")
            for name, sign in (("Wq0", 1), ("Wk0", -1)):
                nc.gpsimd.affine_select(out=w[name][:], in_=w[name][:], pattern=[[sign, P]], channel_multiplier=-sign,
                                        base=0, compare_op=ALU.is_ge, fill=0.0).then_inc(masked, 1)
            nc.gpsimd.memset(ones[:], 1.0).then_inc(ones_set, 1)
            for par in range(NBUF):
                nc.gpsimd.memset(qst[par][:], 0.0).then_inc(ones_set, 1)
                nc.gpsimd.memset(kst[par][:], 0.0).then_inc(ones_set, 1)
                nc.gpsimd.memset(v_head[par][:], 1.0).then_inc(ones_set, 1)
            core.loaded(pool, "bu")
            pool.wait_ge(ln.normed, NT)
            for t in range(NT):
                nc.gpsimd.tensor_tensor(core.x[:, t, :], core.x[:, t, :], w["bu"][:], ALU.add).then_inc(bias_added, 1)
            pool.wait_ge(proj_used, 2 * NC_ + NC_)
            pool.wait_ge(ones_set, 3 * NBUF + 1)

            def stage_v(head, par):
                nc.gpsimd.tensor_copy(v_head[par][:, :, 0:HD], v_all[:, :, bass.ds(head * HD, HD)]).then_inc(v_staged, 1)

            for head in range(NBUF):
                stage_v(head, head)
            with pool.Fori(1, LOOPED) as j:
                for par in range(NBUF):
                    pool.wait_ge(pv_done, j * BODY + (par + 1 - NBUF) * NT)
                    stage_v(j * NBUF + par, par)
            pool.wait_ge(pv_done, (HEADS - NBUF) * NT)
            stage_v(HEADS - 1, (HEADS - 1) % NBUF)

        @block.tensor
        def _(pe):
            ln.tensor(pe)
            pe.wait_ge(masked, 2)
            n = 0
            for name in ("Wq0", "Wk0"):
                for c in range(NC_):
                    if name == "Wq0":
                        pe.wait_ge(ln.T_ready, c + 1)
                    if n >= 4:
                        pe.wait_ge(proj_used, n - 3)
                    nc.tensor.matmul(core.ps[:, 4 + n % 4, :], w[name][:], xnT[:, c * CH:(c + 1) * CH],
                                     start=True, stop=True).then_inc(proj, 1)
                    n += 1
            core.loaded(pe, "Wv0")
            for g in range(NC_):
                pe.wait_ge(proj_used, n - 3)
                for k in range(TPC):
                    last = nc.tensor.matmul(core.ps[:, 4 + n % 4, k * P:(k + 1) * P], tile_of(xnT, g * TPC + k),
                                            w["Wv0"][:], start=True, stop=True)
                last.then_inc(proj, 1)
                n += 1
            pe.wait_ge(proj_used, n)

            def slot(j, gs, maxima=True, scores=True, values=True):
                first_body = isinstance(j, int) and j == 0
                if maxima:
                    buf, u = gs // NT % NBUF, gs % NT
                    if u == 0:
                        pe.wait_ge(stacked[buf], j * STACK + STACK)
                    for b in range(2):
                        if not first_body or gs:
                            pe.wait_ge(max_done, j * (2 * BODY) + (2 * gs + b - 1))
                        for r in range(2):
                            rows = slice(0, KROWS)
                            key = (2 * b + r) * CH
                            last = nc.tensor.matmul(core.ps[:, 2 * b + r, :], qst[buf][rows, u * P:(u + 1) * P],
                                                    kst[buf][rows, key:key + CH], start=True, stop=True)
                        last.then_inc(p1_done, 1)
                if scores:
                    m = gs - LAG_S
                    buf, kt = m // NT % NBUF, m % NT
                    if kt == 0:
                        pe.wait_ge(m_loaded[buf], j * 16 + 16 * (m // BODY + 1))
                    for c in range(NC_):
                        if not first_body or 4 * m + c >= 2:
                            pe.wait_ge(exp_done, j * (4 * BODY) + (4 * m + c - 1))
                        nc.tensor.matmul(core.ps[:, S_BANK + c % 2, :], kst[buf][:, kt * P:(kt + 1) * P],
                                         qst[buf][:, c * CH:(c + 1) * CH], start=True, stop=True).then_inc(s_done, 1)
                if values:
                    m = gs - LAG_V
                    buf, kt = m // NT % NBUF, m % NT
                    if kt == 0:
                        pe.wait_ge(v_staged, j * NBUF + (m // NT + 1))
                        if not first_body or m:
                            pe.wait_ge(evacuated, j * NBUF + m // NT)
                    pe.wait_ge(exp_done, j * (4 * BODY) + 4 * (m + 1))
                    for c in range(NC_):
                        last = nc.tensor.matmul(core.ps[32 * c:32 * c + HD + 1, O_BANK, :], v_head[buf][:, kt, :],
                                                probs[:, m % RING, c * CH:(c + 1) * CH],
                                                start=kt == 0, stop=kt == NT - 1)
                    last.then_inc(pv_done, 1)

            pe.wait_ge(ones_placed, 16 * NBUF)
            for gs in range(BODY):
                slot(0, gs, True, gs >= LAG_S, gs >= LAG_V)
            with pe.Fori(1, LOOPED) as j:
                for gs in range(BODY):
                    slot(j, gs)
            for gs in range(NT + LAG_V):
                slot(LOOPED, gs, gs < NT, gs < NT + LAG_S)
            core.loaded(pe, "Wu0")
            pe.wait_ge(att_ready, 1)
            for g in range(NC_):
                for k in range(TPC):
                    last = nc.tensor.matmul(core.ps[:, g, k * P:(k + 1) * P], tile_of(attT, g * TPC + k), w["Wu0"][:],
                                            start=True, stop=True)
                last.then_inc(out_done, 1)

        @block.scalar
        def _(act):
            ln.scalar(act)
            for which, scale in enumerate((SCALE, 1.0)):
                for c in range(NC_):
                    act.wait_ge(proj, which * NC_ + c + 1)
                    if which == 1 and c == 0:
                        act.wait_ge(split_done, 5)
                    nc.scalar.mul(whole[:, c * CH:(c + 1) * CH], core.ps[:, 4 + c, :], scale).then_inc(proj_used, 1)
            for g in range(NC_):
                act.wait_ge(proj, 2 * NC_ + g + 1)
                nc.scalar.copy(v_all[:, g * TPC:(g + 1) * TPC, :],
                               core.ps[:, 4 + g, :].rearrange("p (k d) -> p k d", d=P)).then_inc(proj_used, 1)

            def unit(m, us, first=False):
                kt = us % NT
                if not first:
                    act.wait_ge(pv_done, m - (RING - 1))
                for c in range(NC_):
                    act.wait_ge(s_done, m * 4 + (c + 1))
                    nc.scalar.activation(probs[:, us % RING, c * CH:(c + 1) * CH], core.ps[:, S_BANK + c % 2, :],
                                         ACT.Exp).then_inc(exp_done, 1)

            def evacuate(head):
                act.wait_ge(pv_done, head * NT + NT)
                if not isinstance(head, int) or head:
                    act.wait_ge(o_stored, head * 64)
                nc.scalar.copy(o_sb[:], core.ps[:, O_BANK, :]).then_inc(evacuated, 1)

            act.wait_ge(core.o_zeroed, 1)
            for us in range(NT):
                unit(us, us, first=us < RING)
            for us in range(NT):
                unit(NT + us, us)
                if us == 2:
                    evacuate(0)
            with act.Fori(2, HEADS) as i:
                for us in range(NT):
                    unit(i * NT + us, us)
                    if us == 2:
                        evacuate(i + (-1))
            evacuate(HEADS - 1)

        @block.vector
        def _(dve):
            line = core.dve_line
            nc.vector.memset(core.ps[:, O_BANK, :], 0.0).then_inc(core.o_zeroed, 1)
            line.after(dve, nc.vector.memset(neg_max[:], 0.0))
            ln.vector(dve)
            for which in range(2):
                dve.wait_ge(proj_used, NC_ * (which + 1))
                pt = [parts[:, which, p, :] for p in range(NPART)]
                base = 5 * which
                nc.vector.tensor_copy(pt[0], whole[:]).then_inc(split_done, 1)
                dve.wait_ge(split_done, base + 1)
                nc.vector.tensor_tensor(whole[:], whole[:], pt[0], ALU.subtract).then_inc(split_done, 1)
                dve.wait_ge(split_done, base + 2)
                nc.vector.tensor_copy(pt[1], whole[:]).then_inc(split_done, 1)
                dve.wait_ge(split_done, base + 3)
                nc.vector.tensor_tensor(whole[:], whole[:], pt[1], ALU.subtract).then_inc(split_done, 1)
                dve.wait_ge(split_done, base + 4)
                nc.vector.tensor_copy(pt[2], whole[:]).then_inc(split_done, 1)

            def maxima(head, first_unit):
                for u in range(NT):
                    for b in range(2):
                        dve.wait_ge(p1_done, first_unit * 2 + (2 * u + b + 1))
                        nc.vector.tensor_reduce(mx[:, u, b:b + 1], core.ps[:, 2 * b:2 * b + 2, :],
                                                mybir.AxisListType.XY, ALU.max).then_inc(max_done, 1)
                dve.wait_ge(max_done, head * (2 * NT) + 2 * NT)
                step = [0]

                def then(ins):
                    step[0] += 1
                    ins.then_inc(nm_line, 1)
                    dve.wait_ge(nm_line, head * 6 + step[0])

                then(nc.vector.tensor_reduce(neg_max[:, 0:NT], mx[:], AX_X, ALU.max, negate=True))
                then(nc.vector.transpose(nmT[:], neg_max[:]))
                if not isinstance(head, int) or head:
                    dve.wait_ge(m_stored, head * 64)
                then(nc.vector.tensor_copy(nm_parts[:, 0, :], nmT[:]))
                then(nc.vector.tensor_tensor(nm_rest[:], nmT[:], nm_parts[:, 0, :], ALU.subtract))
                then(nc.vector.tensor_copy(nm_parts[:, 1, :], nm_rest[:]))
                then(nc.vector.tensor_tensor(nm_rest[:], nm_rest[:], nm_parts[:, 1, :], ALU.subtract))
                nc.vector.tensor_copy(nm_parts[:, 2, :], nm_rest[:]).then_inc(nm_ready, 1)

            maxima(0, 0)
            with dve.Fori(1, HEADS) as i:
                dve.wait_ge(nm_ready, i)
                maxima(i, i * NT)
            dve.wait_ge(den_loaded, 16)
            nc.vector.reciprocal(rden[:], den[:]).then_inc(rden_ready, 1)
            dve.wait_ge(fin_loaded, 16 * 2 * HEADS)
            nc.vector.tensor_tensor(attT, att_raw, rden_rows, ALU.mult).then_inc(att_ready, 1)
            dve.wait_ge(bias_added, NT)
            for g in range(NC_):
                dve.wait_ge(out_done, g + 1)
                xs = core.x[:, g * TPC:(g + 1) * TPC, :]
                line.mark(nc.vector.tensor_tensor(xs, xs, core.ps[:, g, :].rearrange("p (k d) -> p k d", d=P), ALU.add))
            line.wait(dve)


def pick_top(core, dve, scores, top8, keep, work, k):
    nc, line = core.nc, core.dve_line
    ne = scores.shape[-1]
    kth = top8[:, :, k - 1:k].to_broadcast([P, NT, ne])
    line.mark(nc.vector.tensor_tensor(work["gt"][:], scores, kth, ALU.is_gt))
    line.after(dve, nc.vector.tensor_tensor(work["eq"][:], scores, kth, ALU.is_equal))
    line.mark(nc.vector.tensor_tensor_scan(out=work["nth"][:].rearrange("p t e -> p (t e)"),
                                           data0=keep[:].rearrange("p t e -> p (t e)"),
                                           data1=work["eq"][:].rearrange("p t e -> p (t e)"),
                                           initial=0.0, op0=ALU.mult, op1=ALU.add))
    line.after(dve, nc.vector.tensor_reduce(work["above"][:], work["gt"][:], AX_X, ALU.add))
    line.after(dve, nc.vector.tensor_scalar(work["room"][:], work["above"][:], -1.0, float(k), ALU.mult, ALU.add))
    line.after(dve, nc.vector.tensor_tensor(work["nth"][:], work["nth"][:],
                                            work["room"][:].unsqueeze(2).to_broadcast([P, NT, ne]), ALU.is_le))
    line.after(dve, nc.vector.tensor_tensor(work["nth"][:], work["nth"][:], work["eq"][:], ALU.mult))
    line.after(dve, nc.vector.tensor_tensor(work["sel"][:], work["gt"][:], work["nth"][:], ALU.add))


def experts_top2(core, tag):
    nc, w = core.nc, core.w
    NH = H0 // P
    UNITS = E0 * NH
    UP, DOWN = 0, 4
    with ExitStack() as ctx:
        def sb(name, shape, dt=F32):
            return ctx.enter_context(nc.sbuf_tensor(f"{tag}_{name}", shape, dt))

        ln = LayerNorm(core, ctx, f"ln_{tag}", core.x, core.xn, core.xnT)
        xnT = core.xnT
        scores = sb("scores", [P, NT, E0])
        top8 = sb("top8", [P, NT, 8])
        keep = sb("keep", [P, NT, E0])
        work = {n: sb(n, [P, NT, E0]) for n in ("gt", "eq", "nth", "sel")}
        work.update({n: sb(n, [P, NT]) for n in ("above", "room")})
        expd = sb("expd", [P, NT, E0])
        probs = sb("probs", [P, NT, E0])
        total = sb("total", [P, NT])
        gate = [sb(f"gate{i}", [P, CH]) for i in range(2)]
        hidden = [sb(f"hidden{i}", [P, NH, CH]) for i in range(2)]

        scored = core.sem(f"{tag}_scored")
        exp_in = core.sem(f"{tag}_exp_in")
        exp_out = core.sem(f"{tag}_exp_out")
        up_done = core.sem(f"{tag}_up")
        gate_done = core.sem(f"{tag}_gate")
        hidden_done = core.sem(f"{tag}_hidden")
        down_done = core.sem(f"{tag}_down")
        added = core.sem(f"{tag}_added")
        block = ctx.enter_context(nc.Block())

        @block.tensor
        def _(pe):
            ln.tensor(pe)
            core.loaded(pe, "gate0", "w12", "w3")
            for t in range(NT):
                pe.wait_ge(ln.T_ready, t // TPC + 1)
                last = nc.tensor.matmul(core.ps[:, 7, t * E0:(t + 1) * E0], tile_of(xnT, t), w["gate0"][:],
                                        start=True, stop=True)
            last.then_inc(scored, 1)

            def up(j, u, chunk):
                e, half = u // NH, u % NH
                if not (isinstance(j, int) and u < 2):
                    pe.wait_ge(hidden_done, j * UNITS + (u - 1))
                for k in range(2):
                    col = (k * NH + half) * P
                    nc.tensor.matmul(core.ps[:, UP + 2 * (u % 2) + k, :], w["w12"][:, e, col:col + P],
                                     chunk, start=True, stop=True).then_inc(up_done, 1)

            def down(j, e):
                pe.wait_ge(hidden_done, j * UNITS + (e + 1) * NH)
                if not (isinstance(j, int) and e < 2):
                    pe.wait_ge(added, j * (E0 * TPC) + (e - 1) * TPC)
                for k in range(TPC):
                    for half in range(NH):
                        last = nc.tensor.matmul(core.ps[:, DOWN + e % 2, k * P:(k + 1) * P],
                                                hidden[e % 2][:, half, k * P:(k + 1) * P], w["w3"][:, e, half, :],
                                                start=half == 0, stop=half == NH - 1)
                last.then_inc(down_done, 1)

            def body(j, chunk):
                for e in range(E0):
                    for half in range(NH):
                        up(j, e * NH + half, chunk)
                    if e:
                        down(j, e - 1)
                down(j, E0 - 1)

            body(0, xnT[:, 0:CH])
            with pe.Fori(1, NC_) as j:
                body(j, xnT[:, bass.ds(j * CH, CH)])

        @block.scalar
        def _(act):
            ln.scalar(act)
            act.wait_ge(exp_in, 1)
            nc.scalar.activation(expd[:], expd[:], ACT.Exp).then_inc(exp_out, 1)

            def body(j):
                for u in range(UNITS):
                    act.wait_ge(up_done, j * (2 * UNITS) + (2 * u + 1))
                    if not (isinstance(j, int) and u < 2):
                        act.wait_ge(hidden_done, j * UNITS + (u - 1))
                    nc.scalar.activation(gate[u % 2][:], core.ps[:, UP + 2 * (u % 2), :], ACT.Silu).then_inc(gate_done, 1)

            body(0)
            with act.Fori(1, NC_) as j:
                body(j)

        @block.vector
        def _(dve):
            line = core.dve_line
            line.after(dve, nc.vector.memset(keep[:], 1.0))
            line.mark(nc.vector.memset(keep[:, :, 0:1], 0.0))
            ln.vector(dve)
            dve.wait_ge(scored, 1)
            line.after(dve, nc.vector.tensor_copy(scores[:], core.ps[:, 7, 0:NT * E0].rearrange("p (t e) -> p t e", e=E0)))
            for t in range(NT):
                line.mark(nc.vector.max(top8[:, t, :], scores[:, t, :]))
            line.wait(dve)
            nc.vector.tensor_tensor(expd[:], scores[:], top8[:, :, 0:1].to_broadcast([P, NT, E0]),
                                    ALU.subtract).then_inc(exp_in, 1)
            pick_top(core, dve, scores[:], top8, keep, work, TOP0)
            dve.wait_ge(exp_out, 1)
            line.after(dve, nc.vector.tensor_tensor(expd[:], expd[:], work["sel"][:], ALU.mult))
            line.after(dve, nc.vector.tensor_reduce(total[:], expd[:], AX_X, ALU.add))
            line.after(dve, nc.vector.reciprocal(total[:], total[:]))
            line.after(dve, nc.vector.tensor_tensor(probs[:], expd[:], total[:].unsqueeze(2).to_broadcast([P, NT, E0]),
                                                    ALU.mult))

            def multiply(j, u):
                dve.wait_ge(gate_done, j * UNITS + (u + 1))
                dve.wait_ge(up_done, j * (2 * UNITS) + (2 * u + 2))
                e = u // NH
                if not (isinstance(j, int) and e < 2) and u % NH == 0:
                    dve.wait_ge(down_done, j * E0 + (e - 1))
                nc.vector.tensor_tensor(hidden[e % 2][:, u % NH, :], gate[u % 2][:], core.ps[:, UP + 2 * (u % 2) + 1, :],
                                        ALU.mult).then_inc(hidden_done, 1)

            def add(j, e):
                dve.wait_ge(down_done, j * E0 + (e + 1))
                if not (isinstance(j, int) and e == 0):
                    dve.wait_ge(added, j * (E0 * TPC) + e * TPC)
                for k in range(TPC):
                    t = j * TPC + k
                    xs = core.x[:, bass.ds(t, 1), :].rearrange("p t d -> p (t d)")
                    nc.vector.scalar_tensor_tensor(out=xs, in0=core.ps[:, DOWN + e % 2, k * P:(k + 1) * P],
                                                   scalar=probs[:, bass.ds(t, 1), e], in1=xs,
                                                   op0=ALU.mult, op1=ALU.add).then_inc(added, 1)

            def body(j):
                for e in range(E0):
                    for half in range(NH):
                        multiply(j, e * NH + half)
                    if e:
                        add(j, e - 1)
                add(j, E0 - 1)

            body(0)
            with dve.Fori(1, NC_) as j:
                body(j)


def selective_scan(core):
    nc, w = core.nc, core.w
    PAD = DCONV - 1
    with ExitStack() as ctx:
        def sb(name, shape, dt=F32):
            return ctx.enter_context(nc.sbuf_tensor(f"s_{name}", shape, dt))

        delta = [sb(f"delta{d}", [P, T]) for d in range(ND)]
        xn2 = delta[0][:].rearrange("p (t d) -> p t d", d=P)
        xnT = core.xnT
        ln1 = LayerNorm(core, ctx, "ln_s1", core.x, core.xn, None)
        ln2 = LayerNorm(core, ctx, "ln_s2", core.xn, xn2, xnT, w["norm_g"][:], w["norm_b"][:])
        pre = [sb(f"pre{d}", [P, PAD + T]) for d in range(ND)]
        zs = [sb(f"zs{d}", [P, T]) for d in range(ND)]
        xs = [sb(f"xs{d}", [P, T]) for d in range(ND)]
        delta_c = [sb(f"delta_c{d}", [P, CH]) for d in range(ND)]
        dx_c = [sb(f"dx_c{d}", [P, CH]) for d in range(ND)]
        pick = w["pick"][:].bitcast(BF16)
        bc = sb("bc", [96, T], BF16)
        rest = sb("rest", [96, CH])
        mid = sb("mid", [96, CH], BF16)
        dtr = sb("dtr", [DTR, T])
        a_neg = sb("a_neg", [P, ND, DS])
        tmp = [sb(f"tmp{i}", [P, CH]) for i in range(2)]
        tmp2 = [sb(f"tmp2{i}", [P, CH]) for i in range(2)]
        da, dbx = tmp, tmp2
        b_rows = [sb(f"b_rows{i}", [P, CH]) for i in range(2)]
        h = [sb(f"h{i}", [P, CH]) for i in range(2)]
        hc = [sb(f"hc{i}", [P, CH]) for i in range(2)]
        state = sb("state", [P, DS, ND])
        yT = [sb(f"yT{d}", [P, CH]) for d in range(ND)]

        padded = core.sem("s_padded")
        in_done = core.sem("s_in_done")
        in_used = core.sem("s_in_used")
        conv_done = core.sem("s_conv")
        conv_silu = core.sem("s_conv_silu")
        xp_done = core.sem("s_xp")
        bc_ready = core.sem("s_bc_ready")
        dt_copied = core.sem("s_dt_copied")
        dt_done = core.sem("s_dt_done")
        soft = core.sem("s_soft")
        delta_done = core.sem("s_delta")
        chunk_ready = core.sem("s_chunk_ready")
        residual = core.sem("s_residual")
        rows_done = core.sem("s_rows")
        b_copied = core.sem("s_b_copied")
        da_done = core.sem("s_da")
        dbx_done = core.sem("s_dbx")
        scanned = core.sem("s_scanned")
        saved = core.sem("s_saved")
        hc_done = core.sem("s_hc")
        summed = core.sem("s_summed")
        y_done = core.sem("s_y")
        out_done = core.sem("s_out")
        x_added = core.sem("s_x_added")

        B_BANK, C_BANK, Y_BANK, O_BANK = 0, 2, 4, 6
        UNITS = DS * ND
        block = ctx.enter_context(nc.Block())

        @block.gpsimd
        def _(pool):
            for d in range(ND):
                nc.gpsimd.memset(pre[d][:, 0:PAD], 0.0).then_inc(padded, 1)
            nc.gpsimd.memset(state[:], 0.0).then_inc(padded, 1)
            pool.wait_ge(ln1.normed, NT)
            for t in range(NT):
                nc.gpsimd.tensor_tensor(core.x[:, t, :], core.x[:, t, :], core.xn[:, t, :], ALU.add).then_inc(residual, 1)

            def body(j):
                pool.wait_ge(chunk_ready, j * 2 * ND + 2 * ND)
                for s in range(DS):
                    for d in range(ND):
                        u = s * ND + d
                        if not (isinstance(j, int) and u < 2):
                            pool.wait_ge(scanned, j * UNITS + (u - 1))
                        pool.wait_ge(b_copied, j * DS + (s + 1))
                        nc.gpsimd.tensor_tensor(dbx[d][:], dx_c[d][:], b_rows[s % 2][:],
                                                ALU.mult).then_inc(dbx_done, 1)

            body(0)
            with pool.Fori(1, NC_) as j:
                body(j)

        @block.tensor
        def _(pe):
            ln2.tensor(pe)
            core.loaded(pe, "in_proj", "x_bc", "x_dt", "dt_proj", "out_proj")
            n = 0
            for c in range(NC_):
                pe.wait_ge(ln2.T_ready, c + 1)
                for m in range(2 * ND):
                    if n >= 4:
                        pe.wait_ge(in_used, n - 3)
                    nc.tensor.matmul(core.ps[:, 4 + n % 4, :], w["in_proj"][:, m * P:(m + 1) * P],
                                     xnT[:, c * CH:(c + 1) * CH], start=True, stop=True).then_inc(in_done, 1)
                    n += 1
            pe.wait_ge(conv_silu, ND)
            for c in range(NC_):
                if c >= 2:
                    pe.wait_ge(bc_ready, c - 1)
                for d in range(ND):
                    nc.tensor.matmul(core.ps[0:96, c % 2, :], w["x_bc"][:, d, :], xs[d][:, c * CH:(c + 1) * CH],
                                     start=d == 0, stop=d == ND - 1)
                if c >= 2:
                    pe.wait_ge(dt_copied, c - 1)
                for d in range(ND):
                    last = nc.tensor.matmul(core.ps[0:DTR, 2 + c % 2, :], w["x_dt"][:, d, :],
                                            xs[d][:, c * CH:(c + 1) * CH], start=d == 0, stop=d == ND - 1)
                last.then_inc(xp_done, 1)
            pe.wait_ge(in_used, n)
            for c in range(NC_):
                pe.wait_ge(dt_copied, c + 1)
                for d in range(ND):
                    m = c * ND + d
                    if m >= 4:
                        pe.wait_ge(soft, 4 * (m - 4) + 1)
                    nc.tensor.matmul(core.ps[:, 4 + m % 4, :], w["dt_proj"][:, d * P:(d + 1) * P],
                                     dtr[:, c * CH:(c + 1) * CH], start=True, stop=True).then_inc(dt_done, 1)
            pe.wait_ge(bc_ready, NC_)
            core.loaded(pe, "pick")
            pe.wait_ge(soft, 4 * (ND * NC_ - 1) + 1)

            def spread(j, s, chunk):
                if not (isinstance(j, int) and s < 2):
                    pe.wait_ge(b_copied, j * DS + (s - 1))
                    pe.wait_ge(hc_done, j * UNITS + (s - 1) * ND)
                nc.tensor.matmul(core.ps[:, B_BANK + s % 2, :], pick[:, s, :], chunk, start=True, stop=True)
                nc.tensor.matmul(core.ps[:, C_BANK + s % 2, :], pick[:, DS + s, :], chunk,
                                 start=True, stop=True).then_inc(rows_done, 1)

            def add_up(j, s):
                for d in range(ND):
                    pe.wait_ge(hc_done, j * UNITS + (s * ND + d + 1))
                    nc.tensor.matmul(core.ps[:, Y_BANK + d, :], core.ident[:], hc[d][:],
                                     start=s == 0, stop=s == DS - 1).then_inc(summed, 1)

            def body(j, chunk):
                if not isinstance(j, int):
                    pe.wait_ge(y_done, j * 2 * ND)
                for s in range(DS):
                    spread(j, s, chunk)
                    if s:
                        add_up(j, s - 1)
                add_up(j, DS - 1)
                pe.wait_ge(y_done, j * (2 * ND) + 2 * ND)
                if not isinstance(j, int):
                    pe.wait_ge(x_added, j)
                for k in range(TPC):
                    for d in range(ND):
                        last = nc.tensor.matmul(core.ps[:, O_BANK, k * P:(k + 1) * P], yT[d][:, k * P:(k + 1) * P],
                                                w["out_proj"][:, d, :], start=d == 0, stop=d == ND - 1)
                last.then_inc(out_done, 1)

            body(0, bc[:, 0:CH])
            with pe.Fori(1, NC_) as j:
                body(j, bc[:, bass.ds(j * CH, CH)])

        @block.scalar
        def _(act):
            line = core.act_line
            core.loaded(act, "norm_g", "norm_b")
            ln1.scalar(act)
            ln2.scalar(act)
            core.loaded(act, "log_A", "conv_b", "dt_b")
            n = 0
            for c in range(NC_):
                for m in range(2 * ND):
                    act.wait_ge(in_done, n + 1)
                    src = core.ps[:, 4 + n % 4, :]
                    if m < ND:
                        if c == 0:
                            act.wait_ge(padded, ND)
                        ins = nc.scalar.copy(pre[m][:, PAD + c * CH:PAD + (c + 1) * CH], src)
                    else:
                        ins = nc.scalar.activation(zs[m - ND][:, c * CH:(c + 1) * CH], src, ACT.Silu)
                    ins.then_inc(in_used, 1)
                    n += 1
            for d in range(ND):
                act.wait_ge(conv_done, DCONV * (d + 1))
                nc.scalar.activation(xs[d][:], delta[d][:], ACT.Silu).then_inc(conv_silu, 1)
            for c in range(NC_):
                act.wait_ge(xp_done, c + 1)
                nc.scalar.copy(dtr[:, c * CH:(c + 1) * CH], core.ps[0:DTR, 2 + c % 2, :]).then_inc(dt_copied, 1)
            m = 0
            for c in range(NC_):
                for d in range(ND):
                    act.wait_ge(dt_done, m + 1)
                    if m >= 2:
                        act.wait_ge(delta_done, m - 1)
                    v, e = tmp[m % 2], tmp2[m % 2]
                    nc.scalar.activation(v[:], core.ps[:, 4 + m % 4, :], ACT.Identity,
                                         bias=w["dt_b"][:, d:d + 1]).then_inc(soft, 1)
                    act.wait_ge(soft, 4 * m + 1)
                    nc.scalar.activation(e[:], v[:], ACT.Abs).then_inc(soft, 1)
                    act.wait_ge(soft, 4 * m + 2)
                    nc.scalar.activation(e[:], e[:], ACT.Exp, scale=-1.0).then_inc(soft, 1)
                    act.wait_ge(soft, 4 * m + 3)
                    nc.scalar.activation(e[:], e[:], ACT.Ln, bias=1.0).then_inc(soft, 1)
                    m += 1
            line.after(act, nc.scalar.activation(a_neg[:], w["log_A"][:], ACT.Exp))
            line.after(act, nc.scalar.mul(a_neg[:], a_neg[:], -1.0))

            def body(j):
                for s in range(DS):
                    act.wait_ge(rows_done, j * DS + (s + 1))
                    if not (isinstance(j, int) and s < 2):
                        act.wait_ge(dbx_done, j * UNITS + (s - 1) * ND)
                    nc.scalar.copy(b_rows[s % 2][:], core.ps[:, B_BANK + s % 2, :]).then_inc(b_copied, 1)
                    for d in range(ND):
                        u = s * ND + d
                        if not (isinstance(j, int) and u < 2):
                            act.wait_ge(scanned, j * UNITS + (u - 1))
                        if u == 0:
                            act.wait_ge(chunk_ready, j * 2 * ND + 2 * ND)
                        nc.scalar.activation(da[d][:], delta_c[d][:], ACT.Exp,
                                             scale=a_neg[:, d, s:s + 1]).then_inc(da_done, 1)

            body(0)
            with act.Fori(1, NC_) as j:
                body(j)

        @block.vector
        def _(dve):
            line = core.dve_line
            ln1.vector(dve)
            dve.wait_ge(ln1.normed, NT)
            ln2.vector(dve)
            dve.wait_ge(in_used, 2 * ND * NC_)
            core.loaded(dve, "conv_w", "conv_b", "Dp")
            for d in range(ND):
                acc = delta[d]
                nc.vector.tensor_scalar(acc[:], pre[d][:, 0:T], w["conv_w"][:, d, 0:1], w["conv_b"][:, d:d + 1],
                                        ALU.mult, ALU.add).then_inc(conv_done, 1)
                for k in range(1, DCONV):
                    dve.wait_ge(conv_done, DCONV * d + k)
                    nc.vector.scalar_tensor_tensor(out=acc[:], in0=pre[d][:, k:k + T], scalar=w["conv_w"][:, d, k:k + 1],
                                                   in1=acc[:], op0=ALU.mult, op1=ALU.add).then_inc(conv_done, 1)
            for c in range(NC_):
                dve.wait_ge(xp_done, c + 1)
                cols = slice(c * CH, (c + 1) * CH)
                src = core.ps[0:96, c % 2, :]
                line.after(dve, nc.vector.tensor_copy(bc[:, cols], src))
                line.after(dve, nc.vector.tensor_tensor(rest[:], src, bc[:, cols], ALU.subtract))
                line.after(dve, nc.vector.tensor_copy(mid[:], rest[:]))
                line.after(dve, nc.vector.tensor_tensor(rest[:], rest[:], mid[:], ALU.subtract))
                line.after(dve, nc.vector.tensor_copy(bc[32:64, cols], mid[32:64, :]))
                nc.vector.tensor_copy(bc[64:96, cols], rest[64:96, :]).then_inc(bc_ready, 1)
            m = 0
            for c in range(NC_):
                for d in range(ND):
                    dve.wait_ge(soft, 4 * m + 4)
                    if m == 0:
                        dve.wait_ge(conv_silu, ND)
                    nc.vector.scalar_tensor_tensor(out=delta[d][:, c * CH:(c + 1) * CH], in0=tmp[m % 2][:], scalar=0.0,
                                                   in1=tmp2[m % 2][:], op0=ALU.max, op1=ALU.add).then_inc(delta_done, 1)
                    m += 1
            dve.wait_ge(delta_done, m)
            dve.wait_ge(padded, ND + 1)
            dve.wait_ge(residual, NT)

            def body(j):
                for d in range(ND):
                    cols = bass.ds(j * CH, CH)
                    nc.vector.tensor_copy(delta_c[d][:], delta[d][:, cols]).then_inc(chunk_ready, 1)
                    nc.vector.tensor_tensor(dx_c[d][:], delta[d][:, cols], xs[d][:, cols], ALU.mult).then_inc(chunk_ready, 1)
                for s in range(DS):
                    for d in range(ND):
                        u = s * ND + d
                        dve.wait_ge(da_done, j * UNITS + (u + 1))
                        dve.wait_ge(dbx_done, j * UNITS + (u + 1))
                        if not (isinstance(j, int) and u < 2):
                            dve.wait_ge(hc_done, j * UNITS + (u - 1))
                            dve.wait_ge(saved, j * UNITS + (u - 1))
                        nc.vector.tensor_tensor_scan(out=h[d][:], data0=da[d][:], data1=dbx[d][:],
                                                     initial=state[:, s, d:d + 1], op0=ALU.mult,
                                                     op1=ALU.add).then_inc(scanned, 1)
                    for d in range(ND):
                        u = s * ND + d
                        dve.wait_ge(scanned, j * UNITS + (u + 1))
                        if not (isinstance(j, int) and u < 2):
                            dve.wait_ge(summed, j * UNITS + (u - 1))
                            dve.wait_ge(saved, j * UNITS + (u - 1))
                        nc.vector.tensor_tensor(hc[d][:], h[d][:], core.ps[:, C_BANK + s % 2, :],
                                                ALU.mult).then_inc(hc_done, 1)
                        nc.vector.tensor_copy(state[:, s, d:d + 1], h[d][:, CH - 1:CH]).then_inc(saved, 1)
                dve.wait_ge(summed, j * UNITS + UNITS)
                for d in range(ND):
                    if d == 0 and not isinstance(j, int):
                        dve.wait_ge(out_done, j)
                    nc.vector.scalar_tensor_tensor(out=yT[d][:], in0=xs[d][:, bass.ds(j * CH, CH)],
                                                   scalar=w["Dp"][:, d:d + 1], in1=core.ps[:, Y_BANK + d, :],
                                                   op0=ALU.mult, op1=ALU.add).then_inc(y_done, 1)
                dve.wait_ge(y_done, j * (2 * ND) + ND)
                for d in range(ND):
                    nc.vector.tensor_tensor(yT[d][:], yT[d][:], zs[d][:, bass.ds(j * CH, CH)],
                                            ALU.mult).then_inc(y_done, 1)
                dve.wait_ge(out_done, j + 1)
                xc = core.x[:, bass.ds(j * TPC, TPC), :].rearrange("p t d -> p (t d)")
                nc.vector.tensor_tensor(xc, xc, core.ps[:, O_BANK, :], ALU.add).then_inc(x_added, 1)

            body(0)
            with dve.Fori(1, NC_) as j:
                body(j)


def linear_attention(core):
    nc, w = core.nc, core.w
    SCALE = float(HD) ** -0.5 / P
    with ExitStack() as ctx:
        def sb(name, shape, dt=F32):
            return ctx.enter_context(nc.sbuf_tensor(f"l_{name}", shape, dt))

        ln = LayerNorm(core, ctx, "ln_l", core.x, core.xn, core.xnT)
        xnT = core.xnT
        keT = sb("keT", [P, T])
        k_tok = sb("k_tok", [P, NT, P])
        v_tok = sb("v_tok", [P, NT, P])
        q_tok = sb("q_tok", [P, NT, P])
        qT = sb("qT", [P, T])
        k_max = sb("k_max", [P, 1])
        k_sum = sb("k_sum", [P, 1])
        q_max = sb("q_max", [P, NT])
        q_sum = sb("q_sum", [P, NT])
        ctxT = sb("ctxT", [P, P])
        mixed = sb("mixed", [P, P])

        k_done = core.sem("l_k")
        kmax_done = core.sem("l_kmax")
        k_exp = core.sem("l_kexp")
        qv_done = core.sem("l_qv")
        v_copied = core.sem("l_v_copied")
        q_shifted = core.sem("l_q_shifted")
        q_exp = core.sem("l_q_exp")
        turned = core.sem("l_turned")
        k_copied = core.sem("l_k_copied")
        q_copied = core.sem("l_q_copied")
        ctx_done = core.sem("l_ctx")
        ctx_copied = core.sem("l_ctx_copied")
        mix_done = core.sem("l_mix")
        mixed_ready = core.sem("l_mixed")
        out_done = core.sem("l_out")
        added = core.sem("l_added")
        bias_added = core.sem("l_bias")
        block = ctx.enter_context(nc.Block())

        @block.gpsimd
        def _(pool):
            core.loaded(pool, "bo")
            pool.wait_ge(ln.normed, NT)
            for t in range(NT):
                nc.gpsimd.tensor_tensor(core.x[:, t, :], core.x[:, t, :], w["bo"][:], ALU.add).then_inc(bias_added, 1)

        @block.tensor
        def _(pe):
            ln.tensor(pe)
            core.loaded(pe, "Wk1", "Wq1", "Wv1", "Wo1")
            for c in range(NC_):
                pe.wait_ge(ln.T_ready, c + 1)
                last = nc.tensor.matmul(core.ps[:, 2 + c, :], w["Wk1"][:], xnT[:, c * CH:(c + 1) * CH],
                                        start=True, stop=True)
            last.then_inc(k_done, 1)
            for g in range(NC_):
                for i, name in enumerate(("Wq1", "Wv1")):
                    if g:
                        pe.wait_ge(q_shifted if i == 0 else v_copied, g)
                    for k in range(TPC):
                        last = nc.tensor.matmul(core.ps[:, 6 + i, k * P:(k + 1) * P], tile_of(xnT, g * TPC + k),
                                                w[name][:], start=True, stop=True)
                    last.then_inc(qv_done, 1)
            for g in range(NC_):
                pe.wait_ge(k_exp, 1)
                if g >= 2:
                    pe.wait_ge(k_copied, g - 1)
                for k in range(TPC):
                    last = nc.tensor.transpose(core.ps[:, g % 2, k * P:(k + 1) * P], tile_of(keT, g * TPC + k),
                                               core.ident[:])
                last.then_inc(turned, 1)
            for g in range(NC_):
                pe.wait_ge(q_exp, g + 1)
                pe.wait_ge(k_copied, min(NC_, g + 3))
                if g >= 2:
                    pe.wait_ge(q_copied, g - 1)
                for k in range(TPC):
                    last = nc.tensor.transpose(core.ps[:, g % 2, k * P:(k + 1) * P], q_tok[:, g * TPC + k, :],
                                               core.ident[:])
                last.then_inc(turned, 1)
            pe.wait_ge(q_shifted, NC_)
            pe.wait_ge(v_copied, NC_)
            pe.wait_ge(k_copied, NC_)
            for t in range(NT):
                last = nc.tensor.matmul(core.ps[:, 2, 0:P], v_tok[:, t, :], k_tok[:, t, :], start=t == 0, stop=t == NT - 1)
            last.then_inc(ctx_done, 1)
            pe.wait_ge(ctx_copied, 1)
            nc.tensor.matmul(core.ps[:, 3, 0:P], ctxT[:], w["Wo1"][:], start=True, stop=True).then_inc(mix_done, 1)
            pe.wait_ge(mixed_ready, 1)
            pe.wait_ge(q_copied, NC_)
            for g in range(NC_):
                for k in range(TPC):
                    last = nc.tensor.matmul(core.ps[:, 4 + g, k * P:(k + 1) * P], tile_of(qT, g * TPC + k), mixed[:],
                                            start=True, stop=True)
                last.then_inc(out_done, 1)

        @block.scalar
        def _(act):
            ln.scalar(act)
            act.wait_ge(kmax_done, 1)
            nc.scalar.activation(keT[:], core.ps[:, 2:6, :].rearrange("p b n -> p (b n)"), ACT.Exp, bias=k_max[:],
                                 accum_out=k_sum[:]).then_inc(k_exp, 1)
            for g in range(NC_):
                act.wait_ge(q_shifted, g + 1)
                qs = q_tok[:, g * TPC:(g + 1) * TPC, :]
                nc.scalar.activation(qs, qs, ACT.Exp).then_inc(q_exp, 1)
                act.wait_ge(qv_done, 2 * g + 2)
                nc.scalar.copy(v_tok[:, g * TPC:(g + 1) * TPC, :],
                               core.ps[:, 7, :].rearrange("p (k d) -> p k d", d=P)).then_inc(v_copied, 1)
            for g in range(NC_):
                act.wait_ge(turned, g + 1)
                nc.scalar.copy(k_tok[:, g * TPC:(g + 1) * TPC, :],
                               core.ps[:, g % 2, :].rearrange("p (k d) -> p k d", d=P)).then_inc(k_copied, 1)
            for g in range(NC_):
                act.wait_ge(turned, NC_ + g + 1)
                nc.scalar.copy(qT[:, g * CH:(g + 1) * CH], core.ps[:, g % 2, :]).then_inc(q_copied, 1)

        @block.vector
        def _(dve):
            line = core.dve_line
            ln.vector(dve)
            dve.wait_ge(k_done, 1)
            nc.vector.tensor_reduce(k_max[:], core.ps[:, 2:6, :], mybir.AxisListType.XY, ALU.max,
                                    negate=True).then_inc(kmax_done, 1)
            for g in range(NC_):
                dve.wait_ge(qv_done, 2 * g + 1)
                src = core.ps[:, 6, :].rearrange("p (k d) -> p k d", d=P)
                cols = slice(g * TPC, (g + 1) * TPC)
                line.after(dve, nc.vector.tensor_reduce(q_max[:, cols], src, AX_X, ALU.max))
                nc.vector.tensor_tensor(q_tok[:, cols, :], src, q_max[:, cols].unsqueeze(2).to_broadcast([P, TPC, P]),
                                        ALU.subtract).then_inc(q_shifted, 1)
            for g in range(NC_):
                dve.wait_ge(q_exp, g + 1)
                cols = slice(g * TPC, (g + 1) * TPC)
                line.mark(nc.vector.tensor_reduce(q_sum[:, cols], q_tok[:, cols, :], AX_X, ALU.add))
            line.wait(dve)
            line.after(dve, nc.vector.reciprocal(q_sum[:], q_sum[:]))
            dve.wait_ge(k_exp, 1)
            line.after(dve, nc.vector.reciprocal(k_max[:], k_sum[:]))
            dve.wait_ge(ctx_done, 1)
            nc.vector.tensor_copy(ctxT[:], core.ps[:, 2, 0:P]).then_inc(ctx_copied, 1)
            dve.wait_ge(mix_done, 1)
            nc.vector.tensor_scalar(mixed[:], core.ps[:, 3, 0:P], k_max[:], SCALE, ALU.mult,
                                    ALU.mult).then_inc(mixed_ready, 1)
            dve.wait_ge(bias_added, NT)
            for t in range(NT):
                if t % TPC == 0:
                    dve.wait_ge(out_done, t // TPC + 1)
                nc.vector.scalar_tensor_tensor(out=core.x[:, t, :],
                                               in0=core.ps[:, 4 + t // TPC, (t % TPC) * P:(t % TPC + 1) * P],
                                               scalar=q_sum[:, t:t + 1], in1=core.x[:, t, :],
                                               op0=ALU.mult, op1=ALU.add).then_inc(added, 1)
            dve.wait_ge(added, NT)


def experts_top4(core, tag):
    nc, w = core.nc, core.w
    PAIRS = E1 // 2
    UNITS = PAIRS + 1
    PG = E1 // GROUPS
    UP, DOWN, S_BANK = 0, 4, 7
    with ExitStack() as ctx:
        def sb(name, shape, dt=F32):
            return ctx.enter_context(nc.sbuf_tensor(f"{tag}_{name}", shape, dt))

        ln = LayerNorm(core, ctx, f"ln_{tag}", core.x, core.xn, core.xnT)
        xnT = core.xnT
        scores = sb("scores", [P, NT, E1])
        choice = sb("choice", [P, NT, E1])
        tmp_scores = sb("tmp_scores", [P, NT, E1])
        top8 = sb("top8", [P, NT, 8])
        keep = sb("keep", [P, NT, E1])
        work = {n: sb(n, [P, NT, E1]) for n in ("gt", "eq", "nth", "sel")}
        work.update({n: sb(n, [P, NT]) for n in ("above", "room")})
        hi = sb("hi", [P, NT * GROUPS, 2])
        lo = sb("lo", [P, NT * GROUPS, 2])
        g_best = sb("g_best", [P, NT * GROUPS])
        g_next = sb("g_next", [P, NT * GROUPS])
        g_low = sb("g_low", [P, NT * GROUPS])
        g_beats = sb("g_beats", [P, NT * GROUPS, GROUPS])
        g_ties = sb("g_ties", [P, NT * GROUPS, GROUPS])
        g_rank = sb("g_rank", [P, NT * GROUPS])
        probs = sb("probs", [P, NT, E1 + 1])
        total = sb("total", [P, NT])
        gate = [sb(f"gate{i}", [P, CH]) for i in range(2)]
        hidden = [sb(f"hidden{i}", [P, CH]) for i in range(2)]

        scored = core.sem(f"{tag}_scored")
        tanh_done = core.sem(f"{tag}_tanh")
        up_done = core.sem(f"{tag}_up")
        gate_done = core.sem(f"{tag}_gate")
        hidden_done = core.sem(f"{tag}_hidden")
        down_done = core.sem(f"{tag}_down")
        added = core.sem(f"{tag}_added")
        block = ctx.enter_context(nc.Block())

        def experts(u):
            return 2 if u < PAIRS else 1
        ADDS = (2 * PAIRS + 1) * TPC

        @block.tensor
        def _(pe):
            ln.tensor(pe)
            core.loaded(pe, "gate1", "w_up1", "w_down1", "sh_up", "sh_down")
            for t in range(NT):
                pe.wait_ge(ln.T_ready, t // TPC + 1)
                last = nc.tensor.matmul(core.ps[:, S_BANK, t * E1:(t + 1) * E1], tile_of(xnT, t), w["gate1"][:],
                                        start=True, stop=True)
            last.then_inc(scored, 1)

            def up(j, u, chunk):
                if not (isinstance(j, int) and u < 2):
                    pe.wait_ge(hidden_done, j * UNITS + (u - 1))
                for k in range(2):
                    weight = w["w_up1"][:, u, k, :] if u < PAIRS else w["sh_up"][:, k, :]
                    nc.tensor.matmul(core.ps[:, UP + 2 * (u % 2) + k, :], weight, chunk,
                                     start=True, stop=True).then_inc(up_done, 1)

            def down(j, u):
                pe.wait_ge(hidden_done, j * UNITS + (u + 1))
                if not (isinstance(j, int) and u == 0):
                    pe.wait_ge(added, j * ADDS + u * 2 * TPC)
                for k in range(TPC):
                    for i in range(experts(u)):
                        part = slice(I1 * i, I1 * (i + 1))
                        weight = w["w_down1"][part, u, :] if u < PAIRS else w["sh_down"][:]
                        last = nc.tensor.matmul(core.ps[:, DOWN + i, k * P:(k + 1) * P],
                                                hidden[u % 2][part, k * P:(k + 1) * P], weight, start=True, stop=True)
                last.then_inc(down_done, 1)

            def body(j, chunk):
                for u in range(UNITS):
                    up(j, u, chunk)
                    if u:
                        down(j, u - 1)
                down(j, UNITS - 1)

            body(0, xnT[:, 0:CH])
            with pe.Fori(1, NC_) as j:
                body(j, xnT[:, bass.ds(j * CH, CH)])

        @block.scalar
        def _(act):
            ln.scalar(act)
            act.wait_ge(scored, 1)
            nc.scalar.activation(scores[:], core.ps[:, S_BANK, 0:NT * E1].rearrange("p (t e) -> p t e", e=E1),
                                 ACT.Tanh, scale=0.5).then_inc(tanh_done, 1)

            def body(j):
                for u in range(UNITS):
                    act.wait_ge(up_done, j * (2 * UNITS) + (2 * u + 1))
                    if not (isinstance(j, int) and u < 2):
                        act.wait_ge(hidden_done, j * UNITS + (u - 1))
                    nc.scalar.activation(gate[u % 2][:], core.ps[:, UP + 2 * (u % 2), :],
                                         ACT.Silu).then_inc(gate_done, 1)

            body(0)
            with act.Fori(1, NC_) as j:
                body(j)

        @block.vector
        def _(dve):
            line = core.dve_line
            line.after(dve, nc.vector.memset(keep[:], 1.0))
            line.mark(nc.vector.memset(keep[:, :, 0:1], 0.0))
            line.mark(nc.vector.memset(probs[:, :, E1:E1 + 1], 1.0))
            ln.vector(dve)
            core.loaded(dve, "e_bias", "earlier")
            dve.wait_ge(tanh_done, 1)
            line.after(dve, nc.vector.tensor_scalar(scores[:], scores[:], 0.5, 0.5, ALU.mult, ALU.add))
            line.after(dve, nc.vector.tensor_tensor(choice[:], scores[:],
                                                    w["e_bias"][:].unsqueeze(1).to_broadcast([P, NT, E1]), ALU.add))
            quads = choice[:].rearrange("p t (g i k) -> p (t g) i k", g=GROUPS, k=2)
            line.mark(nc.vector.tensor_tensor(hi[:], quads[:, :, :, 0], quads[:, :, :, 1], ALU.max))
            line.after(dve, nc.vector.tensor_tensor(lo[:], quads[:, :, :, 0], quads[:, :, :, 1], ALU.min))
            line.mark(nc.vector.tensor_tensor(g_best[:], hi[:, :, 0], hi[:, :, 1], ALU.max))
            line.mark(nc.vector.tensor_tensor(g_next[:], hi[:, :, 0], hi[:, :, 1], ALU.min))
            line.after(dve, nc.vector.tensor_tensor(g_low[:], lo[:, :, 0], lo[:, :, 1], ALU.max))
            line.after(dve, nc.vector.tensor_tensor(g_next[:], g_next[:], g_low[:], ALU.max))
            line.after(dve, nc.vector.tensor_tensor(g_best[:], g_best[:], g_next[:], ALU.add))
            mine = g_best[:].unsqueeze(2).to_broadcast([P, NT * GROUPS, GROUPS])
            for g in range(GROUPS):
                of_group = g_best[:].rearrange("p (t g) -> p t g", g=GROUPS)
                mine = of_group[:, :, g:g + 1].to_broadcast([P, NT, GROUPS])
                beats = g_beats[:].rearrange("p (t g) h -> p t g h", g=GROUPS)[:, :, g, :]
                ties = g_ties[:].rearrange("p (t g) h -> p t g h", g=GROUPS)[:, :, g, :]
                line.mark(nc.vector.tensor_tensor(beats, of_group, mine, ALU.is_gt))
                line.mark(nc.vector.tensor_tensor(ties, of_group, mine, ALU.is_equal))
            line.wait(dve)
            earlier = w["earlier"][:].unsqueeze(1).to_broadcast([P, NT, GROUPS * GROUPS])
            ties = g_ties[:].rearrange("p (t g) h -> p t (g h)", g=GROUPS)
            line.after(dve, nc.vector.tensor_tensor(ties, ties, earlier, ALU.mult))
            line.after(dve, nc.vector.tensor_tensor(g_beats[:], g_beats[:], g_ties[:], ALU.add))
            line.after(dve, nc.vector.tensor_reduce(g_rank[:], g_beats[:], AX_X, ALU.add))
            line.after(dve, nc.vector.tensor_scalar(g_rank[:], g_rank[:], float(TOPG), None, ALU.is_lt))
            line.after(dve, nc.vector.tensor_tensor(
                tmp_scores[:].rearrange("p t (g k) -> p (t g) k", g=GROUPS),
                choice[:].rearrange("p t (g k) -> p (t g) k", g=GROUPS),
                g_rank[:].unsqueeze(2).to_broadcast([P, NT * GROUPS, PG]), ALU.mult))
            for t in range(NT):
                line.mark(nc.vector.max(top8[:, t, :], tmp_scores[:, t, :]))
            line.wait(dve)
            pick_top(core, dve, tmp_scores[:], top8, keep, work, TOP1)
            line.after(dve, nc.vector.tensor_tensor(work["gt"][:], scores[:], work["sel"][:], ALU.mult))
            line.after(dve, nc.vector.tensor_reduce(total[:], work["gt"][:], AX_X, ALU.add))
            line.after(dve, nc.vector.tensor_scalar(total[:], total[:], 1e-20, None, ALU.add))
            line.after(dve, nc.vector.reciprocal(total[:], total[:]))
            line.after(dve, nc.vector.tensor_scalar(total[:], total[:], SCALING, None, ALU.mult))
            line.after(dve, nc.vector.tensor_tensor(probs[:, :, 0:E1], work["gt"][:],
                                                    total[:].unsqueeze(2).to_broadcast([P, NT, E1]), ALU.mult))

            def multiply(j, u):
                dve.wait_ge(gate_done, j * UNITS + (u + 1))
                dve.wait_ge(up_done, j * (2 * UNITS) + (2 * u + 2))
                if not (isinstance(j, int) and u < 2):
                    dve.wait_ge(down_done, j * UNITS + (u - 1))
                nc.vector.tensor_tensor(hidden[u % 2][:], gate[u % 2][:],
                                        core.ps[:, UP + 2 * (u % 2) + 1, :], ALU.mult).then_inc(hidden_done, 1)

            def add(j, u):
                for i in range(experts(u)):
                    e = 2 * u + i
                    if i == 0:
                        dve.wait_ge(down_done, j * UNITS + (u + 1))
                    if not (isinstance(j, int) and e == 0):
                        dve.wait_ge(added, j * ADDS + e * TPC)
                    for k in range(TPC):
                        t = j * TPC + k
                        xs = core.x[:, bass.ds(t, 1), :].rearrange("p t d -> p (t d)")
                        nc.vector.scalar_tensor_tensor(out=xs, in0=core.ps[:, DOWN + i, k * P:(k + 1) * P],
                                                       scalar=probs[:, bass.ds(t, 1), e], in1=xs,
                                                       op0=ALU.mult, op1=ALU.add).then_inc(added, 1)

            def body(j):
                for u in range(UNITS):
                    multiply(j, u)
                    if u:
                        add(j, u - 1)
                add(j, UNITS - 1)

            body(0)
            with dve.Fori(1, NC_) as j:
                body(j)
            dve.wait_ge(added, NC_ * ADDS)


def gated_linear_attention(core):
    nc, w = core.nc, core.w
    with ExitStack() as ctx:
        def sb(name, shape, dt=F32):
            return ctx.enter_context(nc.sbuf_tensor(f"g_{name}", shape, dt))

        ln = LayerNorm(core, ctx, "ln_g", core.x, core.xn, core.xnT)
        xnT = core.xnT
        qT = sb("qT", [P, T])
        fT = sb("fT", [P, T])
        kT = sb("kT", [P, T])
        suf = sb("suf", [P, T])
        pre = fT
        qd = [sb(f"qd{i}", [P, T]) for i in range(2)]
        kd = [sb(f"kd{i}", [P, T]) for i in range(2)]
        g1T = suf
        v = sb("v", [P, NT, P])
        gate = sb("gate", [P, NT, P])
        att = sb("att", [P, NT, P])
        k_tok = sb("k_tok", [P, NT, P])
        states = sb("states", [P, NT, P])
        o_gated, o_normed, o_T = core.xn, k_tok, kd[0]
        ln_o = LayerNorm(core, ctx, "ln_go", o_gated, o_normed, o_T[:], w["ln_w"][:], None)

        proj = core.sem("g_proj")
        proj_used = core.sem("g_proj_used")
        f_ready = core.sem("g_f")
        decayed = core.sem("g_decayed")
        level_done = core.sem("g_level_done")
        level_taken = core.sem("g_level_taken")
        turned = core.sem("g_turned")
        k_copied = core.sem("g_k_copied")
        u_done = core.sem("g_u")
        state_done = core.sem("g_state")
        o_done = core.sem("g_o")
        o_taken = core.sem("g_o_taken")
        out_done = core.sem("g_out")
        added = core.sem("g_added")
        block = ctx.enter_context(nc.Block())
        NSTEP = LEVELS + 1

        @block.tensor
        def _(pe):
            ln.tensor(pe)
            core.loaded(pe, "W_in", "W_g1", "W_g2", "W_out")
            n = 0
            for name in ("lg", "g1", "v", "gate", "q"):
                for c in range(NC_):
                    if n >= 4:
                        pe.wait_ge(proj_used, n - 3)
                    if n < NC_:
                        pe.wait_ge(ln.T_ready, c + 1)
                    if name == "gate":
                        pe.wait_ge(proj_used, 2 * NC_)
                    bank = core.ps[:, 4 + n % 4, :]
                    if name in ("lg", "g1", "q"):
                        weight = {"lg": w["W_in"][:, 2 * P:3 * P], "q": w["W_in"][:, P:2 * P], "g1": w["W_g1"][:]}[name]
                        last = nc.tensor.matmul(bank, weight, xnT[:, c * CH:(c + 1) * CH], start=True, stop=True)
                    else:
                        src, weight = (xnT, w["W_in"][:, 0:P]) if name == "v" else (g1T, w["W_g2"][:])
                        for k in range(TPC):
                            last = nc.tensor.matmul(bank[:, k * P:(k + 1) * P], tile_of(src, c * TPC + k), weight,
                                                    start=True, stop=True)
                    last.then_inc(proj, 1)
                    n += 1
            pe.wait_ge(proj_used, n)
            pe.wait_ge(f_ready, 1)
            for step in range(NSTEP):
                pe.wait_ge(decayed, step)
                kk, qq = (kT, qT) if step == 0 else (kd[step % 2], qd[step % 2])
                for g in range(NC_):
                    if step >= 2:
                        pe.wait_ge(level_taken, (step - 2) * NC_ + g + 1)
                    for k in range(TPC):
                        t = g * TPC + k
                        last = nc.tensor.matmul(core.ps[:, 4 * (step % 2) + g, k * P:(k + 1) * P], tile_of(kk, t),
                                                tile_of(qq, t), start=True, stop=True)
                    last.then_inc(level_done, 1)
            pe.wait_ge(decayed, NSTEP)
            for g in range(NC_):
                pe.wait_ge(level_taken, (NSTEP - 2) * NC_ + g + 1)
                for k in range(TPC):
                    last = nc.tensor.transpose(core.ps[:, g, k * P:(k + 1) * P], tile_of(kd[NSTEP % 2], g * TPC + k),
                                               core.ident[:])
                last.then_inc(turned, 1)
            for g in range(NC_):
                pe.wait_ge(k_copied, g + 1)
                pe.wait_ge(level_taken, (NSTEP - 1) * NC_ + g + 1)
                for k in range(TPC):
                    t = g * TPC + k
                    last = nc.tensor.matmul(core.ps[:, 4 + g, k * P:(k + 1) * P], k_tok[:, t, :], v[:, t, :],
                                            start=True, stop=True)
                last.then_inc(u_done, 1)
            pe.wait_ge(k_copied, NC_)
            for g in range(NC_):
                for k in range(TPC):
                    t = g * TPC + k
                    bank = core.ps[:, g, k * P:(k + 1) * P]
                    last = nc.tensor.matmul(bank, att[:, t, :], v[:, t, :], start=True, stop=t == 0)
                    if t:
                        pe.wait_ge(state_done, t)
                        last = nc.tensor.matmul(bank, tile_of(qd[NSTEP % 2], t), states[:, t, :], start=False, stop=True)
                last.then_inc(o_done, 1)
            pe.wait_ge(o_taken, NC_)
            ln_o.tensor(pe)
            pe.wait_ge(state_done, NT - 1)
            for g in range(NC_):
                pe.wait_ge(ln_o.T_ready, g + 1)
                for k in range(TPC):
                    last = nc.tensor.matmul(core.ps[:, 4 + g, k * P:(k + 1) * P], tile_of(o_T, g * TPC + k),
                                            w["W_out"][:], start=True, stop=True)
                last.then_inc(out_done, 1)

        @block.scalar
        def _(act):
            core.loaded(act, "ln_w")
            ln.scalar(act)
            n = 0
            for name in ("lg", "g1", "v", "gate", "q"):
                for c in range(NC_):
                    act.wait_ge(proj, n + 1)
                    src = core.ps[:, 4 + n % 4, :]
                    cols = slice(c * CH, (c + 1) * CH)
                    by_tile = src.rearrange("p (k d) -> p k d", d=P)
                    if name == "lg":
                        ins = nc.scalar.activation(fT[:, cols], src, ACT.Tanh, scale=0.5)
                    elif name == "g1":
                        ins = nc.scalar.copy(g1T[:, cols], src)
                    elif name == "v":
                        ins = nc.scalar.copy(v[:, c * TPC:(c + 1) * TPC, :], by_tile)
                    elif name == "gate":
                        ins = nc.scalar.activation(gate[:, c * TPC:(c + 1) * TPC, :], by_tile, ACT.Tanh, scale=0.5)
                    else:
                        ins = nc.scalar.activation(qT[:, cols], src, ACT.Silu)
                    ins.then_inc(proj_used, 1)
                    n += 1
            for g in range(NC_):
                act.wait_ge(turned, g + 1)
                nc.scalar.copy(k_tok[:, g * TPC:(g + 1) * TPC, :],
                               core.ps[:, g, :].rearrange("p (k d) -> p k d", d=P)).then_inc(k_copied, 1)
            ln_o.scalar(act)

        @block.vector
        def _(dve):
            line = core.dve_line
            core.loaded(dve, "masks")
            ln.vector(dve)
            dve.wait_ge(proj_used, NC_)
            nc.vector.tensor_scalar(kT[:], fT[:], -0.5, 0.5, ALU.mult, ALU.add).then_inc(f_ready, 1)
            dve.wait_ge(f_ready, 1)
            line.after(dve, nc.vector.tensor_scalar(fT[:], fT[:], 0.5, 0.5, ALU.mult, ALU.add))
            dve.wait_ge(proj_used, 4 * NC_)
            dve.wait_ge(proj, 4 * NC_)
            line.mark(nc.vector.tensor_scalar(gate[:], gate[:], 0.5, 0.5, ALU.mult, ALU.add))
            line.after(dve, nc.vector.memset(suf[:], 1.0))
            dve.wait_ge(proj_used, 5 * NC_)

            def take(step):
                for g in range(NC_):
                    dve.wait_ge(level_done, step * NC_ + g + 1)
                    src = core.ps[:, 4 * (step % 2) + g, :].rearrange("p (k d) -> p k d", d=P)
                    dst = att[:, g * TPC:(g + 1) * TPC, :]
                    if step == 0:
                        ins = nc.vector.tensor_tensor(dst, src, core.ident[:].unsqueeze(1).to_broadcast([P, TPC, P]),
                                                      ALU.mult)
                    else:
                        dve.wait_ge(level_taken, (step - 1) * NC_ + g + 1)
                        ins = nc.vector.copy_predicated(
                            dst, w["masks"][:, step - 1, :].unsqueeze(1).to_broadcast([P, TPC, P]), src)
                    ins.then_inc(level_taken, 1)

            for step in range(1, NSTEP):
                half = 1 << (step - 1)
                if step >= 3:
                    dve.wait_ge(level_done, (step - 1) * NC_)
                q_out, k_out = qd[step % 2], kd[step % 2]
                if step <= 2:
                    line.mark(nc.vector.tensor_tensor(k_out[:], kT[:], suf[:], ALU.mult))
                    line.wait(dve)
                    nc.vector.tensor_tensor(q_out[:], qT[:], pre[:], ALU.mult).then_inc(decayed, 1)
                else:
                    def part(a, side):
                        return a[:].rearrange("p (n i h) -> p n i h", i=2, h=half)[:, :, side, :]
                    line.after(dve, nc.vector.tensor_tensor(part(k_out, 0), part(kT, 0), part(suf, 0), ALU.mult))
                    nc.vector.tensor_tensor(part(q_out, 1), part(qT, 1), part(pre, 1), ALU.mult).then_inc(decayed, 1)
                dve.wait_ge(decayed, step)
                blocks = [a[:].rearrange("p (n i h) -> p n i h", i=2, h=half) for a in (pre, suf)]
                ends = blocks[0][:, :, :, half - 1:half]
                shape = [P, T // (2 * half), half]
                line.after(dve, nc.vector.tensor_tensor(blocks[1][:, :, 0, :], blocks[1][:, :, 0, :],
                                                        ends[:, :, 1, :].to_broadcast(shape), ALU.mult))
                line.after(dve, nc.vector.tensor_tensor(blocks[0][:, :, 1, :], blocks[0][:, :, 1, :],
                                                        ends[:, :, 0, :].to_broadcast(shape), ALU.mult))
                take(step - 1)
            dve.wait_ge(level_done, (NSTEP - 1) * NC_)
            line.mark(nc.vector.tensor_tensor(qd[NSTEP % 2][:], qT[:], pre[:], ALU.mult))
            line.wait(dve)
            nc.vector.tensor_tensor(kd[NSTEP % 2][:], kT[:], suf[:], ALU.mult).then_inc(decayed, 1)
            take(NSTEP - 1)
            for t in range(1, NT):
                if (t - 1) % TPC == 0:
                    dve.wait_ge(u_done, (t - 1) // TPC + 1)
                u = core.ps[:, 4 + (t - 1) // TPC, ((t - 1) % TPC) * P:((t - 1) % TPC + 1) * P]
                if t == 1:
                    ins = nc.vector.tensor_copy(states[:, t, :], u)
                else:
                    dve.wait_ge(state_done, t - 1)
                    ins = nc.vector.scalar_tensor_tensor(out=states[:, t, :], in0=states[:, t - 1, :],
                                                         scalar=pre[:, t * P - 1:t * P], in1=u,
                                                         op0=ALU.mult, op1=ALU.add)
                ins.then_inc(state_done, 1)
            for g in range(NC_):
                dve.wait_ge(o_done, g + 1)
                cols = slice(g * TPC, (g + 1) * TPC)
                nc.vector.tensor_tensor(o_gated[:, cols, :], core.ps[:, g, :].rearrange("p (k d) -> p k d", d=P),
                                        gate[:, cols, :], ALU.mult).then_inc(o_taken, 1)
            dve.wait_ge(o_taken, NC_)
            ln_o.vector(dve)
            for g in range(NC_):
                dve.wait_ge(out_done, g + 1)
                xc = core.x[:, g * TPC:(g + 1) * TPC, :]
                nc.vector.tensor_tensor(xc, xc, core.ps[:, 4 + g, :].rearrange("p (k d) -> p k d", d=P),
                                        ALU.add).then_inc(added, 1)
            dve.wait_ge(added, NC_)


WEIGHTS = {
    "Wq0": ("L0_attn_a_Wq", lambda a: a.T),
    "Wk0": ("L0_attn_a_Wk", lambda a: a.T),
    "Wv0": ("L0_attn_a_Wv", lambda a: a.T),
    "Wu0": ("L0_attn_a_Wu", lambda a: a.T),
    "bu": ("L0_attn_a_bu", lambda a: np.broadcast_to(a, (P, P))),
    "gate0": ("L0_ffn_gate_w", lambda a: a.T),
    "w12": ("L0_ffn_w12", lambda a: a.transpose(2, 0, 1)),
    "w3": ("L0_ffn_w3", lambda a: a.reshape(E0, P, H0 // P, P).transpose(3, 0, 2, 1)),
    "norm_g": ("L0_attn_b_norm_g", lambda a: a[:, None]),
    "norm_b": ("L0_attn_b_norm_b", lambda a: a[:, None]),
    "in_proj": ("L0_attn_b_in_proj_w", lambda a: a.T),
    "conv_w": ("L0_attn_b_conv_w", lambda a: a.reshape(ND, P, DCONV).transpose(1, 0, 2)),
    "conv_b": ("L0_attn_b_conv_b", lambda a: a.reshape(ND, P).T),
    "x_bc": ("L0_attn_b_x_proj_w", lambda a: np.tile(a[DTR:].T, (1, 3)).reshape(ND, P, 3 * 2 * DS).transpose(1, 0, 2)),
    "x_dt": ("L0_attn_b_x_proj_w", lambda a: a[:DTR].T.reshape(ND, P, DTR).transpose(1, 0, 2)),
    "dt_proj": ("L0_attn_b_dt_proj_w", lambda a: a.T),
    "dt_b": ("L0_attn_b_dt_proj_b", lambda a: a.reshape(ND, P).T),
    "log_A": ("L0_attn_b_log_A", lambda a: a.reshape(ND, P, DS).transpose(1, 0, 2)),
    "Dp": ("L0_attn_b_Dp", lambda a: a.reshape(ND, P).T),
    "out_proj": ("L0_attn_b_out_proj_w", lambda a: a.T.reshape(ND, P, P).transpose(1, 0, 2)),
    "Wq1": ("L1_attn_a_Wq", lambda a: a),
    "Wk1": ("L1_attn_a_Wk", lambda a: a),
    "Wv1": ("L1_attn_a_Wv", lambda a: a),
    "Wo1": ("L1_attn_a_Wo", lambda a: a),
    "bo": ("L1_attn_a_bo", lambda a: np.broadcast_to(a, (P, P))),
    "gate1": ("L1_ffn_gate_w", lambda a: a.T),
    "e_bias": ("L1_ffn_e_bias", lambda a: np.broadcast_to(a, (P, E1))),
    "w_up1": (("L1_ffn_gate_proj", "L1_ffn_up_proj"),
              lambda g, u: np.stack([a.reshape(E1 // 2, 2 * I1, P) for a in (g, u)], 1).transpose(3, 0, 1, 2)),
    "w_down1": ("L1_ffn_down_proj", lambda a: a.reshape(E1 // 2, 2, P, I1).transpose(1, 3, 0, 2).reshape(2 * I1, E1 // 2, P)),
    "sh_up": (("L1_ffn_shared_gate_w", "L1_ffn_shared_up_w"), lambda g, u: np.pad(np.stack([g, u], 0), ((0, 0), (0, I1), (0, 0))).transpose(2, 0, 1)),
    "sh_down": ("L1_ffn_shared_down_w", lambda a: a.T),
    "W_in": ("L1_attn_b_W_in", lambda a: a.T),
    "W_out": ("L1_attn_b_W_out", lambda a: a.T),
    "W_g1": ("L1_attn_b_W_g1", lambda a: a.T),
    "W_g2": ("L1_attn_b_W_g2", lambda a: a.T),
    "ln_w": ("L1_attn_b_ln_w", lambda a: a[:, None]),
}


def constants():
    pick = np.zeros((96, 2 * DS, P), np.uint16)
    for s in range(2 * DS):
        pick[[s, 2 * DS + s, 4 * DS + s], s, :] = 0x3F80
    i = np.arange(P)
    masks = [(i[:, None] // (2 << n) == i // (2 << n)) & (i[:, None] // (1 << n) % 2 == 0) & (i // (1 << n) % 2 == 1)
             for n in range(LEVELS)]
    earlier = np.tril(np.ones((GROUPS, GROUPS), np.float32), -1)
    return {"pick": pick, "masks": np.stack(masks, 1).astype(np.int32),
            "earlier": np.broadcast_to(earlier.reshape(1, -1), (P, GROUPS * GROUPS))}


def stack(nc, x, out, weights, ident, stages):
    with ExitStack() as ctx:
        core = Core(nc, ctx)
        core.ps = ctx.enter_context(nc.psum_tensor("ps", [P, 8, CH], F32))
        core.x = core.sb("x_res", [P, NT, P])
        core.xn = core.sb("xn", [P, NT, P])
        core.xnT = core.sb("xnT", [P, T])
        core.ident = core.sb("ident", [P, P])
        core.o_zeroed = core.sem("o_zeroed")
        x_loaded, out_stored = core.sem("x_loaded"), core.sem("out_stored")
        w_loaded = {}
        for name, ap in weights.items():
            core.w[name] = core.sb(f"w_{name}", list(ap.shape), ap.dtype)
            w_loaded[name] = core.sem(f"loaded_{name}")

        def loaded(eng, *names):
            for n in names:
                eng.wait_ge(w_loaded[n], 16)

        core.loaded = loaded
        with nc.Block() as block:
            @block.sync
            def _(sp):
                sp.dma_start(core.ident[:], ident).then_inc(x_loaded, 16)
                sp.dma_start(core.x[:], x[0].rearrange("(t p) d -> p t d", p=P)).then_inc(x_loaded, 16)
                for name, ap in weights.items():
                    sp.dma_start(core.w[name][:], ap).then_inc(w_loaded[name], 16)
                sp.wait_ge(x_loaded, 32)
        for stage in stages:
            core.run_stage(*stage)
        with nc.Block() as block:
            @block.sync
            def _(sp):
                sp.dma_start(out[0].rearrange("(t p) d -> p t d", p=P), core.x[:]).then_inc(out_stored, 16)
                sp.wait_ge(out_stored, 16)
                for name in weights:
                    sp.wait_ge(w_loaded[name], 16)


STAGES = ((softmax_attention,), (experts_top2, "e1"), (selective_scan,), (experts_top2, "e2"),
          (linear_attention,), (experts_top4, "m1"), (gated_linear_attention,), (experts_top4, "m2"))


def kernel(**inputs):
    import concourse.bacc as bacc
    from concourse.bass_utils import run_bass_kernel_spmd

    nc = bacc.Bacc("TRN2", target_bir_lowering=False, num_devices=1)
    arrays, aps = {}, {}

    def given(name, a):
        a = np.ascontiguousarray(a)
        arrays[name] = a
        return nc.dram_tensor(name, a.shape, mybir.dt.from_np(a.dtype), kind="ExternalInput").ap()

    x = given("x_dram", inputs["L0_attn_a_x"])
    ident = given("ident_dram", np.eye(P, dtype=np.float32))
    for name, (source, layout) in WEIGHTS.items():
        sources = (source,) if isinstance(source, str) else source
        aps[name] = given(f"{name}_dram", layout(*(np.asarray(inputs[n]) for n in sources)))
    for name, a in constants().items():
        aps[name] = given(f"{name}_dram", a)
    out = nc.dram_tensor("out_dram", (1, T, P), F32, kind="ExternalOutput").ap()
    stack(nc, x, out, aps, ident, STAGES)
    r = run_bass_kernel_spmd(nc, [arrays], core_ids=[0])
    return r.results[0]["out_dram"]
```

```python
from contextlib import ExitStack

import numpy as np

import concourse.bass as bass
from concourse import mybir

ALU = mybir.AluOpType
ACT = mybir.ActivationFunctionType
F32 = mybir.dt.float32
BF16 = mybir.dt.bfloat16
U32 = mybir.dt.uint32
AX_X = mybir.AxisListType.X

P = 128
T = 2048
NT = T // P
CH = 512
NC_ = T // CH
TPC = CH // P
EPS = 1e-5

HEADS = 16
HD = P // HEADS
E0, H0, TOP0 = 8, 256, 2
DI, DS, DCONV, DTR = 256, 16, 4, 8
ND = DI // P
E1, I1, GROUPS, TOPG, TOP1 = 16, 64, 4, 2, 4
SCALING = 2.5
LEVELS = 7


class Line:

    def __init__(self, sem):
        self.sem, self.n = sem, 0

    def mark(self, ins):
        self.n += 1
        ins.then_inc(self.sem, 1)

    def wait(self, eng):
        eng.wait_ge(self.sem, self.n)

    def after(self, eng, ins):
        self.mark(ins)
        self.wait(eng)


class Core:

    def __init__(self, nc, ctx):
        self.nc, self.ctx = nc, ctx
        self.w = {}
        self.stage_sems = []
        self.dve_line = Line(self.sem("dve_line"))
        self.act_line = Line(self.sem("act_line"))
        self.stage_sems = []

    def sem(self, name):
        self.stage_sems.append(self.nc.alloc_semaphore(name=name))
        return self.stage_sems[-1]

    def sb(self, name, shape, dt=F32):
        return self.ctx.enter_context(self.nc.sbuf_tensor(name, shape, dt))

    def clear_sems(self):
        self.nc.clear_and_free_semaphores(self.stage_sems)
        self.nc.all_engine_barrier()
        self.stage_sems = []


def tile_of(a, t):
    return a[:, t * P:(t + 1) * P]


class LayerNorm:

    def __init__(self, core, ctx, name, src, out, outT, gain=None, shift=None, banks=(0, 1)):
        nc = core.nc
        self.core, self.src, self.out, self.outT = core, src, out, outT
        self.gain, self.shift, self.banks = gain, shift, banks

        def sb(n, shape):
            return ctx.enter_context(nc.sbuf_tensor(f"{name}_{n}", shape, F32))

        self.stats = sb("stats", [P, NT, 6])
        self.mv = sb("mv", [P, NT, 2])
        self.veps = sb("veps", [P, NT])
        self.root = sb("root", [P, NT])
        self.warm = sb("warm", [P, 1])
        self.parts = (slice(0, TPC), slice(TPC, NT))
        self.r0 = sb("r0", [P, NT])
        self.r2 = sb("r2", [P, NT])
        self.rstd = sb("rstd", [P, NT])
        self.var_ready = core.sem(f"{name}_var_ready")
        self.rooted = core.sem(f"{name}_rooted")
        self.normed = core.sem(f"{name}_normed")
        self.turned = core.sem(f"{name}_turned")
        self.T_ready = core.sem(f"{name}_T_ready")

    def vector(self, dve):
        nc, line = self.core.nc, self.core.dve_line
        for i, part in enumerate(self.parts):
            tiles = range(part.start, part.stop)
            for t in tiles:
                line.mark(nc.vector.bn_stats(self.stats[:, t, :], self.src[:, t, :]))
            line.wait(dve)
            for t in tiles:
                line.mark(nc.vector.bn_aggr(self.mv[:, t, :], self.stats[:, t, :]))
            line.wait(dve)
            veps, root, r0, r2, rstd = (a[:, part] for a in (self.veps, self.root, self.r0, self.r2, self.rstd))
            nc.vector.tensor_scalar(veps, self.mv[:, part, 1], EPS, None, ALU.add).then_inc(self.var_ready, 1)
            dve.wait_ge(self.rooted, i + 1)
            line.after(dve, nc.vector.reciprocal(r0, root))
            line.after(dve, nc.vector.tensor_tensor(r2, r0, r0, ALU.mult))
            line.after(dve, nc.vector.tensor_tensor(r2, r2, veps, ALU.mult))
            line.after(dve, nc.vector.tensor_scalar(r2, r2, -0.5, 1.5, ALU.mult, ALU.add))
            line.after(dve, nc.vector.tensor_tensor(rstd, r0, r2, ALU.mult))
            for t in tiles:
                nc.vector.tensor_scalar(self.out[:, t, :], self.src[:, t, :], self.mv[:, t, 0:1], self.rstd[:, t:t + 1],
                                        ALU.subtract, ALU.mult).then_inc(self.normed, 1)

    def scalar(self, act):
        nc = self.core.nc
        self.core.act_line.after(act, nc.scalar.activation(self.warm[:], self.core.one[:], ACT.Sqrt))
        for i, part in enumerate(self.parts):
            act.wait_ge(self.var_ready, i + 1)
            nc.scalar.activation(self.root[:, part], self.veps[:, part], ACT.Sqrt).then_inc(self.rooted, 1)
            if self.outT is not None:
                self.copy_turned(act, range(part.start // TPC, part.stop // TPC))

    def copy_turned(self, act, chunks):
        nc = self.core.nc
        for c in chunks:
            act.wait_ge(self.turned, c + 1)
            bank = self.core.ps[:, self.banks[c % 2], :]
            dst = self.outT[:, c * CH:(c + 1) * CH]
            if self.gain is None:
                nc.scalar.copy(dst, bank).then_inc(self.T_ready, 1)
            elif self.shift is None:
                nc.scalar.activation(dst, bank, ACT.Identity, scale=self.gain).then_inc(self.T_ready, 1)
            else:
                nc.scalar.activation(dst, bank, ACT.Identity, bias=self.shift, scale=self.gain).then_inc(self.T_ready, 1)

    def tensor(self, pe, then=lambda c: None):
        nc, core = self.core.nc, self.core
        for c in range(NC_):
            if c >= 2:
                pe.wait_ge(self.T_ready, c - 1)
            for k in range(TPC):
                pe.wait_ge(self.normed, c * TPC + k + 1)
                last = nc.tensor.transpose(core.ps[:, self.banks[c % 2], k * P:(k + 1) * P],
                                           self.out[:, c * TPC + k, :], core.ident[:])
            last.then_inc(self.turned, 1)
            for done in {0: (0,), 1: (), NC_ - 1: (NC_ - 2, NC_ - 1)}.get(c, (c - 1,)):
                then(done)


def softmax_attention(core):
    nc, w = core.nc, core.w
    SCALE = float(HD) ** -0.5
    NPART, KROWS = 3, 6 * HD
    ROWS = KROWS + NPART
    QPARTS = ((0, 3), (0, 2), (0, 1))
    KPARTS = (0, 0, 0, 1, 1, 2)
    RING = 4
    LAG_S = NT + 3
    LAG_V = LAG_S + 2
    NBUF = 3
    BODY = NBUF * NT
    LOOPED = (HEADS - 1) // NBUF
    S_BANK, S_RING, O_BANK = 4, 3, 7
    VROWS = 2 * HD
    with ExitStack() as ctx:
        def sb(name, shape, dt=F32):
            return ctx.enter_context(nc.sbuf_tensor(name, shape, dt))

        xn, xnT = core.xn, core.xnT
        ln = LayerNorm(core, ctx, "ln_a", core.x, xn, xnT)
        v_all = sb("v_all", [P, NT, P])
        v_head = [sb(f"v_head{i}", [P, NT, VROWS]) for i in range(NBUF)]
        qst = [sb(f"q_stack{i}", [P, T], BF16) for i in range(NBUF)]
        kst = [sb(f"k_stack{i}", [P, T], BF16) for i in range(NBUF)]
        ones = sb("ones", [NPART, T], BF16)
        probs = sb("probs", [P, RING, T])
        mx = sb("row_max", [P, NT, 2])
        neg_max = sb("neg_max", [P, 32])
        nmT = sb("neg_maxT", [P, 32])
        nm_rest = sb("neg_max_rest", [P, 32])
        nm_parts = sb("neg_max_parts", [P, NPART, 32], BF16)
        o_sb = sb("o_sb", [P, CH])
        whole = sb("whole", [P, T])
        parts = sb("parts", [P, 2, NPART, T], BF16)
        attT, den = whole, xnT
        qd = nc.dram_tensor("q_parts_dram", (HEADS, NPART, HD, T), BF16).ap()
        kd = nc.dram_tensor("k_parts_dram", (HEADS, NPART, HD, T), BF16).ap()
        md = [nc.dram_tensor(f"max_dram{i}", (NPART, T), BF16).ap() for i in range(NBUF)]

        od = nc.dram_tensor("o_dram", (2, HEADS, HD, T), F32).ap()
        proj = core.sem("a_proj")
        proj_used = core.sem("a_proj_used")
        whole_done = core.sem("a_whole")
        split_done = core.sem("a_split")
        parts_stored = core.sem("a_parts_stored")
        masked = core.sem("a_masked")
        ones_set = core.sem("a_ones")
        ones_placed = core.sem("a_ones_placed")
        stacked = [core.sem(f"a_stacked{i}") for i in range(NBUF)]
        p1_done = core.sem("a_pass1_scores")
        max_done = core.sem("a_max_done")
        nm_line = core.sem("a_nm_line")
        nm_ready = core.sem("a_nm_ready")
        m_stored = core.sem("a_max_stored")
        m_loaded = [core.sem(f"a_max_loaded{i}") for i in range(NBUF)]
        v_staged = core.sem("a_v_staged")
        s_done = core.sem("a_scores")
        exp_done = core.sem("a_exp")
        pv_done = core.sem("a_pv")
        evacuated = core.sem("a_evacuated")
        o_stored = core.sem("a_o_stored")
        fin_loaded = core.sem("a_fin_loaded")
        rden_ready = core.sem("a_rden_ready")
        att_ready = core.sem("a_att_ready")
        out_done = core.sem("a_out_done")
        bias_added = core.sem("a_bias_added")

        block = ctx.enter_context(nc.Block())
        O_STORE = 16 * NC_
        STACK = 16 * (len(QPARTS) + len(KPARTS))

        @block.sync
        def _(sp):
            core.load_weights(sp)
            for which, dram in enumerate((qd, kd)):
                sp.wait_ge(split_done, 5 * (which + 1))
                for p in range(NPART):
                    sp.dma_start(dram[:, p].rearrange("h s t -> h s t"),
                                 parts[:, which, p, :]).then_inc(parts_stored, 16)
            sp.wait_ge(parts_stored, 16 * 2 * NPART)
            sp.wait_ge(ones_set, 3 * NBUF + 1)
            for buf in range(NBUF):
                sp.dma_start(kst[buf][KROWS:ROWS, :], ones[:]).then_inc(ones_placed, 16)

            def load_stack(head, par):
                row = 0
                for first, n in QPARTS:
                    sp.dma_start(qst[par][row:row + n * HD, :],
                                 qd[head, first:first + n].rearrange("p s t -> (p s) t")).then_inc(stacked[par], 16)
                    row += n * HD
                for i, part in enumerate(KPARTS):
                    sp.dma_start(kst[par][i * HD:(i + 1) * HD, :], kd[head, part]).then_inc(stacked[par], 16)

            def store_max(head, par):
                sp.wait_ge(nm_ready, head + 1)
                for b in range(P // 32):
                    sp.dma_start(md[par].rearrange("p (j b i) -> b j p i", b=P // 32, i=32)[b],
                                   nm_parts[32 * b:32 * b + NT, :, :]).then_inc(m_stored, 16)
                sp.wait_ge(m_stored, (head + 1) * 64)
                sp.dma_start(qst[par][KROWS:ROWS, :], md[par]).then_inc(m_loaded[par], 16)

            def store_o(head):
                sp.wait_ge(evacuated, head + 1)
                for c in range(NC_):
                    sp.dma_start(od[:, head, :, c * CH:(c + 1) * CH],
                                 o_sb[32 * c:32 * c + VROWS, :]).then_inc(o_stored, 16)

            for head in range(NBUF):
                load_stack(head, head)
            for head in range(NBUF - 1):
                store_max(head, head)
            store_o(0)
            with sp.Fori(1, LOOPED) as j:
                for par in range(NBUF):
                    sp.wait_ge(s_done, j * (4 * BODY) + (par + 1 - NBUF) * 4 * NT)
                    load_stack(j * NBUF + par, par)
                    store_max(j * NBUF + (par - 1), (par - 1) % NBUF)
                    store_o(j * NBUF + (par - 2))
            sp.wait_ge(s_done, (HEADS - NBUF) * 4 * NT)
            load_stack(HEADS - 1, (HEADS - 1) % NBUF)
            store_max(HEADS - 2, (HEADS - 2) % NBUF)
            store_o(HEADS - 3)
            store_max(HEADS - 1, (HEADS - 1) % NBUF)
            for head in (HEADS - 2, HEADS - 1):
                store_o(head)
            sp.wait_ge(o_stored, O_STORE * HEADS)
            for which, dst in enumerate((attT, den)):
                sp.dma_start(dst[:], od[which]).then_inc(fin_loaded, 16)

        @block.gpsimd
        def _(pool):
            core.loaded(pool, "Wq0", "Wk0")
            for name, sign in (("Wq0", 1), ("Wk0", -1)):
                nc.gpsimd.affine_select(out=w[name][:], in_=w[name][:], pattern=[[sign, P]], channel_multiplier=-sign,
                                        base=0, compare_op=ALU.is_ge, fill=0.0).then_inc(masked, 1)
            nc.gpsimd.memset(ones[:], 1.0).then_inc(ones_set, 1)
            for par in range(NBUF):
                nc.gpsimd.memset(qst[par][:], 0.0).then_inc(ones_set, 1)
                nc.gpsimd.memset(kst[par][:], 0.0).then_inc(ones_set, 1)
                nc.gpsimd.memset(v_head[par][:], 1.0).then_inc(ones_set, 1)
            core.loaded(pool, "bu")
            pool.wait_ge(ln.normed, NT)
            for t in range(NT):
                nc.gpsimd.tensor_tensor(core.x[:, t, :], core.x[:, t, :], w["bu"][:], ALU.add).then_inc(bias_added, 1)
            pool.wait_ge(proj_used, 2 * NC_ + NC_)
            pool.wait_ge(ones_set, 3 * NBUF + 1)

            def stage_v(head, par):
                nc.gpsimd.tensor_copy(v_head[par][:, :, 0:HD], v_all[:, :, bass.ds(head * HD, HD)]).then_inc(v_staged, 1)

            for head in range(NBUF):
                stage_v(head, head)
            with pool.Fori(1, LOOPED) as j:
                for par in range(NBUF):
                    pool.wait_ge(pv_done, j * BODY + (par + 1 - NBUF) * NT)
                    stage_v(j * NBUF + par, par)
            pool.wait_ge(pv_done, (HEADS - NBUF) * NT)
            stage_v(HEADS - 1, (HEADS - 1) % NBUF)

        @block.tensor
        def _(pe):
            ln.tensor(pe)
            pe.wait_ge(masked, 2)
            n = 0
            for name in ("Wq0", "Wk0"):
                for c in range(NC_):
                    if name == "Wq0":
                        pe.wait_ge(ln.T_ready, c + 1)
                    if n >= 4:
                        pe.wait_ge(proj_used, n - 3)
                    nc.tensor.matmul(core.ps[:, 4 + n % 4, :], w[name][:], xnT[:, c * CH:(c + 1) * CH],
                                     start=True, stop=True).then_inc(proj, 1)
                    n += 1
            core.loaded(pe, "Wv0")
            for g in range(NC_):
                pe.wait_ge(proj_used, n - 3)
                for k in range(TPC):
                    last = nc.tensor.matmul(core.ps[:, 4 + n % 4, k * P:(k + 1) * P], tile_of(xnT, g * TPC + k),
                                            w["Wv0"][:], start=True, stop=True)
                last.then_inc(proj, 1)
                n += 1
            pe.wait_ge(proj_used, n)

            def slot(j, gs, maxima=True, scores=True, values=True):
                first_body = isinstance(j, int) and j == 0

                def find(b):
                    buf, u = gs // NT % NBUF, gs % NT
                    if u == 0 and b == 0:
                        pe.wait_ge(stacked[buf], j * STACK + STACK)
                    if not first_body or gs:
                        pe.wait_ge(max_done, j * (2 * BODY) + (2 * gs + b - 1))
                    for r in range(2):
                        key = (2 * b + r) * CH
                        last = nc.tensor.matmul(core.ps[:, 2 * b + r, :], qst[buf][0:KROWS, u * P:(u + 1) * P],
                                                kst[buf][0:KROWS, key:key + CH], start=True, stop=True)
                    last.then_inc(p1_done, 1)

                def score(c):
                    m = gs - LAG_S
                    buf, kt = m // NT % NBUF, m % NT
                    if kt == 0 and c == 0:
                        pe.wait_ge(m_loaded[buf], j * 16 + 16 * (m // BODY + 1))
                    n = 4 * m + c
                    if not first_body or n >= S_RING:
                        pe.wait_ge(exp_done, j * (4 * BODY) + (n - S_RING + 1))
                    nc.tensor.matmul(core.ps[:, S_BANK + n % S_RING, :], kst[buf][:, kt * P:(kt + 1) * P],
                                     qst[buf][:, c * CH:(c + 1) * CH], start=True, stop=True).then_inc(s_done, 1)

                for b in range(2):
                    if maxima:
                        find(b)
                    if scores:
                        score(2 * b)
                        score(2 * b + 1)
                if values:
                    m = gs - LAG_V
                    buf, kt = m // NT % NBUF, m % NT
                    if kt == 0:
                        pe.wait_ge(v_staged, j * NBUF + (m // NT + 1))
                        if not first_body or m:
                            pe.wait_ge(evacuated, j * NBUF + m // NT)
                    pe.wait_ge(exp_done, j * (4 * BODY) + 4 * (m + 1))
                    for c in range(NC_):
                        last = nc.tensor.matmul(core.ps[32 * c:32 * c + VROWS, O_BANK, :], v_head[buf][:, kt, :],
                                                probs[:, m % RING, c * CH:(c + 1) * CH],
                                                start=kt == 0, stop=kt == NT - 1)
                    last.then_inc(pv_done, 1)

            pe.wait_ge(ones_placed, 16 * NBUF)
            for gs in range(BODY):
                slot(0, gs, True, gs >= LAG_S, gs >= LAG_V)
            with pe.Fori(1, LOOPED) as j:
                for gs in range(BODY):
                    slot(j, gs)
            for gs in range(NT + LAG_V):
                slot(LOOPED, gs, gs < NT, gs < NT + LAG_S)
            core.loaded(pe, "Wu0")
            for g in range(NC_):
                pe.wait_ge(att_ready, g + 1)
                for k in range(TPC):
                    last = nc.tensor.matmul(core.ps[:, g, k * P:(k + 1) * P], tile_of(attT, g * TPC + k), w["Wu0"][:],
                                            start=True, stop=True)
                last.then_inc(out_done, 1)

        @block.scalar
        def _(act):
            ln.scalar(act)
            for which, scale in enumerate((SCALE, 1.0)):
                for c in range(NC_):
                    act.wait_ge(proj, which * NC_ + c + 1)
                    if which == 1 and c == 0:
                        act.wait_ge(split_done, 5)
                    nc.scalar.mul(whole[:, c * CH:(c + 1) * CH], core.ps[:, 4 + c, :], scale).then_inc(proj_used, 1)
            for g in range(NC_):
                act.wait_ge(proj, 2 * NC_ + g + 1)
                nc.scalar.copy(v_all[:, g * TPC:(g + 1) * TPC, :],
                               core.ps[:, 4 + g, :].rearrange("p (k d) -> p k d", d=P)).then_inc(proj_used, 1)

            def unit(j, us, first=False):
                if not first:
                    act.wait_ge(pv_done, j * BODY + (us - (RING - 1)))
                for c in range(NC_):
                    n = us * NC_ + c
                    act.wait_ge(s_done, j * (4 * BODY) + (n + 1))
                    nc.scalar.activation(probs[:, us % RING, c * CH:(c + 1) * CH], core.ps[:, S_BANK + n % S_RING, :],
                                         ACT.Exp).then_inc(exp_done, 1)

            def evacuate(head):
                act.wait_ge(pv_done, head * NT + NT)
                if not isinstance(head, int) or head:
                    act.wait_ge(o_stored, head * O_STORE)
                nc.scalar.copy(o_sb[:], core.ps[:, O_BANK, :]).then_inc(evacuated, 1)

            act.wait_ge(core.o_zeroed, 1)

            def body(j, units, first=False):
                for us in range(units):
                    unit(j, us, first and us < RING)
                    if us % NT == 2 and not (first and us == 2):
                        evacuate(j * NBUF + (us // NT - 1))

            body(0, BODY, first=True)
            with act.Fori(1, LOOPED) as j:
                body(j, BODY)
            body(LOOPED, NT)
            evacuate(HEADS - 1)

        @block.vector
        def _(dve):
            line = core.dve_line
            nc.vector.memset(core.ps[:, O_BANK, :], 0.0).then_inc(core.o_zeroed, 1)
            line.after(dve, nc.vector.memset(neg_max[:], 0.0))
            ln.vector(dve)
            for which in range(2):
                dve.wait_ge(proj_used, NC_ * (which + 1))
                pt = [parts[:, which, p, :] for p in range(NPART)]
                base = 5 * which
                nc.vector.tensor_copy(pt[0], whole[:]).then_inc(split_done, 1)
                dve.wait_ge(split_done, base + 1)
                nc.vector.tensor_tensor(whole[:], whole[:], pt[0], ALU.subtract).then_inc(split_done, 1)
                dve.wait_ge(split_done, base + 2)
                nc.vector.tensor_copy(pt[1], whole[:]).then_inc(split_done, 1)
                dve.wait_ge(split_done, base + 3)
                nc.vector.tensor_tensor(whole[:], whole[:], pt[1], ALU.subtract).then_inc(split_done, 1)
                dve.wait_ge(split_done, base + 4)
                nc.vector.tensor_copy(pt[2], whole[:]).then_inc(split_done, 1)

            def maxima(head, first_unit):
                for u in range(NT):
                    for b in range(2):
                        dve.wait_ge(p1_done, first_unit * 2 + (2 * u + b + 1))
                        nc.vector.tensor_reduce(mx[:, u, b:b + 1], core.ps[:, 2 * b:2 * b + 2, :],
                                                mybir.AxisListType.XY, ALU.max).then_inc(max_done, 1)
                dve.wait_ge(max_done, head * (2 * NT) + 2 * NT)
                step = [0]

                def then(ins):
                    step[0] += 1
                    ins.then_inc(nm_line, 1)
                    dve.wait_ge(nm_line, head * 6 + step[0])

                then(nc.vector.tensor_reduce(neg_max[:, 0:NT], mx[:], AX_X, ALU.max, negate=True))
                then(nc.vector.transpose(nmT[:], neg_max[:]))
                if not isinstance(head, int) or head:
                    dve.wait_ge(m_stored, head * 64)
                then(nc.vector.tensor_copy(nm_parts[:, 0, :], nmT[:]))
                then(nc.vector.tensor_tensor(nm_rest[:], nmT[:], nm_parts[:, 0, :], ALU.subtract))
                then(nc.vector.tensor_copy(nm_parts[:, 1, :], nm_rest[:]))
                then(nc.vector.tensor_tensor(nm_rest[:], nm_rest[:], nm_parts[:, 1, :], ALU.subtract))
                nc.vector.tensor_copy(nm_parts[:, 2, :], nm_rest[:]).then_inc(nm_ready, 1)

            maxima(0, 0)
            with dve.Fori(1, HEADS) as i:
                dve.wait_ge(nm_ready, i)
                maxima(i, i * NT)
            for c in range(NC_):
                cols = slice(c * CH, (c + 1) * CH)
                if c == 0:
                    dve.wait_ge(fin_loaded, 32)
                nc.vector.reciprocal(den[:, cols], den[:, cols]).then_inc(rden_ready, 1)
                dve.wait_ge(rden_ready, c + 1)
                nc.vector.tensor_tensor(attT[:, cols], attT[:, cols], den[:, cols], ALU.mult).then_inc(att_ready, 1)
            dve.wait_ge(bias_added, NT)
            for g in range(NC_):
                dve.wait_ge(out_done, g + 1)
                xs = core.x[:, g * TPC:(g + 1) * TPC, :]
                line.mark(nc.vector.tensor_tensor(xs, xs, core.ps[:, g, :].rearrange("p (k d) -> p k d", d=P), ALU.add))
            line.wait(dve)


def pick_top(core, dve, scores, top8, keep, work, k):
    nc, line = core.nc, core.dve_line
    ne = scores.shape[-1]
    kth = top8[:, :, k - 1:k].to_broadcast([P, NT, ne])
    line.mark(nc.vector.tensor_tensor(work["gt"][:], scores, kth, ALU.is_gt))
    line.after(dve, nc.vector.tensor_tensor(work["eq"][:], scores, kth, ALU.is_equal))
    line.mark(nc.vector.tensor_tensor_scan(out=work["nth"][:].rearrange("p t e -> p (t e)"),
                                           data0=keep[:].rearrange("p t e -> p (t e)"),
                                           data1=work["eq"][:].rearrange("p t e -> p (t e)"),
                                           initial=0.0, op0=ALU.mult, op1=ALU.add))
    line.after(dve, nc.vector.tensor_reduce(work["above"][:], work["gt"][:], AX_X, ALU.add))
    line.after(dve, nc.vector.tensor_scalar(work["room"][:], work["above"][:], -1.0, float(k), ALU.mult, ALU.add))
    line.after(dve, nc.vector.tensor_tensor(work["nth"][:], work["nth"][:],
                                            work["room"][:].unsqueeze(2).to_broadcast([P, NT, ne]), ALU.is_le))
    line.after(dve, nc.vector.tensor_tensor(work["nth"][:], work["nth"][:], work["eq"][:], ALU.mult))
    line.after(dve, nc.vector.tensor_tensor(work["sel"][:], work["gt"][:], work["nth"][:], ALU.add))


def experts_top2(core, tag):
    nc, w = core.nc, core.w
    NH = H0 // P
    UNITS = E0 * NH
    UP, DOWN = 0, 4
    with ExitStack() as ctx:
        def sb(name, shape, dt=F32):
            return ctx.enter_context(nc.sbuf_tensor(f"{tag}_{name}", shape, dt))

        ln = LayerNorm(core, ctx, f"ln_{tag}", core.x, core.xn, core.xnT, banks=(4, 5))
        xnT = core.xnT
        scores = sb("scores", [P, NT, E0])
        top8 = sb("top8", [P, NT, 8])
        keep = sb("keep", [P, NT, E0])
        work = {n: sb(n, [P, NT, E0]) for n in ("gt", "eq", "nth", "sel")}
        work.update({n: sb(n, [P, NT]) for n in ("above", "room")})
        expd = sb("expd", [P, NT, E0])
        probs = sb("probs", [P, NT, E0])
        total = sb("total", [P, NT])
        gate = [sb(f"gate{i}", [P, CH]) for i in range(2)]
        hidden = [sb(f"hidden{i}", [P, NH, CH]) for i in range(2)]

        scored = core.sem(f"{tag}_scored")
        exp_in = core.sem(f"{tag}_exp_in")
        exp_out = core.sem(f"{tag}_exp_out")
        up_done = core.sem(f"{tag}_up")
        gate_done = core.sem(f"{tag}_gate")
        hidden_done = core.sem(f"{tag}_hidden")
        down_done = core.sem(f"{tag}_down")
        added = core.sem(f"{tag}_added")
        block = ctx.enter_context(nc.Block())

        @block.tensor
        def _(pe):
            core.loaded(pe, "gate0", "w12", "w3")

            def up(j, u, chunk):
                e, half = u // NH, u % NH
                if not (isinstance(j, int) and u < 2):
                    pe.wait_ge(hidden_done, j * UNITS + (u - 1))
                for k in range(2):
                    col = (k * NH + half) * P
                    nc.tensor.matmul(core.ps[:, UP + 2 * (u % 2) + k, :], w["w12"][:, e, col:col + P],
                                     chunk, start=True, stop=True).then_inc(up_done, 1)

            def down(j, e):
                pe.wait_ge(hidden_done, j * UNITS + (e + 1) * NH)
                if not (isinstance(j, int) and e < 2):
                    pe.wait_ge(added, j * (E0 * TPC) + (e - 1) * TPC)
                for k in range(TPC):
                    for half in range(NH):
                        last = nc.tensor.matmul(core.ps[:, DOWN + e % 2, k * P:(k + 1) * P],
                                                hidden[e % 2][:, half, k * P:(k + 1) * P], w["w3"][:, e, half, :],
                                                start=half == 0, stop=half == NH - 1)
                last.then_inc(down_done, 1)

            def body(j, chunk):
                for e in range(E0):
                    for half in range(NH):
                        if e or not isinstance(j, int):
                            up(j, e * NH + half, chunk)
                    if e:
                        down(j, e - 1)
                down(j, E0 - 1)

            def start(c):
                pe.wait_ge(ln.T_ready, c + 1)
                for t in range(c * TPC, (c + 1) * TPC):
                    last = nc.tensor.matmul(core.ps[:, 7, t * E0:(t + 1) * E0], tile_of(xnT, t), w["gate0"][:],
                                            start=True, stop=True)
                if c == 0:
                    for u in range(2):
                        up(0, u, xnT[:, 0:CH])
                if c == NC_ - 1:
                    last.then_inc(scored, 1)

            ln.tensor(pe, start)
            body(0, xnT[:, 0:CH])
            with pe.Fori(1, NC_) as j:
                body(j, xnT[:, bass.ds(j * CH, CH)])

        @block.scalar
        def _(act):
            def silu(j, units):
                for u in units:
                    act.wait_ge(up_done, j * (2 * UNITS) + (2 * u + 1))
                    if not (isinstance(j, int) and u < 2):
                        act.wait_ge(hidden_done, j * UNITS + (u - 1))
                    nc.scalar.activation(gate[u % 2][:], core.ps[:, UP + 2 * (u % 2), :], ACT.Silu).then_inc(gate_done, 1)

            ln.scalar(act)
            silu(0, range(2))
            act.wait_ge(exp_in, 1)
            nc.scalar.activation(expd[:], expd[:], ACT.Exp).then_inc(exp_out, 1)

            silu(0, range(2, UNITS))
            with act.Fori(1, NC_) as j:
                silu(j, range(UNITS))

        @block.vector
        def _(dve):
            line = core.dve_line

            def multiply(j, u):
                dve.wait_ge(gate_done, j * UNITS + (u + 1))
                dve.wait_ge(up_done, j * (2 * UNITS) + (2 * u + 2))
                e = u // NH
                if not (isinstance(j, int) and e < 2) and u % NH == 0:
                    dve.wait_ge(down_done, j * E0 + (e - 1))
                nc.vector.tensor_tensor(hidden[e % 2][:, u % NH, :], gate[u % 2][:], core.ps[:, UP + 2 * (u % 2) + 1, :],
                                        ALU.mult).then_inc(hidden_done, 1)

            line.after(dve, nc.vector.memset(keep[:], 1.0))
            line.mark(nc.vector.memset(keep[:, :, 0:1], 0.0))
            ln.vector(dve)
            for u in range(2):
                multiply(0, u)
            dve.wait_ge(scored, 1)
            line.after(dve, nc.vector.tensor_copy(scores[:], core.ps[:, 7, 0:NT * E0].rearrange("p (t e) -> p t e", e=E0)))
            for t in range(NT):
                line.mark(nc.vector.max(top8[:, t, :], scores[:, t, :]))
            line.wait(dve)
            nc.vector.tensor_tensor(expd[:], scores[:], top8[:, :, 0:1].to_broadcast([P, NT, E0]),
                                    ALU.subtract).then_inc(exp_in, 1)
            pick_top(core, dve, scores[:], top8, keep, work, TOP0)
            dve.wait_ge(exp_out, 1)
            line.after(dve, nc.vector.tensor_tensor(expd[:], expd[:], work["sel"][:], ALU.mult))
            line.after(dve, nc.vector.tensor_reduce(total[:], expd[:], AX_X, ALU.add))
            line.after(dve, nc.vector.reciprocal(total[:], total[:]))
            line.after(dve, nc.vector.tensor_tensor(probs[:], expd[:], total[:].unsqueeze(2).to_broadcast([P, NT, E0]),
                                                    ALU.mult))

            def add(j, e):
                dve.wait_ge(down_done, j * E0 + (e + 1))
                for k in range(TPC):
                    if e:
                        dve.wait_ge(added, j * (E0 * TPC) + ((e - 1) * TPC + k + 1))
                    t = j * TPC + k
                    xs = core.x[:, bass.ds(t, 1), :].rearrange("p t d -> p (t d)")
                    nc.vector.scalar_tensor_tensor(out=xs, in0=core.ps[:, DOWN + e % 2, k * P:(k + 1) * P],
                                                   scalar=probs[:, bass.ds(t, 1), e], in1=xs,
                                                   op0=ALU.mult, op1=ALU.add).then_inc(added, 1)

            def body(j):
                for e in range(E0):
                    for half in range(NH):
                        if e or not isinstance(j, int):
                            multiply(j, e * NH + half)
                    if e:
                        add(j, e - 1)
                add(j, E0 - 1)

            body(0)
            with dve.Fori(1, NC_) as j:
                body(j)


def selective_scan(core):
    nc, w = core.nc, core.w
    PAD = DCONV - 1
    with ExitStack() as ctx:
        def sb(name, shape, dt=F32):
            return ctx.enter_context(nc.sbuf_tensor(f"s_{name}", shape, dt))

        delta = [sb(f"delta{d}", [P, T]) for d in range(ND)]
        xn2 = delta[0][:].rearrange("p (t d) -> p t d", d=P)
        xnT = core.xnT
        ln1 = LayerNorm(core, ctx, "ln_s1", core.x, core.xn, None)
        ln2 = LayerNorm(core, ctx, "ln_s2", core.xn, xn2, xnT, w["norm_g"][:], w["norm_b"][:])
        pre = [sb(f"pre{d}", [P, PAD + T]) for d in range(ND)]
        soft = [pre[d][:, 0:T] for d in range(ND)]
        zs = [sb(f"zs{d}", [P, T]) for d in range(ND)]
        xs = [sb(f"xs{d}", [P, T]) for d in range(ND)]
        delta_c = [sb(f"delta_c{d}", [P, CH]) for d in range(ND)]
        dx_c = [sb(f"dx_c{d}", [P, CH]) for d in range(ND)]
        pick = w["pick"][:].bitcast(BF16)
        bc = sb("bc", [96, T], BF16)
        dtr = sb("dtr", [DTR, T])
        a_neg = sb("a_neg", [P, ND, DS])
        RING = 4
        B_RING = 3
        da = [sb(f"da{i}", [P, CH]) for i in range(RING)]
        rest = da[0][0:96, :]
        dbx = [sb(f"dbx{i}", [P, CH]) for i in range(RING)]
        mid = dbx[0][0:96, :].bitcast(BF16)[:, 0:CH]
        b_rows = [sb(f"b_rows{i}", [P, CH]) for i in range(B_RING)]
        h = sb("h", [P, ND, CH])
        hc = [sb(f"hc{i}", [P, CH]) for i in range(2)]
        state = sb("state", [P, DS, ND])
        yT = [sb(f"yT{d}", [P, CH]) for d in range(ND)]

        padded = core.sem("s_padded")
        in_done = core.sem("s_in_done")
        in_used = core.sem("s_in_used")
        conv_done = core.sem("s_conv")
        conv_silu = core.sem("s_conv_silu")
        xp_done = core.sem("s_xp")
        bc_ready = core.sem("s_bc_ready")
        dt_copied = core.sem("s_dt_copied")
        dt_done = core.sem("s_dt_done")
        absolute = core.sem("s_absolute")
        positive = core.sem("s_positive")
        exp_done = core.sem("s_exp_done")
        log_done = core.sem("s_log_done")
        delta_done = core.sem("s_delta")
        chunk_ready = core.sem("s_chunk_ready")
        residual = core.sem("s_residual")
        b_spread = core.sem("s_b_spread")
        c_spread = core.sem("s_c_spread")
        b_copied = core.sem("s_b_copied")
        da_done = core.sem("s_da")
        dbx_done = core.sem("s_dbx")
        scanned = core.sem("s_scanned")
        saved = core.sem("s_saved")
        hc_done = core.sem("s_hc")
        summed = core.sem("s_summed")
        y_done = core.sem("s_y")
        out_done = core.sem("s_out")
        x_added = core.sem("s_x_added")

        B_BANKS, C_BANK, Y_BANK, O_BANK = (0, 1, 7), 2, 4, 6
        UNITS = DS * ND
        block = ctx.enter_context(nc.Block())

        @block.gpsimd
        def _(pool):
            for d in range(ND):
                nc.gpsimd.memset(pre[d][:, 0:PAD], 0.0).then_inc(padded, 1)
            nc.gpsimd.memset(state[:], 0.0).then_inc(padded, 1)
            pool.wait_ge(ln1.normed, NT)
            for t in range(NT):
                nc.gpsimd.tensor_tensor(core.x[:, t, :], core.x[:, t, :], core.xn[:, t, :], ALU.add).then_inc(residual, 1)

            def body(j):
                pool.wait_ge(chunk_ready, j * 2 * ND + 2 * ND)
                for s in range(DS):
                    for d in range(ND):
                        u = s * ND + d
                        if not (isinstance(j, int) and u < RING):
                            pool.wait_ge(scanned, j * UNITS + (u - RING + 1))
                        pool.wait_ge(b_copied, j * DS + (s + 1))
                        nc.gpsimd.tensor_tensor(dbx[u % RING][:], dx_c[d][:], b_rows[s % B_RING][:],
                                                ALU.mult).then_inc(dbx_done, 1)

            body(0)
            with pool.Fori(1, NC_) as j:
                body(j)

        @block.tensor
        def _(pe):
            ln2.tensor(pe)
            core.loaded(pe, "in_proj", "x_bc", "x_dt", "dt_proj", "out_proj")

            def project_in(c):
                pe.wait_ge(ln2.T_ready, c + 1)
                for m in range(2 * ND):
                    if c:
                        pe.wait_ge(in_used, (c - 1) * 2 * ND + m + 1)
                    nc.tensor.matmul(core.ps[:, 4 + m, :], w["in_proj"][:, m * P:(m + 1) * P],
                                     xnT[:, c * CH:(c + 1) * CH], start=True, stop=True).then_inc(in_done, 1)

            def project_x(c):
                if c == 0:
                    pe.wait_ge(ln2.T_ready, NC_)
                pe.wait_ge(conv_silu, (c + 1) * ND)
                if c >= 2:
                    pe.wait_ge(bc_ready, c - 1)
                for d in range(ND):
                    nc.tensor.matmul(core.ps[0:96, c % 2, :], w["x_bc"][:, d, :], xs[d][:, c * CH:(c + 1) * CH],
                                     start=d == 0, stop=d == ND - 1)
                if c >= 2:
                    pe.wait_ge(dt_copied, c - 1)
                for d in range(ND):
                    last = nc.tensor.matmul(core.ps[0:DTR, 2 + c % 2, :], w["x_dt"][:, d, :],
                                            xs[d][:, c * CH:(c + 1) * CH], start=d == 0, stop=d == ND - 1)
                last.then_inc(xp_done, 1)

            project_in(0)
            for c in range(1, NC_):
                project_in(c)
                project_x(c - 1)
            project_x(NC_ - 1)
            pe.wait_ge(in_used, NC_ * 2 * ND)
            for c in range(NC_):
                pe.wait_ge(dt_copied, c + 1)
                for d in range(ND):
                    m = c * ND + d
                    if m >= 4:
                        pe.wait_ge(positive, m - 3)
                    nc.tensor.matmul(core.ps[:, 4 + m % 4, :], w["dt_proj"][:, d * P:(d + 1) * P],
                                     dtr[:, c * CH:(c + 1) * CH], start=True, stop=True).then_inc(dt_done, 1)
            pe.wait_ge(bc_ready, NC_)
            core.loaded(pe, "pick")
            pe.wait_ge(positive, ND * NC_)

            def spread_b(j, s, chunk):
                if not (isinstance(j, int) and s < B_RING):
                    pe.wait_ge(b_copied, j * DS + max(s - B_RING + 1, 0))
                nc.tensor.matmul(core.ps[:, B_BANKS[s % B_RING], :], pick[:, s, :], chunk,
                                 start=True, stop=True).then_inc(b_spread, 1)

            def spread_c(j, s, chunk):
                if not (isinstance(j, int) and s < 2):
                    pe.wait_ge(hc_done, j * UNITS + (s - 1) * ND)
                nc.tensor.matmul(core.ps[:, C_BANK + s % 2, :], pick[:, DS + s, :], chunk,
                                 start=True, stop=True).then_inc(c_spread, 1)

            def add_up(j, s):
                for d in range(ND):
                    pe.wait_ge(hc_done, j * UNITS + (s * ND + d + 1))
                    nc.tensor.matmul(core.ps[:, Y_BANK + d, :], core.ident[:], hc[d][:],
                                     start=s == 0, stop=s == DS - 1).then_inc(summed, 1)

            def project_out(after):
                pe.wait_ge(y_done, after * (2 * ND))
                for k in range(TPC):
                    for d in range(ND):
                        last = nc.tensor.matmul(core.ps[:, O_BANK, k * P:(k + 1) * P], yT[d][:, k * P:(k + 1) * P],
                                                w["out_proj"][:, d, :], start=d == 0, stop=d == ND - 1)
                last.then_inc(out_done, 1)

            def body(j, chunk):
                for s in range(B_RING):
                    spread_b(j, s, chunk)
                spread_c(j, 0, chunk)
                for s in range(DS):
                    if s + B_RING < DS:
                        spread_b(j, s + B_RING, chunk)
                    if s == 0 and not isinstance(j, int):
                        project_out(j)
                    if s:
                        spread_c(j, s, chunk)
                        add_up(j, s - 1)
                add_up(j, DS - 1)

            body(0, bc[:, 0:CH])
            with pe.Fori(1, NC_) as j:
                body(j, bc[:, bass.ds(j * CH, CH)])
            project_out(NC_)

        @block.scalar
        def _(act):
            line = core.act_line
            core.loaded(act, "norm_g", "norm_b")
            ln1.scalar(act)
            ln2.scalar(act)
            core.loaded(act, "log_A", "conv_b", "dt_b")

            def silu_x(c):
                for d in range(ND):
                    act.wait_ge(conv_done, (DCONV * c + DCONV - 1) * ND + d + 1)
                    cols = slice(c * CH, (c + 1) * CH)
                    nc.scalar.activation(xs[d][:, cols], delta[d][:, cols], ACT.Silu).then_inc(conv_silu, 1)

            def copy_dt(c):
                act.wait_ge(xp_done, c + 1)
                nc.scalar.copy(dtr[:, c * CH:(c + 1) * CH], core.ps[0:DTR, 2 + c % 2, :]).then_inc(dt_copied, 1)

            act.wait_ge(padded, ND)
            for c in range(NC_):
                for m in range(2 * ND):
                    act.wait_ge(in_done, c * 2 * ND + m + 1)
                    src = core.ps[:, 4 + m, :]
                    if m < ND:
                        ins = nc.scalar.copy(pre[m][:, PAD + c * CH:PAD + (c + 1) * CH], src)
                    else:
                        ins = nc.scalar.activation(zs[m - ND][:, c * CH:(c + 1) * CH], src, ACT.Silu)
                    ins.then_inc(in_used, 1)
                if c:
                    silu_x(c - 1)
                if c > 1:
                    copy_dt(c - 2)
            silu_x(NC_ - 1)
            copy_dt(NC_ - 2)
            copy_dt(NC_ - 1)
            for m in range(ND * NC_):
                act.wait_ge(dt_done, m + 1)
                c, d = m // ND, m % ND
                if m == 0:
                    act.wait_ge(conv_done, DCONV * ND * NC_)
                nc.scalar.activation(soft[d][:, c * CH:(c + 1) * CH], core.ps[:, 4 + m % 4, :], ACT.Abs,
                                     bias=w["dt_b"][:, d:d + 1]).then_inc(absolute, 1)
            act.wait_ge(absolute, ND * NC_)
            for d in range(ND):
                nc.scalar.activation(soft[d], soft[d], ACT.Exp, scale=-1.0).then_inc(exp_done, 1)
            for d in range(ND):
                act.wait_ge(exp_done, d + 1)
                nc.scalar.activation(soft[d], soft[d], ACT.Ln, bias=1.0).then_inc(log_done, 1)
            line.after(act, nc.scalar.activation(a_neg[:], w["log_A"][:], ACT.Exp))
            line.after(act, nc.scalar.mul(a_neg[:], a_neg[:], -1.0))

            def copy_b(j, s):
                act.wait_ge(b_spread, j * DS + (s + 1))
                if not (isinstance(j, int) and s < B_RING):
                    act.wait_ge(dbx_done, j * UNITS + max(s - B_RING + 1, 0) * ND)
                nc.scalar.copy(b_rows[s % B_RING][:], core.ps[:, B_BANKS[s % B_RING], :]).then_inc(b_copied, 1)

            def body(j):
                copy_b(j, 0)
                copy_b(j, 1)
                act.wait_ge(chunk_ready, j * 2 * ND + 2 * ND)
                for s in range(DS):
                    for d in range(ND):
                        u = s * ND + d
                        if not (isinstance(j, int) and u < RING):
                            act.wait_ge(scanned, j * UNITS + (u - RING + 1))
                        nc.scalar.activation(da[u % RING][:], delta_c[d][:], ACT.Exp,
                                             scale=a_neg[:, d, s:s + 1]).then_inc(da_done, 1)
                    if s + 2 < DS:
                        copy_b(j, s + 2)

            body(0)
            with act.Fori(1, NC_) as j:
                body(j)

        @block.vector
        def _(dve):
            line = core.dve_line
            ln1.vector(dve)
            dve.wait_ge(ln1.normed, NT)
            ln2.vector(dve)
            core.loaded(dve, "conv_w", "conv_b", "Dp", "dt_b")

            def convolve(c):
                dve.wait_ge(in_used, (c + 1) * 2 * ND)
                cols = slice(c * CH, (c + 1) * CH)
                for d in range(ND):
                    nc.vector.tensor_scalar(delta[d][:, cols], pre[d][:, cols], w["conv_w"][:, d, 0:1],
                                            w["conv_b"][:, d:d + 1], ALU.mult, ALU.add).then_inc(conv_done, 1)
                for k in range(1, DCONV):
                    for d in range(ND):
                        dve.wait_ge(conv_done, (DCONV * c + k - 1) * ND + d + 1)
                        nc.vector.scalar_tensor_tensor(out=delta[d][:, cols], in0=pre[d][:, c * CH + k:c * CH + k + CH],
                                                       scalar=w["conv_w"][:, d, k:k + 1], in1=delta[d][:, cols],
                                                       op0=ALU.mult, op1=ALU.add).then_inc(conv_done, 1)

            def cut_bc(c):
                dve.wait_ge(xp_done, c + 1)
                cols = slice(c * CH, (c + 1) * CH)
                src = core.ps[0:96, c % 2, :]
                line.after(dve, nc.vector.tensor_copy(bc[:, cols], src))
                line.after(dve, nc.vector.tensor_tensor(rest, src, bc[:, cols], ALU.subtract))
                line.after(dve, nc.vector.tensor_copy(mid, rest))
                line.after(dve, nc.vector.tensor_tensor(rest, rest, mid, ALU.subtract))
                line.after(dve, nc.vector.tensor_copy(bc[32:64, cols], mid[32:64, :]))
                nc.vector.tensor_copy(bc[64:96, cols], rest[64:96, :]).then_inc(bc_ready, 1)

            for c in range(NC_):
                convolve(c)
                if c >= 2:
                    cut_bc(c - 2)
            cut_bc(NC_ - 2)
            cut_bc(NC_ - 1)
            for m in range(ND * NC_):
                c, d = m // ND, m % ND
                dve.wait_ge(absolute, m + 1)
                if m == 0:
                    dve.wait_ge(conv_silu, ND * NC_)
                nc.vector.tensor_scalar(delta[d][:, c * CH:(c + 1) * CH], core.ps[:, 4 + m % 4, :],
                                        w["dt_b"][:, d:d + 1], 0.0, ALU.add, ALU.max).then_inc(positive, 1)
            dve.wait_ge(positive, ND * NC_)
            for d in range(ND):
                dve.wait_ge(log_done, d + 1)
                nc.vector.tensor_tensor(delta[d][:], delta[d][:], soft[d], ALU.add).then_inc(delta_done, 1)
            dve.wait_ge(delta_done, ND)
            dve.wait_ge(padded, ND + 1)
            dve.wait_ge(residual, NT)

            def finish(after, cols):
                dve.wait_ge(summed, after * UNITS)
                for d in range(ND):
                    nc.vector.scalar_tensor_tensor(out=yT[d][:], in0=xs[d][:, cols],
                                                   scalar=w["Dp"][:, d:d + 1], in1=core.ps[:, Y_BANK + d, :],
                                                   op0=ALU.mult, op1=ALU.add).then_inc(y_done, 1)
                for d in range(ND):
                    dve.wait_ge(y_done, after * (2 * ND) + (d + 1 - 2 * ND))
                    nc.vector.tensor_tensor(yT[d][:], yT[d][:], zs[d][:, cols], ALU.mult).then_inc(y_done, 1)

            def add_out(after, tiles):
                dve.wait_ge(out_done, after * 1)
                xc = core.x[:, tiles, :].rearrange("p t d -> p (t d)")
                nc.vector.tensor_tensor(xc, xc, core.ps[:, O_BANK, :], ALU.add).then_inc(x_added, 1)
                dve.wait_ge(x_added, after * 1)

            def body(j):
                cols = bass.ds(j * CH, CH)
                for d in range(ND):
                    nc.vector.tensor_copy(delta_c[d][:], delta[d][:, cols]).then_inc(chunk_ready, 1)
                    nc.vector.tensor_tensor(dx_c[d][:], delta[d][:, cols], xs[d][:, cols], ALU.mult).then_inc(chunk_ready, 1)
                if not isinstance(j, int):
                    finish(j, bass.ds(j * CH + (-CH), CH))
                for s in range(DS):
                    for d in range(ND):
                        u = s * ND + d
                        dve.wait_ge(da_done, j * UNITS + (u + 1))
                        dve.wait_ge(dbx_done, j * UNITS + (u + 1))
                        if not (isinstance(j, int) and u < 2):
                            dve.wait_ge(hc_done, j * UNITS + (u - 1))
                            dve.wait_ge(saved, j * DS + s)
                        nc.vector.tensor_tensor_scan(out=h[:, d, :], data0=da[u % RING][:], data1=dbx[u % RING][:],
                                                     initial=state[:, s, d:d + 1], op0=ALU.mult,
                                                     op1=ALU.add).then_inc(scanned, 1)
                    dve.wait_ge(c_spread, j * DS + (s + 1))
                    for d in range(ND):
                        u = s * ND + d
                        dve.wait_ge(scanned, j * UNITS + (u + 1))
                        if not (isinstance(j, int) and u < 2):
                            dve.wait_ge(summed, j * UNITS + (u - 1))
                        nc.vector.tensor_tensor(hc[d][:], h[:, d, :], core.ps[:, C_BANK + s % 2, :],
                                                ALU.mult).then_inc(hc_done, 1)
                        if d == 0:
                            dve.wait_ge(scanned, j * UNITS + (s + 1) * ND)
                            nc.vector.tensor_copy(state[:, s, :], h[:, :, CH - 1]).then_inc(saved, 1)
                    if s == 2 and not isinstance(j, int):
                        add_out(j, bass.ds(j * TPC + (-TPC), TPC))

            body(0)
            with dve.Fori(1, NC_) as j:
                body(j)
            finish(NC_, slice(T - CH, T))
            add_out(NC_, slice(NT - TPC, NT))


def linear_attention(core):
    nc, w = core.nc, core.w
    SCALE = float(HD) ** -0.5 / P
    with ExitStack() as ctx:
        def sb(name, shape, dt=F32):
            return ctx.enter_context(nc.sbuf_tensor(f"l_{name}", shape, dt))

        ln = LayerNorm(core, ctx, "ln_l", core.x, core.xn, core.xnT)
        xnT = core.xnT
        keT = sb("keT", [P, T])
        k_tok = sb("k_tok", [P, NT, P])
        v_tok = sb("v_tok", [P, NT, P])
        q_tok = sb("q_tok", [P, NT, P])
        qT = sb("qT", [P, T])
        k_max = sb("k_max", [P, 1])
        k_sum = sb("k_sum", [P, 1])
        q_max = sb("q_max", [P, NT])
        q_sum = sb("q_sum", [P, NT])
        ctxT = sb("ctxT", [P, P])
        mixed = sb("mixed", [P, P])

        k_done = core.sem("l_k")
        kmax_done = core.sem("l_kmax")
        k_exp = core.sem("l_kexp")
        qv_done = core.sem("l_qv")
        v_copied = core.sem("l_v_copied")
        q_shifted = core.sem("l_q_shifted")
        q_exp = core.sem("l_q_exp")
        turned = core.sem("l_turned")
        k_copied = core.sem("l_k_copied")
        q_copied = core.sem("l_q_copied")
        ctx_done = core.sem("l_ctx")
        ctx_copied = core.sem("l_ctx_copied")
        mix_done = core.sem("l_mix")
        mixed_ready = core.sem("l_mixed")
        out_done = core.sem("l_out")
        added = core.sem("l_added")
        bias_added = core.sem("l_bias")
        block = ctx.enter_context(nc.Block())

        @block.gpsimd
        def _(pool):
            core.loaded(pool, "bo")
            pool.wait_ge(ln.normed, NT)
            for t in range(NT):
                nc.gpsimd.tensor_tensor(core.x[:, t, :], core.x[:, t, :], w["bo"][:], ALU.add).then_inc(bias_added, 1)

        @block.tensor
        def _(pe):
            ln.tensor(pe)
            core.loaded(pe, "Wk1", "Wq1", "Wv1", "Wo1")
            for c in range(NC_):
                pe.wait_ge(ln.T_ready, c + 1)
                last = nc.tensor.matmul(core.ps[:, 2 + c, :], w["Wk1"][:], xnT[:, c * CH:(c + 1) * CH],
                                        start=True, stop=True)
            last.then_inc(k_done, 1)
            for g in range(NC_):
                for i, name in enumerate(("Wq1", "Wv1")):
                    if g:
                        pe.wait_ge(q_shifted if i == 0 else v_copied, g)
                    for k in range(TPC):
                        last = nc.tensor.matmul(core.ps[:, 6 + i, k * P:(k + 1) * P], tile_of(xnT, g * TPC + k),
                                                w[name][:], start=True, stop=True)
                    last.then_inc(qv_done, 1)
            for g in range(NC_):
                pe.wait_ge(k_exp, 1)
                if g >= 2:
                    pe.wait_ge(k_copied, g - 1)
                for k in range(TPC):
                    last = nc.tensor.transpose(core.ps[:, g % 2, k * P:(k + 1) * P], tile_of(keT, g * TPC + k),
                                               core.ident[:])
                last.then_inc(turned, 1)
            for g in range(NC_):
                pe.wait_ge(q_exp, g + 1)
                pe.wait_ge(k_copied, min(NC_, g + 3))
                if g >= 2:
                    pe.wait_ge(q_copied, g - 1)
                for k in range(TPC):
                    last = nc.tensor.transpose(core.ps[:, g % 2, k * P:(k + 1) * P], q_tok[:, g * TPC + k, :],
                                               core.ident[:])
                last.then_inc(turned, 1)
            pe.wait_ge(q_shifted, NC_)
            pe.wait_ge(v_copied, NC_)
            pe.wait_ge(k_copied, NC_)
            for t in range(NT):
                last = nc.tensor.matmul(core.ps[:, 2, 0:P], v_tok[:, t, :], k_tok[:, t, :], start=t == 0, stop=t == NT - 1)
            last.then_inc(ctx_done, 1)
            pe.wait_ge(ctx_copied, 1)
            nc.tensor.matmul(core.ps[:, 3, 0:P], ctxT[:], w["Wo1"][:], start=True, stop=True).then_inc(mix_done, 1)
            pe.wait_ge(mixed_ready, 1)
            pe.wait_ge(q_copied, NC_)
            for g in range(NC_):
                for k in range(TPC):
                    last = nc.tensor.matmul(core.ps[:, 4 + g, k * P:(k + 1) * P], tile_of(qT, g * TPC + k), mixed[:],
                                            start=True, stop=True)
                last.then_inc(out_done, 1)

        @block.scalar
        def _(act):
            ln.scalar(act)
            act.wait_ge(kmax_done, 1)
            nc.scalar.activation(keT[:], core.ps[:, 2:6, :].rearrange("p b n -> p (b n)"), ACT.Exp, bias=k_max[:],
                                 accum_out=k_sum[:]).then_inc(k_exp, 1)
            for g in range(NC_):
                act.wait_ge(q_shifted, g + 1)
                qs = q_tok[:, g * TPC:(g + 1) * TPC, :]
                nc.scalar.activation(qs, qs, ACT.Exp).then_inc(q_exp, 1)
                act.wait_ge(qv_done, 2 * g + 2)
                nc.scalar.copy(v_tok[:, g * TPC:(g + 1) * TPC, :],
                               core.ps[:, 7, :].rearrange("p (k d) -> p k d", d=P)).then_inc(v_copied, 1)
            for g in range(NC_):
                act.wait_ge(turned, g + 1)
                nc.scalar.copy(k_tok[:, g * TPC:(g + 1) * TPC, :],
                               core.ps[:, g % 2, :].rearrange("p (k d) -> p k d", d=P)).then_inc(k_copied, 1)
            for g in range(NC_):
                act.wait_ge(turned, NC_ + g + 1)
                nc.scalar.copy(qT[:, g * CH:(g + 1) * CH], core.ps[:, g % 2, :]).then_inc(q_copied, 1)

        @block.vector
        def _(dve):
            line = core.dve_line
            ln.vector(dve)
            dve.wait_ge(k_done, 1)
            nc.vector.tensor_reduce(k_max[:], core.ps[:, 2:6, :], mybir.AxisListType.XY, ALU.max,
                                    negate=True).then_inc(kmax_done, 1)
            for g in range(NC_):
                dve.wait_ge(qv_done, 2 * g + 1)
                src = core.ps[:, 6, :].rearrange("p (k d) -> p k d", d=P)
                cols = slice(g * TPC, (g + 1) * TPC)
                line.after(dve, nc.vector.tensor_reduce(q_max[:, cols], src, AX_X, ALU.max))
                nc.vector.tensor_tensor(q_tok[:, cols, :], src, q_max[:, cols].unsqueeze(2).to_broadcast([P, TPC, P]),
                                        ALU.subtract).then_inc(q_shifted, 1)
            for g in range(NC_):
                dve.wait_ge(q_exp, g + 1)
                cols = slice(g * TPC, (g + 1) * TPC)
                line.mark(nc.vector.tensor_reduce(q_sum[:, cols], q_tok[:, cols, :], AX_X, ALU.add))
            line.wait(dve)
            line.after(dve, nc.vector.reciprocal(q_sum[:], q_sum[:]))
            dve.wait_ge(k_exp, 1)
            line.after(dve, nc.vector.reciprocal(k_max[:], k_sum[:]))
            dve.wait_ge(ctx_done, 1)
            nc.vector.tensor_copy(ctxT[:], core.ps[:, 2, 0:P]).then_inc(ctx_copied, 1)
            dve.wait_ge(mix_done, 1)
            nc.vector.tensor_scalar(mixed[:], core.ps[:, 3, 0:P], k_max[:], SCALE, ALU.mult,
                                    ALU.mult).then_inc(mixed_ready, 1)
            dve.wait_ge(bias_added, NT)
            for t in range(NT):
                if t % TPC == 0:
                    dve.wait_ge(out_done, t // TPC + 1)
                nc.vector.scalar_tensor_tensor(out=core.x[:, t, :],
                                               in0=core.ps[:, 4 + t // TPC, (t % TPC) * P:(t % TPC + 1) * P],
                                               scalar=q_sum[:, t:t + 1], in1=core.x[:, t, :],
                                               op0=ALU.mult, op1=ALU.add).then_inc(added, 1)
            dve.wait_ge(added, NT)


def experts_top4(core, tag):
    nc, w = core.nc, core.w
    PAIRS = E1 // 2
    UNITS = PAIRS + 1
    PG = E1 // GROUPS
    UP, DOWN, S_BANK = 0, 4, 7
    with ExitStack() as ctx:
        def sb(name, shape, dt=F32):
            return ctx.enter_context(nc.sbuf_tensor(f"{tag}_{name}", shape, dt))

        ln = LayerNorm(core, ctx, f"ln_{tag}", core.x, core.xn, core.xnT, banks=(4, 5))
        xnT = core.xnT
        scores = sb("scores", [P, NT, E1])
        choice = sb("choice", [P, NT, E1])
        tmp_scores = sb("tmp_scores", [P, NT, E1])
        top8 = sb("top8", [P, NT, 8])
        keep = sb("keep", [P, NT, E1])
        work = {n: sb(n, [P, NT, E1]) for n in ("gt", "eq", "nth", "sel")}
        work.update({n: sb(n, [P, NT]) for n in ("above", "room")})
        hi = sb("hi", [P, NT * GROUPS, 2])
        lo = sb("lo", [P, NT * GROUPS, 2])
        g_best = sb("g_best", [P, NT * GROUPS])
        g_next = sb("g_next", [P, NT * GROUPS])
        g_low = sb("g_low", [P, NT * GROUPS])
        g_beats = sb("g_beats", [P, NT * GROUPS, GROUPS])
        g_ties = sb("g_ties", [P, NT * GROUPS, GROUPS])
        g_rank = sb("g_rank", [P, NT * GROUPS])
        probs = sb("probs", [P, NT, E1 + 1])
        total = sb("total", [P, NT])
        gate = [sb(f"gate{i}", [P, CH]) for i in range(2)]
        hidden = [sb(f"hidden{i}", [P, CH]) for i in range(2)]

        scored = core.sem(f"{tag}_scored")
        tanh_done = core.sem(f"{tag}_tanh")
        up_done = core.sem(f"{tag}_up")
        gate_done = core.sem(f"{tag}_gate")
        hidden_done = core.sem(f"{tag}_hidden")
        down_done = core.sem(f"{tag}_down")
        added = core.sem(f"{tag}_added")
        block = ctx.enter_context(nc.Block())

        def experts(u):
            return 2 if u < PAIRS else 1
        ADDS = (2 * PAIRS + 1) * TPC

        @block.tensor
        def _(pe):
            core.loaded(pe, "gate1", "w_up1", "w_down1", "sh_up", "sh_down")

            def up(j, u, chunk):
                if not (isinstance(j, int) and u < 2):
                    pe.wait_ge(hidden_done, j * UNITS + (u - 1))
                for k in range(2):
                    weight = w["w_up1"][:, u, k, :] if u < PAIRS else w["sh_up"][:, k, :]
                    nc.tensor.matmul(core.ps[:, UP + 2 * (u % 2) + k, :], weight, chunk,
                                     start=True, stop=True).then_inc(up_done, 1)

            def down(j, u):
                pe.wait_ge(hidden_done, j * UNITS + (u + 1))
                if isinstance(j, int) and u == 1:
                    pe.wait_ge(tanh_done, 1)
                elif not isinstance(j, int) or u > 1:
                    pe.wait_ge(added, j * ADDS + max(u - 1, 0) * 2 * TPC)
                for k in range(TPC):
                    for i in range(experts(u)):
                        part = slice(I1 * i, I1 * (i + 1))
                        weight = w["w_down1"][part, u, :] if u < PAIRS else w["sh_down"][:]
                        last = nc.tensor.matmul(core.ps[:, DOWN + 2 * (u % 2) + i, k * P:(k + 1) * P],
                                                hidden[u % 2][part, k * P:(k + 1) * P], weight, start=True, stop=True)
                last.then_inc(down_done, 1)

            def body(j, chunk):
                for u in range(UNITS):
                    if u >= 2 or not isinstance(j, int):
                        up(j, u, chunk)
                    if u:
                        down(j, u - 1)
                down(j, UNITS - 1)

            def start(c):
                pe.wait_ge(ln.T_ready, c + 1)
                for t in range(c * TPC, (c + 1) * TPC):
                    last = nc.tensor.matmul(core.ps[:, S_BANK, t * E1:(t + 1) * E1], tile_of(xnT, t), w["gate1"][:],
                                            start=True, stop=True)
                if c == 0:
                    for u in range(2):
                        up(0, u, xnT[:, 0:CH])
                if c == NC_ - 1:
                    last.then_inc(scored, 1)

            ln.tensor(pe, start)
            body(0, xnT[:, 0:CH])
            with pe.Fori(1, NC_) as j:
                body(j, xnT[:, bass.ds(j * CH, CH)])

        @block.scalar
        def _(act):
            def silu(j, units):
                for u in units:
                    act.wait_ge(up_done, j * (2 * UNITS) + (2 * u + 1))
                    if not (isinstance(j, int) and u < 2):
                        act.wait_ge(hidden_done, j * UNITS + (u - 1))
                    nc.scalar.activation(gate[u % 2][:], core.ps[:, UP + 2 * (u % 2), :],
                                         ACT.Silu).then_inc(gate_done, 1)

            ln.scalar(act)
            act.wait_ge(scored, 1)
            nc.scalar.activation(scores[:], core.ps[:, S_BANK, 0:NT * E1].rearrange("p (t e) -> p t e", e=E1),
                                 ACT.Tanh, scale=0.5).then_inc(tanh_done, 1)

            silu(0, range(UNITS))
            with act.Fori(1, NC_) as j:
                silu(j, range(UNITS))

        @block.vector
        def _(dve):
            line = core.dve_line

            def multiply(j, u):
                dve.wait_ge(gate_done, j * UNITS + (u + 1))
                dve.wait_ge(up_done, j * (2 * UNITS) + (2 * u + 2))
                if not (isinstance(j, int) and u < 2):
                    dve.wait_ge(down_done, j * UNITS + (u - 1))
                nc.vector.tensor_tensor(hidden[u % 2][:], gate[u % 2][:],
                                        core.ps[:, UP + 2 * (u % 2) + 1, :], ALU.mult).then_inc(hidden_done, 1)

            line.after(dve, nc.vector.memset(keep[:], 1.0))
            line.mark(nc.vector.memset(keep[:, :, 0:1], 0.0))
            line.mark(nc.vector.memset(probs[:, :, E1:E1 + 1], 1.0))
            ln.vector(dve)
            core.loaded(dve, "e_bias", "earlier")
            dve.wait_ge(tanh_done, 1)
            line.after(dve, nc.vector.tensor_scalar(scores[:], scores[:], 0.5, 0.5, ALU.mult, ALU.add))
            line.after(dve, nc.vector.tensor_tensor(choice[:], scores[:],
                                                    w["e_bias"][:].unsqueeze(1).to_broadcast([P, NT, E1]), ALU.add))
            quads = choice[:].rearrange("p t (g i k) -> p (t g) i k", g=GROUPS, k=2)
            line.mark(nc.vector.tensor_tensor(hi[:], quads[:, :, :, 0], quads[:, :, :, 1], ALU.max))
            line.after(dve, nc.vector.tensor_tensor(lo[:], quads[:, :, :, 0], quads[:, :, :, 1], ALU.min))
            line.mark(nc.vector.tensor_tensor(g_best[:], hi[:, :, 0], hi[:, :, 1], ALU.max))
            line.mark(nc.vector.tensor_tensor(g_next[:], hi[:, :, 0], hi[:, :, 1], ALU.min))
            line.after(dve, nc.vector.tensor_tensor(g_low[:], lo[:, :, 0], lo[:, :, 1], ALU.max))
            line.after(dve, nc.vector.tensor_tensor(g_next[:], g_next[:], g_low[:], ALU.max))
            line.after(dve, nc.vector.tensor_tensor(g_best[:], g_best[:], g_next[:], ALU.add))
            mine = g_best[:].unsqueeze(2).to_broadcast([P, NT * GROUPS, GROUPS])
            for g in range(GROUPS):
                of_group = g_best[:].rearrange("p (t g) -> p t g", g=GROUPS)
                mine = of_group[:, :, g:g + 1].to_broadcast([P, NT, GROUPS])
                beats = g_beats[:].rearrange("p (t g) h -> p t g h", g=GROUPS)[:, :, g, :]
                ties = g_ties[:].rearrange("p (t g) h -> p t g h", g=GROUPS)[:, :, g, :]
                line.mark(nc.vector.tensor_tensor(beats, of_group, mine, ALU.is_gt))
                line.mark(nc.vector.tensor_tensor(ties, of_group, mine, ALU.is_equal))
            line.wait(dve)
            earlier = w["earlier"][:].unsqueeze(1).to_broadcast([P, NT, GROUPS * GROUPS])
            ties = g_ties[:].rearrange("p (t g) h -> p t (g h)", g=GROUPS)
            line.after(dve, nc.vector.tensor_tensor(ties, ties, earlier, ALU.mult))
            line.after(dve, nc.vector.tensor_tensor(g_beats[:], g_beats[:], g_ties[:], ALU.add))
            line.after(dve, nc.vector.tensor_reduce(g_rank[:], g_beats[:], AX_X, ALU.add))
            line.after(dve, nc.vector.tensor_scalar(g_rank[:], g_rank[:], float(TOPG), None, ALU.is_lt))
            line.after(dve, nc.vector.tensor_tensor(
                tmp_scores[:].rearrange("p t (g k) -> p (t g) k", g=GROUPS),
                choice[:].rearrange("p t (g k) -> p (t g) k", g=GROUPS),
                g_rank[:].unsqueeze(2).to_broadcast([P, NT * GROUPS, PG]), ALU.mult))
            for u in range(2):
                multiply(0, u)
            for t in range(NT):
                line.mark(nc.vector.max(top8[:, t, :], tmp_scores[:, t, :]))
            line.wait(dve)
            pick_top(core, dve, tmp_scores[:], top8, keep, work, TOP1)
            line.after(dve, nc.vector.tensor_tensor(work["gt"][:], scores[:], work["sel"][:], ALU.mult))
            line.after(dve, nc.vector.tensor_reduce(total[:], work["gt"][:], AX_X, ALU.add))
            line.after(dve, nc.vector.tensor_scalar(total[:], total[:], 1e-20, None, ALU.add))
            line.after(dve, nc.vector.reciprocal(total[:], total[:]))
            line.after(dve, nc.vector.tensor_scalar(total[:], total[:], SCALING, None, ALU.mult))
            line.after(dve, nc.vector.tensor_tensor(probs[:, :, 0:E1], work["gt"][:],
                                                    total[:].unsqueeze(2).to_broadcast([P, NT, E1]), ALU.mult))

            def add(j, u):
                for i in range(experts(u)):
                    e = 2 * u + i
                    if i == 0:
                        dve.wait_ge(down_done, j * UNITS + (u + 1))
                    for k in range(TPC):
                        if e:
                            dve.wait_ge(added, j * ADDS + ((e - 1) * TPC + k + 1))
                        t = j * TPC + k
                        xs = core.x[:, bass.ds(t, 1), :].rearrange("p t d -> p (t d)")
                        nc.vector.scalar_tensor_tensor(out=xs, in0=core.ps[:, DOWN + 2 * (u % 2) + i, k * P:(k + 1) * P],
                                                       scalar=probs[:, bass.ds(t, 1), e], in1=xs,
                                                       op0=ALU.mult, op1=ALU.add).then_inc(added, 1)

            def body(j):
                for u in range(UNITS):
                    if u >= 2 or not isinstance(j, int):
                        multiply(j, u)
                    if u:
                        add(j, u - 1)
                add(j, UNITS - 1)

            body(0)
            with dve.Fori(1, NC_) as j:
                body(j)
            dve.wait_ge(added, NC_ * ADDS)


def gated_linear_attention(core):
    nc, w = core.nc, core.w
    with ExitStack() as ctx:
        def sb(name, shape, dt=F32):
            return ctx.enter_context(nc.sbuf_tensor(f"g_{name}", shape, dt))

        ln = LayerNorm(core, ctx, "ln_g", core.x, core.xn, core.xnT)
        xnT = core.xnT
        qT = sb("qT", [P, T])
        fT = sb("fT", [P, T])
        kT = sb("kT", [P, T])
        suf = sb("suf", [P, T])
        pre = fT
        qd = [sb(f"qd{i}", [P, T]) for i in range(2)]
        kd = [sb(f"kd{i}", [P, T]) for i in range(2)]
        g1T = suf
        v = sb("v", [P, NT, P])
        gate = sb("gate", [P, NT, P])
        att = sb("att", [P, NT, P])
        k_tok = sb("k_tok", [P, NT, P])
        states = sb("states", [P, NT, P])
        o_gated, o_normed, o_T = core.xn, k_tok, kd[0]
        ln_o = LayerNorm(core, ctx, "ln_go", o_gated, o_normed, o_T[:], w["ln_w"][:], None)

        proj = core.sem("g_proj")
        proj_used = core.sem("g_proj_used")
        f_ready = core.sem("g_f")
        decayed = core.sem("g_decayed")
        level_done = core.sem("g_level_done")
        level_taken = core.sem("g_level_taken")
        turned = core.sem("g_turned")
        k_copied = core.sem("g_k_copied")
        u_done = core.sem("g_u")
        state_done = core.sem("g_state")
        o_done = core.sem("g_o")
        o_taken = core.sem("g_o_taken")
        out_done = core.sem("g_out")
        added = core.sem("g_added")
        block = ctx.enter_context(nc.Block())
        NSTEP = LEVELS + 1

        @block.tensor
        def _(pe):
            ln.tensor(pe)
            core.loaded(pe, "W_in", "W_g1", "W_g2", "W_out")
            n = 0
            for name in ("lg", "g1", "v", "gate", "q"):
                for c in range(NC_):
                    if n >= 4:
                        pe.wait_ge(proj_used, n - 3)
                    if n < NC_:
                        pe.wait_ge(ln.T_ready, c + 1)
                    if name == "gate":
                        pe.wait_ge(proj_used, 2 * NC_)
                    bank = core.ps[:, 4 + n % 4, :]
                    if name in ("lg", "g1", "q"):
                        weight = {"lg": w["W_in"][:, 2 * P:3 * P], "q": w["W_in"][:, P:2 * P], "g1": w["W_g1"][:]}[name]
                        last = nc.tensor.matmul(bank, weight, xnT[:, c * CH:(c + 1) * CH], start=True, stop=True)
                    else:
                        src, weight = (xnT, w["W_in"][:, 0:P]) if name == "v" else (g1T, w["W_g2"][:])
                        for k in range(TPC):
                            last = nc.tensor.matmul(bank[:, k * P:(k + 1) * P], tile_of(src, c * TPC + k), weight,
                                                    start=True, stop=True)
                    last.then_inc(proj, 1)
                    n += 1
            pe.wait_ge(proj_used, n)
            pe.wait_ge(f_ready, 1)
            for step in range(NSTEP):
                pe.wait_ge(decayed, step)
                kk, qq = (kT, qT) if step == 0 else (kd[step % 2], qd[step % 2])
                for g in range(NC_):
                    if step >= 2:
                        pe.wait_ge(level_taken, (step - 2) * NC_ + g + 1)
                    for k in range(TPC):
                        t = g * TPC + k
                        last = nc.tensor.matmul(core.ps[:, 4 * (step % 2) + g, k * P:(k + 1) * P], tile_of(kk, t),
                                                tile_of(qq, t), start=True, stop=True)
                    last.then_inc(level_done, 1)
            pe.wait_ge(decayed, NSTEP)
            for g in range(NC_):
                pe.wait_ge(level_taken, (NSTEP - 2) * NC_ + g + 1)
                for k in range(TPC):
                    last = nc.tensor.transpose(core.ps[:, g, k * P:(k + 1) * P], tile_of(kd[NSTEP % 2], g * TPC + k),
                                               core.ident[:])
                last.then_inc(turned, 1)
            for g in range(NC_):
                pe.wait_ge(k_copied, g + 1)
                pe.wait_ge(level_taken, (NSTEP - 1) * NC_ + g + 1)
                for k in range(TPC):
                    t = g * TPC + k
                    last = nc.tensor.matmul(core.ps[:, 4 + g, k * P:(k + 1) * P], k_tok[:, t, :], v[:, t, :],
                                            start=True, stop=True)
                last.then_inc(u_done, 1)
            pe.wait_ge(k_copied, NC_)
            for g in range(NC_):
                for k in range(TPC):
                    t = g * TPC + k
                    bank = core.ps[:, g, k * P:(k + 1) * P]
                    last = nc.tensor.matmul(bank, att[:, t, :], v[:, t, :], start=True, stop=t == 0)
                    if t:
                        pe.wait_ge(state_done, t)
                        last = nc.tensor.matmul(bank, tile_of(qd[NSTEP % 2], t), states[:, t, :], start=False, stop=True)
                last.then_inc(o_done, 1)
            pe.wait_ge(o_taken, NC_)
            ln_o.tensor(pe)
            pe.wait_ge(state_done, NT - 1)
            for g in range(NC_):
                pe.wait_ge(ln_o.T_ready, g + 1)
                for k in range(TPC):
                    last = nc.tensor.matmul(core.ps[:, 4 + g, k * P:(k + 1) * P], tile_of(o_T, g * TPC + k),
                                            w["W_out"][:], start=True, stop=True)
                last.then_inc(out_done, 1)

        @block.scalar
        def _(act):
            core.loaded(act, "ln_w")
            ln.scalar(act)
            n = 0
            for name in ("lg", "g1", "v", "gate", "q"):
                for c in range(NC_):
                    act.wait_ge(proj, n + 1)
                    src = core.ps[:, 4 + n % 4, :]
                    cols = slice(c * CH, (c + 1) * CH)
                    by_tile = src.rearrange("p (k d) -> p k d", d=P)
                    if name == "lg":
                        ins = nc.scalar.activation(fT[:, cols], src, ACT.Tanh, scale=0.5)
                    elif name == "g1":
                        ins = nc.scalar.copy(g1T[:, cols], src)
                    elif name == "v":
                        ins = nc.scalar.copy(v[:, c * TPC:(c + 1) * TPC, :], by_tile)
                    elif name == "gate":
                        ins = nc.scalar.activation(gate[:, c * TPC:(c + 1) * TPC, :], by_tile, ACT.Tanh, scale=0.5)
                    else:
                        ins = nc.scalar.activation(qT[:, cols], src, ACT.Silu)
                    ins.then_inc(proj_used, 1)
                    n += 1
            for g in range(NC_):
                act.wait_ge(turned, g + 1)
                nc.scalar.copy(k_tok[:, g * TPC:(g + 1) * TPC, :],
                               core.ps[:, g, :].rearrange("p (k d) -> p k d", d=P)).then_inc(k_copied, 1)
            ln_o.scalar(act)

        @block.vector
        def _(dve):
            line = core.dve_line
            core.loaded(dve, "masks")
            ln.vector(dve)
            dve.wait_ge(proj_used, NC_)
            nc.vector.tensor_scalar(kT[:], fT[:], -0.5, 0.5, ALU.mult, ALU.add).then_inc(f_ready, 1)
            dve.wait_ge(f_ready, 1)
            line.after(dve, nc.vector.tensor_scalar(fT[:], fT[:], 0.5, 0.5, ALU.mult, ALU.add))
            dve.wait_ge(proj_used, 4 * NC_)
            dve.wait_ge(proj, 4 * NC_)
            line.mark(nc.vector.tensor_scalar(gate[:], gate[:], 0.5, 0.5, ALU.mult, ALU.add))
            line.after(dve, nc.vector.memset(suf[:], 1.0))
            dve.wait_ge(proj_used, 5 * NC_)

            def take(step):
                for g in range(NC_):
                    dve.wait_ge(level_done, step * NC_ + g + 1)
                    src = core.ps[:, 4 * (step % 2) + g, :].rearrange("p (k d) -> p k d", d=P)
                    dst = att[:, g * TPC:(g + 1) * TPC, :]
                    if step == 0:
                        ins = nc.vector.tensor_tensor(dst, src, core.ident[:].unsqueeze(1).to_broadcast([P, TPC, P]),
                                                      ALU.mult)
                    else:
                        dve.wait_ge(level_taken, (step - 1) * NC_ + g + 1)
                        ins = nc.vector.copy_predicated(
                            dst, w["masks"][:, step - 1, :].unsqueeze(1).to_broadcast([P, TPC, P]), src)
                    ins.then_inc(level_taken, 1)

            for step in range(1, NSTEP):
                half = 1 << (step - 1)
                if step >= 3:
                    dve.wait_ge(level_done, (step - 1) * NC_)
                q_out, k_out = qd[step % 2], kd[step % 2]
                if step <= 2:
                    line.mark(nc.vector.tensor_tensor(k_out[:], kT[:], suf[:], ALU.mult))
                    line.wait(dve)
                    nc.vector.tensor_tensor(q_out[:], qT[:], pre[:], ALU.mult).then_inc(decayed, 1)
                else:
                    def part(a, side):
                        return a[:].rearrange("p (n i h) -> p n i h", i=2, h=half)[:, :, side, :]
                    line.after(dve, nc.vector.tensor_tensor(part(k_out, 0), part(kT, 0), part(suf, 0), ALU.mult))
                    nc.vector.tensor_tensor(part(q_out, 1), part(qT, 1), part(pre, 1), ALU.mult).then_inc(decayed, 1)
                dve.wait_ge(decayed, step)
                blocks = [a[:].rearrange("p (n i h) -> p n i h", i=2, h=half) for a in (pre, suf)]
                ends = blocks[0][:, :, :, half - 1:half]
                shape = [P, T // (2 * half), half]
                line.after(dve, nc.vector.tensor_tensor(blocks[1][:, :, 0, :], blocks[1][:, :, 0, :],
                                                        ends[:, :, 1, :].to_broadcast(shape), ALU.mult))
                line.after(dve, nc.vector.tensor_tensor(blocks[0][:, :, 1, :], blocks[0][:, :, 1, :],
                                                        ends[:, :, 0, :].to_broadcast(shape), ALU.mult))
                take(step - 1)
            dve.wait_ge(level_done, (NSTEP - 1) * NC_)
            line.mark(nc.vector.tensor_tensor(qd[NSTEP % 2][:], qT[:], pre[:], ALU.mult))
            line.wait(dve)
            nc.vector.tensor_tensor(kd[NSTEP % 2][:], kT[:], suf[:], ALU.mult).then_inc(decayed, 1)
            take(NSTEP - 1)
            for t in range(1, NT):
                if (t - 1) % TPC == 0:
                    dve.wait_ge(u_done, (t - 1) // TPC + 1)
                u = core.ps[:, 4 + (t - 1) // TPC, ((t - 1) % TPC) * P:((t - 1) % TPC + 1) * P]
                if t == 1:
                    ins = nc.vector.tensor_copy(states[:, t, :], u)
                else:
                    dve.wait_ge(state_done, t - 1)
                    ins = nc.vector.scalar_tensor_tensor(out=states[:, t, :], in0=states[:, t - 1, :],
                                                         scalar=pre[:, t * P - 1:t * P], in1=u,
                                                         op0=ALU.mult, op1=ALU.add)
                ins.then_inc(state_done, 1)
            for g in range(NC_):
                dve.wait_ge(o_done, g + 1)
                cols = slice(g * TPC, (g + 1) * TPC)
                nc.vector.tensor_tensor(o_gated[:, cols, :], core.ps[:, g, :].rearrange("p (k d) -> p k d", d=P),
                                        gate[:, cols, :], ALU.mult).then_inc(o_taken, 1)
            dve.wait_ge(o_taken, NC_)
            ln_o.vector(dve)
            for g in range(NC_):
                dve.wait_ge(out_done, g + 1)
                xc = core.x[:, g * TPC:(g + 1) * TPC, :]
                nc.vector.tensor_tensor(xc, xc, core.ps[:, 4 + g, :].rearrange("p (k d) -> p k d", d=P),
                                        ALU.add).then_inc(added, 1)
            dve.wait_ge(added, NC_)


WEIGHTS = {
    "Wq0": ("L0_attn_a_Wq", lambda a: a.T),
    "Wk0": ("L0_attn_a_Wk", lambda a: a.T),
    "Wv0": ("L0_attn_a_Wv", lambda a: a.T),
    "Wu0": ("L0_attn_a_Wu", lambda a: a.T),
    "bu": ("L0_attn_a_bu", lambda a: np.broadcast_to(a, (P, P))),
    "gate0": ("L0_ffn_gate_w", lambda a: a.T),
    "w12": ("L0_ffn_w12", lambda a: a.transpose(2, 0, 1)),
    "w3": ("L0_ffn_w3", lambda a: a.reshape(E0, P, H0 // P, P).transpose(3, 0, 2, 1)),
    "norm_g": ("L0_attn_b_norm_g", lambda a: a[:, None]),
    "norm_b": ("L0_attn_b_norm_b", lambda a: a[:, None]),
    "in_proj": ("L0_attn_b_in_proj_w", lambda a: a.T),
    "conv_w": ("L0_attn_b_conv_w", lambda a: a.reshape(ND, P, DCONV).transpose(1, 0, 2)),
    "conv_b": ("L0_attn_b_conv_b", lambda a: a.reshape(ND, P).T),
    "x_bc": ("L0_attn_b_x_proj_w", lambda a: np.tile(a[DTR:].T, (1, 3)).reshape(ND, P, 3 * 2 * DS).transpose(1, 0, 2)),
    "x_dt": ("L0_attn_b_x_proj_w", lambda a: a[:DTR].T.reshape(ND, P, DTR).transpose(1, 0, 2)),
    "dt_proj": ("L0_attn_b_dt_proj_w", lambda a: a.T),
    "dt_b": ("L0_attn_b_dt_proj_b", lambda a: a.reshape(ND, P).T),
    "log_A": ("L0_attn_b_log_A", lambda a: a.reshape(ND, P, DS).transpose(1, 0, 2)),
    "Dp": ("L0_attn_b_Dp", lambda a: a.reshape(ND, P).T),
    "out_proj": ("L0_attn_b_out_proj_w", lambda a: a.T.reshape(ND, P, P).transpose(1, 0, 2)),
    "Wq1": ("L1_attn_a_Wq", lambda a: a),
    "Wk1": ("L1_attn_a_Wk", lambda a: a),
    "Wv1": ("L1_attn_a_Wv", lambda a: a),
    "Wo1": ("L1_attn_a_Wo", lambda a: a),
    "bo": ("L1_attn_a_bo", lambda a: np.broadcast_to(a, (P, P))),
    "gate1": ("L1_ffn_gate_w", lambda a: a.T),
    "e_bias": ("L1_ffn_e_bias", lambda a: np.broadcast_to(a, (P, E1))),
    "w_up1": (("L1_ffn_gate_proj", "L1_ffn_up_proj"),
              lambda g, u: np.stack([a.reshape(E1 // 2, 2 * I1, P) for a in (g, u)], 1).transpose(3, 0, 1, 2)),
    "w_down1": ("L1_ffn_down_proj", lambda a: a.reshape(E1 // 2, 2, P, I1).transpose(1, 3, 0, 2).reshape(2 * I1, E1 // 2, P)),
    "sh_up": (("L1_ffn_shared_gate_w", "L1_ffn_shared_up_w"), lambda g, u: np.pad(np.stack([g, u], 0), ((0, 0), (0, I1), (0, 0))).transpose(2, 0, 1)),
    "sh_down": ("L1_ffn_shared_down_w", lambda a: a.T),
    "W_in": ("L1_attn_b_W_in", lambda a: a.T),
    "W_out": ("L1_attn_b_W_out", lambda a: a.T),
    "W_g1": ("L1_attn_b_W_g1", lambda a: a.T),
    "W_g2": ("L1_attn_b_W_g2", lambda a: a.T),
    "ln_w": ("L1_attn_b_ln_w", lambda a: a[:, None]),
}


def constants():
    pick = np.zeros((96, 2 * DS, P), np.uint16)
    for s in range(2 * DS):
        pick[[s, 2 * DS + s, 4 * DS + s], s, :] = 0x3F80
    i = np.arange(P)
    masks = [(i[:, None] // (2 << n) == i // (2 << n)) & (i[:, None] // (1 << n) % 2 == 0) & (i // (1 << n) % 2 == 1)
             for n in range(LEVELS)]
    earlier = np.tril(np.ones((GROUPS, GROUPS), np.float32), -1)
    return {"pick": pick, "masks": np.stack(masks, 1).astype(np.int32),
            "earlier": np.broadcast_to(earlier.reshape(1, -1), (P, GROUPS * GROUPS))}


def stack(nc, x, out, weights, ident, stages):
    with ExitStack() as ctx:
        core = Core(nc, ctx)
        core.ps = ctx.enter_context(nc.psum_tensor("ps", [P, 8, CH], F32))
        core.x = core.sb("x_res", [P, NT, P])
        core.xn = core.sb("xn", [P, NT, P])
        core.xnT = core.sb("xnT", [P, T])
        core.ident = core.sb("ident", [P, P])
        core.one = core.sb("one", [P, 1])
        core.o_zeroed = core.sem("o_zeroed")
        x_loaded, out_stored = core.sem("x_loaded"), core.sem("out_stored")
        w_loaded = {}
        for name, ap in weights.items():
            core.w[name] = core.sb(f"w_{name}", list(ap.shape), ap.dtype)
            w_loaded[name] = core.sem(f"loaded_{name}")

        def loaded(eng, *names):
            for n in names:
                eng.wait_ge(w_loaded[n], 16)

        def load_weights(eng):
            for name, ap in weights.items():
                eng.dma_start(core.w[name][:], ap).then_inc(w_loaded[name], 16)

        core.loaded = loaded
        core.load_weights = load_weights
        with nc.Block() as block:
            @block.vector
            def _(dve):
                core.dve_line.after(dve, nc.vector.memset(core.one[:], 1.0))

            @block.sync
            def _(sp):
                sp.dma_start(core.ident[:], ident).then_inc(x_loaded, 16)
                sp.dma_start(core.x[:], x[0].rearrange("(t p) d -> p t d", p=P)).then_inc(x_loaded, 16)
                sp.wait_ge(x_loaded, 32)
        core.stage_sems = []
        for i, (build, *args) in enumerate(stages):
            if i == len(STAGES) // 2:
                core.clear_sems()
            build(core, *args)
        with nc.Block() as block:
            @block.sync
            def _(sp):
                sp.dma_start(out[0].rearrange("(t p) d -> p t d", p=P), core.x[:]).then_inc(out_stored, 16)
                sp.wait_ge(out_stored, 16)
                for name in weights:
                    sp.wait_ge(w_loaded[name], 16)


STAGES = ((softmax_attention,), (experts_top2, "e1"), (selective_scan,), (experts_top2, "e2"),
          (linear_attention,), (experts_top4, "m1"), (gated_linear_attention,), (experts_top4, "m2"))


def kernel(**inputs):
    import concourse.bacc as bacc
    from concourse.bass_utils import run_bass_kernel_spmd

    nc = bacc.Bacc("TRN2", target_bir_lowering=False, num_devices=1)
    arrays, aps = {}, {}

    def given(name, a):
        a = np.ascontiguousarray(a)
        arrays[name] = a
        return nc.dram_tensor(name, a.shape, mybir.dt.from_np(a.dtype), kind="ExternalInput").ap()

    x = given("x_dram", inputs["L0_attn_a_x"])
    ident = given("ident_dram", np.eye(P, dtype=np.float32))
    for name, (source, layout) in WEIGHTS.items():
        sources = (source,) if isinstance(source, str) else source
        aps[name] = given(f"{name}_dram", layout(*(np.asarray(inputs[n]) for n in sources)))
    for name, a in constants().items():
        aps[name] = given(f"{name}_dram", a)
    out = nc.dram_tensor("out_dram", (1, T, P), F32, kind="ExternalOutput").ap()
    stack(nc, x, out, aps, ident, STAGES)
    r = run_bass_kernel_spmd(nc, [arrays], core_ids=[0])
    return r.results[0]["out_dram"]
```

```python
from contextlib import ExitStack

import numpy as np

import concourse.bass as bass
from concourse import mybir

ALU = mybir.AluOpType
ACT = mybir.ActivationFunctionType
F32 = mybir.dt.float32
BF16 = mybir.dt.bfloat16
U32 = mybir.dt.uint32
AX_X = mybir.AxisListType.X

P = 128
T = 2048
NT = T // P
CH = 512
NC_ = T // CH
TPC = CH // P
EPS = 1e-5

HEADS = 16
HD = P // HEADS
E0, H0, TOP0 = 8, 256, 2
DI, DS, DCONV, DTR = 256, 16, 4, 8
ND = DI // P
E1, I1, GROUPS, TOPG, TOP1 = 16, 64, 4, 2, 4
SCALING = 2.5
LEVELS = 7


class Line:

    def __init__(self, sem):
        self.sem, self.n = sem, 0

    def mark(self, ins):
        self.n += 1
        ins.then_inc(self.sem, 1)

    def wait(self, eng):
        eng.wait_ge(self.sem, self.n)

    def after(self, eng, ins):
        self.mark(ins)
        self.wait(eng)


class Core:

    def __init__(self, nc, ctx):
        self.nc, self.ctx = nc, ctx
        self.w = {}
        self.stage_sems = []
        self.dve_line = Line(self.sem("dve_line"))
        self.act_line = Line(self.sem("act_line"))

    def sem(self, name):
        self.stage_sems.append(self.nc.alloc_semaphore(name=name))
        return self.stage_sems[-1]

    def sb(self, name, shape, dt=F32):
        return self.ctx.enter_context(self.nc.sbuf_tensor(name, shape, dt))

    def clear_sems(self):
        self.nc.clear_and_free_semaphores(self.stage_sems)
        self.nc.all_engine_barrier()
        self.stage_sems = []


def tile_of(a, t):
    return a[:, t * P:(t + 1) * P]


class LayerNorm:

    def __init__(self, core, ctx, name, src, out, outT, gain=None, shift=None, banks=(0, 1)):
        nc = core.nc
        self.core, self.src, self.out, self.outT = core, src, out, outT
        self.gain, self.shift, self.banks = gain, shift, banks

        def sb(n, shape):
            return ctx.enter_context(nc.sbuf_tensor(f"{name}_{n}", shape, F32))

        self.stats = sb("stats", [P, NT, 6])
        self.mv = sb("mv", [P, NT, 2])
        self.veps = sb("veps", [P, NT])
        self.root = sb("root", [P, NT])
        self.warm = sb("warm", [P, 1])
        self.parts = (slice(0, TPC), slice(TPC, NT))
        self.r0 = sb("r0", [P, NT])
        self.r2 = sb("r2", [P, NT])
        self.rstd = sb("rstd", [P, NT])
        self.var_ready = core.sem(f"{name}_var_ready")
        self.rooted = core.sem(f"{name}_rooted")
        self.normed = core.sem(f"{name}_normed")
        self.turned = core.sem(f"{name}_turned")
        self.T_ready = core.sem(f"{name}_T_ready")

    def vector(self, dve):
        nc, line = self.core.nc, self.core.dve_line
        for i, part in enumerate(self.parts):
            tiles = range(part.start, part.stop)
            for t in tiles:
                line.mark(nc.vector.bn_stats(self.stats[:, t, :], self.src[:, t, :]))
            line.wait(dve)
            for t in tiles:
                line.mark(nc.vector.bn_aggr(self.mv[:, t, :], self.stats[:, t, :]))
            line.wait(dve)
            veps, root, r0, r2, rstd = (a[:, part] for a in (self.veps, self.root, self.r0, self.r2, self.rstd))
            nc.vector.tensor_scalar(veps, self.mv[:, part, 1], EPS, None, ALU.add).then_inc(self.var_ready, 1)
            dve.wait_ge(self.rooted, i + 1)
            line.after(dve, nc.vector.reciprocal(r0, root))
            line.after(dve, nc.vector.tensor_tensor(r2, r0, r0, ALU.mult))
            line.after(dve, nc.vector.tensor_tensor(r2, r2, veps, ALU.mult))
            line.after(dve, nc.vector.tensor_scalar(r2, r2, -0.5, 1.5, ALU.mult, ALU.add))
            line.after(dve, nc.vector.tensor_tensor(rstd, r0, r2, ALU.mult))
            for t in tiles:
                nc.vector.tensor_scalar(self.out[:, t, :], self.src[:, t, :], self.mv[:, t, 0:1], self.rstd[:, t:t + 1],
                                        ALU.subtract, ALU.mult).then_inc(self.normed, 1)

    def scalar(self, act):
        nc = self.core.nc
        self.core.act_line.after(act, nc.scalar.activation(self.warm[:], self.core.one[:], ACT.Sqrt))
        for i, part in enumerate(self.parts):
            act.wait_ge(self.var_ready, i + 1)
            nc.scalar.activation(self.root[:, part], self.veps[:, part], ACT.Sqrt).then_inc(self.rooted, 1)
            if self.outT is not None:
                self.copy_turned(act, range(part.start // TPC, part.stop // TPC))

    def copy_turned(self, act, chunks):
        nc = self.core.nc
        for c in chunks:
            act.wait_ge(self.turned, c + 1)
            bank = self.core.ps[:, self.banks[c % 2], :]
            dst = self.outT[:, c * CH:(c + 1) * CH]
            if self.gain is None:
                nc.scalar.copy(dst, bank).then_inc(self.T_ready, 1)
            elif self.shift is None:
                nc.scalar.activation(dst, bank, ACT.Identity, scale=self.gain).then_inc(self.T_ready, 1)
            else:
                nc.scalar.activation(dst, bank, ACT.Identity, bias=self.shift, scale=self.gain).then_inc(self.T_ready, 1)

    def tensor(self, pe, then=lambda c: None):
        nc, core = self.core.nc, self.core
        for c in range(NC_):
            if c >= 2:
                pe.wait_ge(self.T_ready, c - 1)
            for k in range(TPC):
                pe.wait_ge(self.normed, c * TPC + k + 1)
                last = nc.tensor.transpose(core.ps[:, self.banks[c % 2], k * P:(k + 1) * P],
                                           self.out[:, c * TPC + k, :], core.ident[:])
            last.then_inc(self.turned, 1)
            for done in {0: (0,), 1: (), NC_ - 1: (NC_ - 2, NC_ - 1)}.get(c, (c - 1,)):
                then(done)


def softmax_attention(core):
    nc, w = core.nc, core.w
    SCALE = float(HD) ** -0.5
    NPART, KROWS = 3, 6 * HD
    ROWS = KROWS + NPART
    QPARTS = ((0, 3), (0, 2), (0, 1))
    KTIMES = (3, 2, 1)
    RING = 4
    LAG_S = NT + 3
    LAG_V = LAG_S + 2
    NBUF = 3
    BODY = NBUF * NT
    LOOPED = (HEADS - 1) // NBUF
    S_BANK, S_RING, O_BANK = 4, 3, 7
    VROWS = 2 * HD
    with ExitStack() as ctx:
        def sb(name, shape, dt=F32):
            return ctx.enter_context(nc.sbuf_tensor(name, shape, dt))

        xn, xnT = core.xn, core.xnT
        ln = LayerNorm(core, ctx, "ln_a", core.x, xn, xnT)
        v_all = sb("v_all", [P, NT, P])
        v_head = [sb(f"v_head{i}", [P, NT, VROWS]) for i in range(NBUF)]
        qst = [sb(f"q_stack{i}", [P, T], BF16) for i in range(NBUF)]
        kst = [sb(f"k_stack{i}", [P, T], BF16) for i in range(NBUF)]
        ones = sb("ones", [NPART, T], BF16)
        probs = sb("probs", [P, RING, T])
        mx = sb("row_max", [P, NT, 2])
        neg_max = sb("neg_max", [P, 32])
        nmT = sb("neg_maxT", [P, 32])
        nm_rest = sb("neg_max_rest", [P, 32])
        nm_parts = sb("neg_max_parts", [P, NPART, 32], BF16)
        by_one = sb("by_one", [P, 32])
        o_sb = sb("o_sb", [P, CH])
        whole = [probs[:, i, :] for i in range(2)]
        parts = sb("parts", [P, 2, NPART, T], BF16)
        attT, den = sb("attT", [P, T]), xnT
        late = sb("late", [P, 2, P])
        FULL = (HEADS - 1) * HD
        qd = nc.dram_tensor("q_parts_dram", (HEADS, NPART, HD, T), BF16).ap()
        kd = nc.dram_tensor("k_parts_dram", (HEADS, NPART, HD, T), BF16).ap()
        md = [nc.dram_tensor(f"max_dram{i}", (NPART, T), BF16).ap() for i in range(NBUF)]

        od = nc.dram_tensor("o_dram", (2, HEADS, HD, T), F32).ap()
        proj = core.sem("a_proj")
        proj_used = core.sem("a_proj_used")
        first_parts = core.sem("a_first_parts")
        split_done = core.sem("a_split")
        parts_stored = core.sem("a_parts_stored")
        masked = core.sem("a_masked")
        ones_set = core.sem("a_ones")
        ones_placed = core.sem("a_ones_placed")
        stacked = [core.sem(f"a_stacked{i}") for i in range(NBUF)]
        p1_done = core.sem("a_pass1_scores")
        max_done = core.sem("a_max_done")
        nm_found = core.sem("a_nm_found")
        nm_turned = core.sem("a_nm_turned")
        nm_line = core.sem("a_nm_line")
        nm_ready = core.sem("a_nm_ready")
        m_stored = core.sem("a_max_stored")
        m_loaded = [core.sem(f"a_max_loaded{i}") for i in range(NBUF)]
        v_staged = core.sem("a_v_staged")
        s_done = core.sem("a_scores")
        exp_done = core.sem("a_exp")
        pv_done = core.sem("a_pv")
        evacuated = core.sem("a_evacuated")
        o_stored = core.sem("a_o_stored")
        fin_loaded = core.sem("a_fin_loaded")
        cleared = core.sem("a_cleared")
        late_loaded = core.sem("a_late_loaded")
        late_rden = core.sem("a_late_rden")
        late_ready = core.sem("a_late_ready")
        late_placed = core.sem("a_late_placed")
        rden_ready = core.sem("a_rden_ready")
        att_ready = core.sem("a_att_ready")
        out_done = core.sem("a_out_done")
        bias_added = core.sem("a_bias_added")

        block = ctx.enter_context(nc.Block())
        O_STORE = 16 * NC_
        STACK = 16 * (len(QPARTS) + len(KTIMES))

        @block.sync
        def _(sp):
            core.load_weights(sp)
            for which, dram in enumerate((qd, kd)):
                for p in range(NPART):
                    if p == 0:
                        sp.wait_ge(first_parts, NC_ * (which + 1))
                    else:
                        sp.wait_ge(split_done, 3 * NC_ * which + (p + 1) * NC_)
                    sp.dma_start(dram[:, p].rearrange("h s t -> h s t"),
                                 parts[:, which, p, :]).then_inc(parts_stored, 16)
            sp.wait_ge(parts_stored, 16 * 2 * NPART)
            sp.wait_ge(ones_set, 3 * NBUF + 2)

            def load_stack(head, par):
                row = 0
                for first, n in QPARTS:
                    sp.dma_start(qst[par][row:row + n * HD, :],
                                 qd[head, first:first + n].rearrange("p s t -> (p s) t")).then_inc(stacked[par], 16)
                    row += n * HD
                row = 0
                for part, n in enumerate(KTIMES):
                    sp.dma_start(kst[par][row:row + n * HD, :],
                                 kd[head, part:part + 1].to_broadcast([n, HD, T])).then_inc(stacked[par], 16)
                    row += n * HD

            def store_max(head, par):
                sp.wait_ge(nm_ready, head + 1)
                for b in range(P // 32):
                    sp.dma_start(md[par].rearrange("p (j b i) -> b j p i", b=P // 32, i=32)[b],
                                   nm_parts[32 * b:32 * b + NT, :, :]).then_inc(m_stored, 16)
                sp.wait_ge(m_stored, (head + 1) * 64)
                sp.dma_start(qst[par][KROWS:ROWS, :], md[par]).then_inc(m_loaded[par], 16)

            def store_o(head):
                sp.wait_ge(evacuated, head + 1)
                for c in range(NC_):
                    sp.dma_start(od[:, head, :, c * CH:(c + 1) * CH],
                                 o_sb[32 * c:32 * c + VROWS, :]).then_inc(o_stored, 16)

            for head in range(NBUF):
                load_stack(head, head)
                sp.dma_start(kst[head][KROWS:ROWS, :], ones[:]).then_inc(ones_placed, 16)
            for head in range(NBUF - 1):
                store_max(head, head)
            store_o(0)
            with sp.Fori(1, LOOPED) as j:
                for par in range(NBUF):
                    sp.wait_ge(s_done, j * (4 * BODY) + (par + 1 - NBUF) * 4 * NT)
                    load_stack(j * NBUF + par, par)
                    store_max(j * NBUF + (par - 1), (par - 1) % NBUF)
                    store_o(j * NBUF + (par - 2))
            sp.wait_ge(s_done, (HEADS - NBUF) * 4 * NT)
            load_stack(HEADS - 1, (HEADS - 1) % NBUF)
            store_max(HEADS - 2, (HEADS - 2) % NBUF)
            store_o(HEADS - 3)
            store_max(HEADS - 1, (HEADS - 1) % NBUF)
            store_o(HEADS - 2)
            sp.wait_ge(o_stored, O_STORE * (HEADS - 1))
            sp.wait_ge(cleared, 2)
            for which, dst in enumerate((attT, den)):
                sp.dma_start(dst[0:FULL, :], od[which, 0:HEADS - 1]).then_inc(fin_loaded, 16)
            store_o(HEADS - 1)
            sp.wait_ge(o_stored, O_STORE * HEADS)
            for which in range(2):
                sp.dma_start(late[:, which, :],
                             od[which, HEADS - 1].rearrange("s (k n) -> (s k) n", n=P)).then_inc(late_loaded, 16)
            sp.wait_ge(att_ready, NC_)
            sp.wait_ge(late_ready, 1)
            sp.dma_start(attT[FULL:P, :].rearrange("s (k n) -> s k n", n=P), late[:, 0, :]).then_inc(late_placed, 16)

        @block.gpsimd
        def _(pool):
            core.loaded(pool, "Wq0", "Wk0")
            for name, sign in (("Wq0", 1), ("Wk0", -1)):
                nc.gpsimd.affine_select(out=w[name][:], in_=w[name][:], pattern=[[sign, P]], channel_multiplier=-sign,
                                        base=0, compare_op=ALU.is_ge, fill=0.0).then_inc(masked, 1)
            nc.gpsimd.memset(ones[:], 1.0).then_inc(ones_set, 1)
            nc.gpsimd.memset(by_one[:], 1.0).then_inc(ones_set, 1)
            for par in range(NBUF):
                nc.gpsimd.memset(qst[par][:], 0.0).then_inc(ones_set, 1)
                nc.gpsimd.memset(kst[par][:], 0.0).then_inc(ones_set, 1)
                nc.gpsimd.memset(v_head[par][:], 1.0).then_inc(ones_set, 1)
            core.loaded(pool, "bu")
            pool.wait_ge(ln.normed, NT)
            for t in range(NT):
                nc.gpsimd.tensor_tensor(core.x[:, t, :], core.x[:, t, :], w["bu"][:], ALU.add).then_inc(bias_added, 1)
            pool.wait_ge(proj_used, 2 * NC_ + NC_)
            pool.wait_ge(ones_set, 3 * NBUF + 2)

            def stage_v(head, par):
                nc.gpsimd.tensor_copy(v_head[par][:, :, 0:HD], v_all[:, :, bass.ds(head * HD, HD)]).then_inc(v_staged, 1)

            def round_to(out, a):
                return nc.gpsimd.tensor_tensor(out, a, by_one[:], ALU.mult)

            def cut_max(head):
                pool.wait_ge(nm_turned, head + 1)
                if not isinstance(head, int) or head:
                    pool.wait_ge(m_stored, head * 64)
                round_to(nm_parts[:, 0, :], nmT[:]).then_inc(nm_line, 1)
                pool.wait_ge(nm_line, head * 4 + 1)
                nc.gpsimd.tensor_tensor(nm_rest[:], nmT[:], nm_parts[:, 0, :], ALU.subtract).then_inc(nm_line, 1)
                pool.wait_ge(nm_line, head * 4 + 2)
                round_to(nm_parts[:, 1, :], nm_rest[:]).then_inc(nm_line, 1)
                pool.wait_ge(nm_line, head * 4 + 3)
                nc.gpsimd.tensor_tensor(nm_rest[:], nm_rest[:], nm_parts[:, 1, :], ALU.subtract).then_inc(nm_line, 1)
                pool.wait_ge(nm_line, head * 4 + 4)
                round_to(nm_parts[:, 2, :], nm_rest[:]).then_inc(nm_ready, 1)

            for head in range(NBUF):
                stage_v(head, head)
            for a in (attT, den):
                nc.gpsimd.memset(a[:], 1.0).then_inc(cleared, 1)
            for head in range(NBUF - 1):
                cut_max(head)
            with pool.Fori(1, LOOPED) as j:
                for par in range(NBUF):
                    pool.wait_ge(pv_done, j * BODY + (par + 1 - NBUF) * NT)
                    stage_v(j * NBUF + par, par)
                    cut_max(j * NBUF + (par - 1))
            pool.wait_ge(pv_done, (HEADS - NBUF) * NT)
            stage_v(HEADS - 1, (HEADS - 1) % NBUF)
            for head in range(HEADS - 2, HEADS):
                cut_max(head)

        @block.tensor
        def _(pe):
            ln.tensor(pe)
            pe.wait_ge(masked, 2)
            n = 0
            for name in ("Wq0", "Wk0"):
                for c in range(NC_):
                    if name == "Wq0":
                        pe.wait_ge(ln.T_ready, c + 1)
                    if n >= 4:
                        pe.wait_ge(proj_used, n - 3)
                    nc.tensor.matmul(core.ps[:, 4 + n % 4, :], w[name][:], xnT[:, c * CH:(c + 1) * CH],
                                     start=True, stop=True).then_inc(proj, 1)
                    n += 1
            core.loaded(pe, "Wv0")
            for g in range(NC_):
                pe.wait_ge(proj_used, n - 3)
                for k in range(TPC):
                    last = nc.tensor.matmul(core.ps[:, 4 + n % 4, k * P:(k + 1) * P], tile_of(xnT, g * TPC + k),
                                            w["Wv0"][:], start=True, stop=True)
                last.then_inc(proj, 1)
                n += 1
            pe.wait_ge(proj_used, n)

            def slot(j, gs, maxima=True, scores=True, values=True):
                first_body = isinstance(j, int) and j == 0

                def find(b):
                    buf, u = gs // NT % NBUF, gs % NT
                    if u == 0 and b == 0:
                        pe.wait_ge(stacked[buf], j * STACK + STACK)
                    if not first_body or gs:
                        pe.wait_ge(max_done, j * (2 * BODY) + (2 * gs + b - 1))
                    for r in range(2):
                        key = (2 * b + r) * CH
                        last = nc.tensor.matmul(core.ps[:, 2 * b + r, :], qst[buf][0:KROWS, u * P:(u + 1) * P],
                                                kst[buf][0:KROWS, key:key + CH], start=True, stop=True)
                    last.then_inc(p1_done, 1)

                def score(c):
                    m = gs - LAG_S
                    buf, kt = m // NT % NBUF, m % NT
                    if kt == 0 and c == 0:
                        pe.wait_ge(m_loaded[buf], j * 16 + 16 * (m // BODY + 1))
                    n = 4 * m + c
                    if not first_body or n >= S_RING:
                        pe.wait_ge(exp_done, j * (4 * BODY) + (n - S_RING + 1))
                    nc.tensor.matmul(core.ps[:, S_BANK + n % S_RING, :], kst[buf][:, kt * P:(kt + 1) * P],
                                     qst[buf][:, c * CH:(c + 1) * CH], start=True, stop=True).then_inc(s_done, 1)

                for b in range(2):
                    if maxima:
                        find(b)
                    if scores:
                        score(2 * b)
                        score(2 * b + 1)
                if values:
                    m = gs - LAG_V
                    buf, kt = m // NT % NBUF, m % NT
                    if kt == 0:
                        pe.wait_ge(v_staged, j * NBUF + (m // NT + 1))
                        if not first_body or m:
                            pe.wait_ge(evacuated, j * NBUF + m // NT)
                    pe.wait_ge(exp_done, j * (4 * BODY) + 4 * (m + 1))
                    for c in range(NC_):
                        last = nc.tensor.matmul(core.ps[32 * c:32 * c + VROWS, O_BANK, :], v_head[buf][:, kt, :],
                                                probs[:, m % RING, c * CH:(c + 1) * CH],
                                                start=kt == 0, stop=kt == NT - 1)
                    last.then_inc(pv_done, 1)

            for gs in range(BODY):
                if gs == LAG_S:
                    pe.wait_ge(ones_placed, 16 * NBUF)
                slot(0, gs, True, gs >= LAG_S, gs >= LAG_V)
            with pe.Fori(1, LOOPED) as j:
                for gs in range(BODY):
                    slot(j, gs)
            for gs in range(NT + LAG_V):
                slot(LOOPED, gs, gs < NT, gs < NT + LAG_S)
            core.loaded(pe, "Wu0")
            pe.wait_ge(att_ready, NC_)
            pe.wait_ge(late_placed, 16)
            for g in range(NC_):
                for k in range(TPC):
                    last = nc.tensor.matmul(core.ps[:, g, k * P:(k + 1) * P], tile_of(attT, g * TPC + k), w["Wu0"][:],
                                            start=True, stop=True)
                last.then_inc(out_done, 1)

        @block.scalar
        def _(act):
            ln.scalar(act)
            for which, scale in enumerate((SCALE, 1.0)):
                for c in range(NC_):
                    act.wait_ge(proj, which * NC_ + c + 1)
                    cols = slice(c * CH, (c + 1) * CH)
                    nc.scalar.mul(whole[which][:, cols], core.ps[:, 4 + c, :], scale).then_inc(proj_used, 1)
                    act.wait_ge(proj_used, which * NC_ + c + 1)
                    nc.scalar.copy(parts[:, which, 0, cols], whole[which][:, cols]).then_inc(first_parts, 1)
            for g in range(NC_):
                act.wait_ge(proj, 2 * NC_ + g + 1)
                nc.scalar.copy(v_all[:, g * TPC:(g + 1) * TPC, :],
                               core.ps[:, 4 + g, :].rearrange("p (k d) -> p k d", d=P)).then_inc(proj_used, 1)

            def unit(j, us, first=False):
                if not first:
                    act.wait_ge(pv_done, j * BODY + (us - (RING - 1)))
                for c in range(NC_):
                    n = us * NC_ + c
                    act.wait_ge(s_done, j * (4 * BODY) + (n + 1))
                    nc.scalar.activation(probs[:, us % RING, c * CH:(c + 1) * CH], core.ps[:, S_BANK + n % S_RING, :],
                                         ACT.Exp).then_inc(exp_done, 1)

            def evacuate(head):
                act.wait_ge(pv_done, head * NT + NT)
                if not isinstance(head, int) or head:
                    act.wait_ge(o_stored, head * O_STORE)
                nc.scalar.copy(o_sb[:], core.ps[:, O_BANK, :]).then_inc(evacuated, 1)

            act.wait_ge(core.o_zeroed, 1)

            def body(j, units, first=False):
                for us in range(units):
                    if us % NT == 2 and not (first and us == 2):
                        evacuate(j * NBUF + (us // NT - 1))
                    unit(j, us, first and us < RING)

            body(0, BODY, first=True)
            with act.Fori(1, LOOPED) as j:
                body(j, BODY)
            body(LOOPED, NT)
            evacuate(HEADS - 1)

        @block.vector
        def _(dve):
            line = core.dve_line
            nc.vector.memset(core.ps[:, O_BANK, :], 0.0).then_inc(core.o_zeroed, 1)
            line.after(dve, nc.vector.memset(neg_max[:], 0.0))
            ln.vector(dve)
            for which in range(2):
                base = 3 * NC_ * which
                for step in range(3):
                    for c in range(NC_):
                        cols = slice(c * CH, (c + 1) * CH)
                        rest, (p0, p1, p2) = whole[which][:, cols], (parts[:, which, p, cols] for p in range(NPART))
                        if step == 0:
                            dve.wait_ge(first_parts, which * NC_ + c + 1)
                            ins = nc.vector.tensor_tensor(rest, rest, p0, ALU.subtract)
                        else:
                            dve.wait_ge(split_done, base + (step - 1) * NC_ + c + 1)
                            if step == 1:
                                ins = nc.vector.tensor_copy(p1, rest)
                            else:
                                ins = nc.vector.tensor_tensor(p2, rest, p1, ALU.subtract)
                        ins.then_inc(split_done, 1)

            def maxima(head, first_unit):
                for u in range(NT):
                    for b in range(2):
                        dve.wait_ge(p1_done, first_unit * 2 + (2 * u + b + 1))
                        nc.vector.tensor_reduce(mx[:, u, b:b + 1], core.ps[:, 2 * b:2 * b + 2, :],
                                                mybir.AxisListType.XY, ALU.max).then_inc(max_done, 1)
                dve.wait_ge(max_done, head * (2 * NT) + 2 * NT)
                nc.vector.tensor_reduce(neg_max[:, 0:NT], mx[:], AX_X, ALU.max, negate=True).then_inc(nm_found, 1)
                dve.wait_ge(nm_found, head + 1)
                if not isinstance(head, int) or head:
                    dve.wait_ge(nm_ready, head)
                nc.vector.transpose(nmT[:], neg_max[:]).then_inc(nm_turned, 1)
                dve.wait_ge(nm_turned, head + 1)

            maxima(0, 0)
            with dve.Fori(1, HEADS) as i:
                maxima(i, i * NT)
            for c in range(NC_):
                cols = slice(c * CH, (c + 1) * CH)
                if c == 0:
                    dve.wait_ge(cleared, 2)
                    dve.wait_ge(fin_loaded, 32)
                nc.vector.reciprocal(den[:, cols], den[:, cols]).then_inc(rden_ready, 1)
                dve.wait_ge(rden_ready, c + 1)
                nc.vector.tensor_tensor(attT[:, cols], attT[:, cols], den[:, cols], ALU.mult).then_inc(att_ready, 1)
            dve.wait_ge(late_loaded, 32)
            nc.vector.reciprocal(late[:, 1, :], late[:, 1, :]).then_inc(late_rden, 1)
            dve.wait_ge(late_rden, 1)
            nc.vector.tensor_tensor(late[:, 0, :], late[:, 0, :], late[:, 1, :], ALU.mult).then_inc(late_ready, 1)
            dve.wait_ge(bias_added, NT)
            for g in range(NC_):
                dve.wait_ge(out_done, g + 1)
                xs = core.x[:, g * TPC:(g + 1) * TPC, :]
                line.mark(nc.vector.tensor_tensor(xs, xs, core.ps[:, g, :].rearrange("p (k d) -> p k d", d=P), ALU.add))
            line.wait(dve)


def pick_top(core, dve, scores, top8, keep, work, k):
    nc, line = core.nc, core.dve_line
    ne = scores.shape[-1]
    kth = top8[:, :, k - 1:k].to_broadcast([P, NT, ne])
    line.mark(nc.vector.tensor_tensor(work["gt"][:], scores, kth, ALU.is_gt))
    line.after(dve, nc.vector.tensor_tensor(work["eq"][:], scores, kth, ALU.is_equal))
    line.mark(nc.vector.tensor_tensor_scan(out=work["nth"][:].rearrange("p t e -> p (t e)"),
                                           data0=keep[:].rearrange("p t e -> p (t e)"),
                                           data1=work["eq"][:].rearrange("p t e -> p (t e)"),
                                           initial=0.0, op0=ALU.mult, op1=ALU.add))
    line.after(dve, nc.vector.tensor_reduce(work["above"][:], work["gt"][:], AX_X, ALU.add))
    line.after(dve, nc.vector.tensor_scalar(work["room"][:], work["above"][:], -1.0, float(k), ALU.mult, ALU.add))
    line.after(dve, nc.vector.tensor_tensor(work["nth"][:], work["nth"][:],
                                            work["room"][:].unsqueeze(2).to_broadcast([P, NT, ne]), ALU.is_le))
    line.after(dve, nc.vector.tensor_tensor(work["nth"][:], work["nth"][:], work["eq"][:], ALU.mult))
    line.after(dve, nc.vector.tensor_tensor(work["sel"][:], work["gt"][:], work["nth"][:], ALU.add))


def experts_top2(core, tag):
    nc, w = core.nc, core.w
    NH = H0 // P
    UNITS = E0 * NH
    UP, DOWN = 0, 4
    with ExitStack() as ctx:
        def sb(name, shape, dt=F32):
            return ctx.enter_context(nc.sbuf_tensor(f"{tag}_{name}", shape, dt))

        ln = LayerNorm(core, ctx, f"ln_{tag}", core.x, core.xn, core.xnT, banks=(4, 5))
        xnT = core.xnT
        scores = sb("scores", [P, NT, E0])
        top8 = sb("top8", [P, NT, 8])
        keep = sb("keep", [P, NT, E0])
        work = {n: sb(n, [P, NT, E0]) for n in ("gt", "eq", "nth", "sel")}
        work.update({n: sb(n, [P, NT]) for n in ("above", "room")})
        expd = sb("expd", [P, NT, E0])
        probs = sb("probs", [P, NT, E0])
        total = sb("total", [P, NT])
        gate = [sb(f"gate{i}", [P, CH]) for i in range(2)]
        hidden = [sb(f"hidden{i}", [P, NH, CH]) for i in range(2)]

        scored = core.sem(f"{tag}_scored")
        exp_in = core.sem(f"{tag}_exp_in")
        exp_out = core.sem(f"{tag}_exp_out")
        up_done = core.sem(f"{tag}_up")
        gate_done = core.sem(f"{tag}_gate")
        hidden_done = core.sem(f"{tag}_hidden")
        down_done = core.sem(f"{tag}_down")
        added = core.sem(f"{tag}_added")
        block = ctx.enter_context(nc.Block())

        @block.tensor
        def _(pe):
            core.loaded(pe, "gate0", "w12", "w3")

            def up(j, u, chunk):
                e, half = u // NH, u % NH
                if not (isinstance(j, int) and u < 2):
                    pe.wait_ge(hidden_done, j * UNITS + (u - 1))
                for k in range(2):
                    col = (k * NH + half) * P
                    nc.tensor.matmul(core.ps[:, UP + 2 * (u % 2) + k, :], w["w12"][:, e, col:col + P],
                                     chunk, start=True, stop=True).then_inc(up_done, 1)

            def down(j, e):
                pe.wait_ge(hidden_done, j * UNITS + (e + 1) * NH)
                if not (isinstance(j, int) and e < 2):
                    pe.wait_ge(added, j * (E0 * TPC) + (e - 1) * TPC)
                for k in range(TPC):
                    for half in range(NH):
                        last = nc.tensor.matmul(core.ps[:, DOWN + e % 2, k * P:(k + 1) * P],
                                                hidden[e % 2][:, half, k * P:(k + 1) * P], w["w3"][:, e, half, :],
                                                start=half == 0, stop=half == NH - 1)
                last.then_inc(down_done, 1)

            def body(j, chunk):
                for e in range(E0):
                    for half in range(NH):
                        if e or not isinstance(j, int):
                            up(j, e * NH + half, chunk)
                    if e:
                        down(j, e - 1)
                down(j, E0 - 1)

            def start(c):
                pe.wait_ge(ln.T_ready, c + 1)
                for t in range(c * TPC, (c + 1) * TPC):
                    last = nc.tensor.matmul(core.ps[:, 7, t * E0:(t + 1) * E0], tile_of(xnT, t), w["gate0"][:],
                                            start=True, stop=True)
                if c == 0:
                    for u in range(2):
                        up(0, u, xnT[:, 0:CH])
                if c == NC_ - 1:
                    last.then_inc(scored, 1)

            ln.tensor(pe, start)
            body(0, xnT[:, 0:CH])
            with pe.Fori(1, NC_) as j:
                body(j, xnT[:, bass.ds(j * CH, CH)])

        @block.scalar
        def _(act):
            def silu(j, units):
                for u in units:
                    act.wait_ge(up_done, j * (2 * UNITS) + (2 * u + 1))
                    if not (isinstance(j, int) and u < 2):
                        act.wait_ge(hidden_done, j * UNITS + (u - 1))
                    nc.scalar.activation(gate[u % 2][:], core.ps[:, UP + 2 * (u % 2), :], ACT.Silu).then_inc(gate_done, 1)

            ln.scalar(act)
            silu(0, range(2))
            act.wait_ge(exp_in, 1)
            nc.scalar.activation(expd[:], expd[:], ACT.Exp).then_inc(exp_out, 1)

            silu(0, range(2, UNITS))
            with act.Fori(1, NC_) as j:
                silu(j, range(UNITS))

        @block.vector
        def _(dve):
            line = core.dve_line

            def multiply(j, u):
                dve.wait_ge(gate_done, j * UNITS + (u + 1))
                dve.wait_ge(up_done, j * (2 * UNITS) + (2 * u + 2))
                e = u // NH
                if not (isinstance(j, int) and e < 2) and u % NH == 0:
                    dve.wait_ge(down_done, j * E0 + (e - 1))
                nc.vector.tensor_tensor(hidden[e % 2][:, u % NH, :], gate[u % 2][:], core.ps[:, UP + 2 * (u % 2) + 1, :],
                                        ALU.mult).then_inc(hidden_done, 1)

            line.after(dve, nc.vector.memset(keep[:], 1.0))
            line.mark(nc.vector.memset(keep[:, :, 0:1], 0.0))
            ln.vector(dve)
            for u in range(2):
                multiply(0, u)
            dve.wait_ge(scored, 1)
            line.after(dve, nc.vector.tensor_copy(scores[:], core.ps[:, 7, 0:NT * E0].rearrange("p (t e) -> p t e", e=E0)))
            for t in range(NT):
                line.mark(nc.vector.max(top8[:, t, :], scores[:, t, :]))
            line.wait(dve)
            nc.vector.tensor_tensor(expd[:], scores[:], top8[:, :, 0:1].to_broadcast([P, NT, E0]),
                                    ALU.subtract).then_inc(exp_in, 1)
            pick_top(core, dve, scores[:], top8, keep, work, TOP0)
            dve.wait_ge(exp_out, 1)
            line.after(dve, nc.vector.tensor_tensor(expd[:], expd[:], work["sel"][:], ALU.mult))
            line.after(dve, nc.vector.tensor_reduce(total[:], expd[:], AX_X, ALU.add))
            line.after(dve, nc.vector.reciprocal(total[:], total[:]))
            line.after(dve, nc.vector.tensor_tensor(probs[:], expd[:], total[:].unsqueeze(2).to_broadcast([P, NT, E0]),
                                                    ALU.mult))

            def add(j, e):
                dve.wait_ge(down_done, j * E0 + (e + 1))
                for k in range(TPC):
                    if e:
                        dve.wait_ge(added, j * (E0 * TPC) + ((e - 1) * TPC + k + 1))
                    t = j * TPC + k
                    xs = core.x[:, bass.ds(t, 1), :].rearrange("p t d -> p (t d)")
                    nc.vector.scalar_tensor_tensor(out=xs, in0=core.ps[:, DOWN + e % 2, k * P:(k + 1) * P],
                                                   scalar=probs[:, bass.ds(t, 1), e], in1=xs,
                                                   op0=ALU.mult, op1=ALU.add).then_inc(added, 1)

            def body(j):
                for e in range(E0):
                    for half in range(NH):
                        if e or not isinstance(j, int):
                            multiply(j, e * NH + half)
                    if e:
                        add(j, e - 1)
                add(j, E0 - 1)

            body(0)
            with dve.Fori(1, NC_) as j:
                body(j)


def selective_scan(core):
    nc, w = core.nc, core.w
    PAD = DCONV - 1
    with ExitStack() as ctx:
        def sb(name, shape, dt=F32):
            return ctx.enter_context(nc.sbuf_tensor(f"s_{name}", shape, dt))

        delta = [sb(f"delta{d}", [P, T]) for d in range(ND)]
        xn2 = delta[0][:].rearrange("p (t d) -> p t d", d=P)
        xnT = core.xnT
        ln1 = LayerNorm(core, ctx, "ln_s1", core.x, core.xn, None)
        ln2 = LayerNorm(core, ctx, "ln_s2", core.xn, xn2, xnT, w["norm_g"][:], w["norm_b"][:])
        pre = [sb(f"pre{d}", [P, PAD + T]) for d in range(ND)]
        soft = [pre[d][:, 0:T] for d in range(ND)]
        zs = [sb(f"zs{d}", [P, T]) for d in range(ND)]
        xs = [sb(f"xs{d}", [P, T]) for d in range(ND)]
        delta_c = [sb(f"delta_c{d}", [P, CH]) for d in range(ND)]
        dx_c = [sb(f"dx_c{d}", [P, CH]) for d in range(ND)]
        pick = w["pick"][:].bitcast(BF16)
        bc = sb("bc", [96, T], BF16)
        w_delta = sb("w_delta", [P, ND, DI])
        a_neg = sb("a_neg", [P, ND, DS])
        RING = 4
        B_RING = 3
        da = [sb(f"da{i}", [P, CH]) for i in range(RING)]
        rest = da[0][0:96, :]
        dbx = [sb(f"dbx{i}", [P, CH]) for i in range(RING)]
        full = da[1][0:96, :]
        mid = dbx[0][0:96, :].bitcast(BF16)[:, 0:CH]
        b_rows = [sb(f"b_rows{i}", [P, CH]) for i in range(B_RING)]
        h = sb("h", [P, ND, CH])
        hc = [sb(f"hc{i}", [P, CH]) for i in range(2)]
        state = sb("state", [P, DS, ND])
        yT = [sb(f"yT{d}", [P, CH]) for d in range(ND)]

        padded = core.sem("s_padded")
        in_done = core.sem("s_in_done")
        in_used = core.sem("s_in_used")
        conv_done = core.sem("s_conv")
        conv_silu = core.sem("s_conv_silu")
        xp_done = core.sem("s_xp")
        bc_ready = core.sem("s_bc_ready")
        full_copied = core.sem("s_full_copied")
        cut_line = core.sem("s_cut_line")
        merged = core.sem("s_merged")
        merged_copied = core.sem("s_merged_copied")
        dt_done = core.sem("s_dt_done")
        absolute = core.sem("s_absolute")
        positive = core.sem("s_positive")
        exp_done = core.sem("s_exp_done")
        log_done = core.sem("s_log_done")
        delta_done = core.sem("s_delta")
        chunk_ready = core.sem("s_chunk_ready")
        residual = core.sem("s_residual")
        b_spread = core.sem("s_b_spread")
        c_spread = core.sem("s_c_spread")
        b_copied = core.sem("s_b_copied")
        da_done = core.sem("s_da")
        dbx_done = core.sem("s_dbx")
        scanned = core.sem("s_scanned")
        saved = core.sem("s_saved")
        hc_done = core.sem("s_hc")
        summed = core.sem("s_summed")
        y_done = core.sem("s_y")
        out_done = core.sem("s_out")
        x_added = core.sem("s_x_added")

        DT_BANKS = (2, 4, 6, 2)
        B_BANKS, C_BANK, Y_BANK, O_BANK = (0, 1, 7), 2, 4, 6
        UNITS = DS * ND
        block = ctx.enter_context(nc.Block())

        @block.gpsimd
        def _(pool):
            for d in range(ND):
                nc.gpsimd.memset(pre[d][:, 0:PAD], 0.0).then_inc(padded, 1)
            nc.gpsimd.memset(state[:], 0.0).then_inc(padded, 1)
            pool.wait_ge(ln1.normed, NT)
            for t in range(NT):
                nc.gpsimd.tensor_tensor(core.x[:, t, :], core.x[:, t, :], core.xn[:, t, :], ALU.add).then_inc(residual, 1)

            for c in range(NC_):
                cols = slice(c * CH, (c + 1) * CH)
                pool.wait_ge(full_copied, 2 * (c + 1))
                nc.gpsimd.tensor_tensor(rest, full, bc[:, cols], ALU.subtract).then_inc(cut_line, 1)
                pool.wait_ge(cut_line, 3 * c + 1)
                nc.gpsimd.tensor_copy(mid, rest).then_inc(cut_line, 1)
                pool.wait_ge(cut_line, 3 * c + 2)
                nc.gpsimd.tensor_copy(bc[32:64, cols], mid[32:64, :]).then_inc(cut_line, 1)
                pool.wait_ge(cut_line, 3 * c + 3)
                nc.gpsimd.tensor_tensor(bc[64:96, cols], rest[64:96, :], mid[64:96, :],
                                        ALU.subtract).then_inc(bc_ready, 1)
                pool.wait_ge(bc_ready, c + 1)

            def body(j):
                pool.wait_ge(chunk_ready, j * 2 * ND + 2 * ND)
                for s in range(DS):
                    for d in range(ND):
                        u = s * ND + d
                        if not (isinstance(j, int) and u < RING):
                            pool.wait_ge(scanned, j * UNITS + (u - RING + 1))
                        pool.wait_ge(b_copied, j * DS + (s + 1))
                        nc.gpsimd.tensor_tensor(dbx[u % RING][:], dx_c[d][:], b_rows[s % B_RING][:],
                                                ALU.mult).then_inc(dbx_done, 1)

            body(0)
            with pool.Fori(1, NC_) as j:
                body(j)

        @block.tensor
        def _(pe):
            core.loaded(pe, "x_dt", "dt_proj")
            for d in range(ND):
                last = nc.tensor.matmul(core.ps[:, DT_BANKS[0], d * DI:(d + 1) * DI], w["x_dt"][:, d * P:(d + 1) * P],
                                        w["dt_proj"][:], start=True, stop=True)
            last.then_inc(merged, 1)
            core.loaded(pe, "in_proj", "x_bc", "out_proj")

            def project_in(c):
                pe.wait_ge(ln2.T_ready, c + 1)
                for m in range(2 * ND):
                    if c:
                        pe.wait_ge(in_used, (c - 1) * 2 * ND + m + 1)
                    nc.tensor.matmul(core.ps[:, 4 + m, :], w["in_proj"][:, m * P:(m + 1) * P],
                                     xnT[:, c * CH:(c + 1) * CH], start=True, stop=True).then_inc(in_done, 1)

            def project_x(c):
                if c == 0:
                    pe.wait_ge(ln2.T_ready, NC_)
                    pe.wait_ge(merged_copied, 1)
                pe.wait_ge(conv_silu, (c + 1) * ND)
                if c >= 2:
                    pe.wait_ge(full_copied, 2 * (c - 1))
                for d in range(ND):
                    last = nc.tensor.matmul(core.ps[0:96, c % 2, :], w["x_bc"][:, d, :], xs[d][:, c * CH:(c + 1) * CH],
                                            start=d == 0, stop=d == ND - 1)
                last.then_inc(xp_done, 1)
                for out in range(ND):
                    if c == NC_ - 1:
                        pe.wait_ge(positive, out + 1)
                    for d in range(ND):
                        last = nc.tensor.matmul(core.ps[:, DT_BANKS[c] + out, :], w_delta[:, d, out * P:(out + 1) * P],
                                                xs[d][:, c * CH:(c + 1) * CH], start=d == 0, stop=d == ND - 1)
                    last.then_inc(dt_done, 1)

            ln2.tensor(pe, lambda c: project_in(0) if c == 0 else None)
            for c in range(1, NC_):
                project_in(c)
            for c in range(NC_):
                if c == 1:
                    pe.wait_ge(in_used, NC_ * 2 * ND)
                project_x(c)
            pe.wait_ge(bc_ready, NC_)
            core.loaded(pe, "pick")
            pe.wait_ge(positive, ND * NC_)

            def spread_b(j, s, chunk):
                if not (isinstance(j, int) and s < B_RING):
                    pe.wait_ge(b_copied, j * DS + max(s - B_RING + 1, 0))
                nc.tensor.matmul(core.ps[:, B_BANKS[s % B_RING], :], pick[:, s, :], chunk,
                                 start=True, stop=True).then_inc(b_spread, 1)

            def spread_c(j, s, chunk):
                if not (isinstance(j, int) and s < 2):
                    pe.wait_ge(hc_done, j * UNITS + (s - 1) * ND)
                nc.tensor.matmul(core.ps[:, C_BANK + s % 2, :], pick[:, DS + s, :], chunk,
                                 start=True, stop=True).then_inc(c_spread, 1)

            def add_up(j, s):
                for d in range(ND):
                    pe.wait_ge(hc_done, j * UNITS + (s * ND + d + 1))
                    nc.tensor.matmul(core.ps[:, Y_BANK + d, :], core.ident[:], hc[d][:],
                                     start=s == 0, stop=s == DS - 1).then_inc(summed, 1)

            def project_out(after):
                pe.wait_ge(y_done, after * (2 * ND))
                for k in range(TPC):
                    for d in range(ND):
                        last = nc.tensor.matmul(core.ps[:, O_BANK, k * P:(k + 1) * P], yT[d][:, k * P:(k + 1) * P],
                                                w["out_proj"][:, d, :], start=d == 0, stop=d == ND - 1)
                last.then_inc(out_done, 1)

            def body(j, chunk):
                for s in range(B_RING):
                    spread_b(j, s, chunk)
                spread_c(j, 0, chunk)
                for s in range(DS):
                    if s + B_RING < DS:
                        spread_b(j, s + B_RING, chunk)
                    if s == 0 and not isinstance(j, int):
                        project_out(j)
                    if s:
                        spread_c(j, s, chunk)
                        add_up(j, s - 1)
                add_up(j, DS - 1)

            body(0, bc[:, 0:CH])
            with pe.Fori(1, NC_) as j:
                body(j, bc[:, bass.ds(j * CH, CH)])
            project_out(NC_)

        @block.scalar
        def _(act):
            line = core.act_line
            core.loaded(act, "norm_g", "norm_b")
            ln1.scalar(act)
            act.wait_ge(merged, 1)
            nc.scalar.copy(w_delta[:].rearrange("p d n -> p (d n)"), core.ps[:, DT_BANKS[0], :]).then_inc(merged_copied, 1)
            ln2.scalar(act)
            core.loaded(act, "log_A", "conv_b", "dt_b")

            def silu_x(c):
                for d in range(ND):
                    act.wait_ge(conv_done, (DCONV * c + DCONV - 1) * ND + d + 1)
                    cols = slice(c * CH, (c + 1) * CH)
                    nc.scalar.activation(xs[d][:, cols], delta[d][:, cols], ACT.Silu).then_inc(conv_silu, 1)

            def copy_bc(c):
                cols = slice(c * CH, (c + 1) * CH)
                act.wait_ge(xp_done, c + 1)
                nc.scalar.copy(bc[:, cols], core.ps[0:96, c % 2, :]).then_inc(full_copied, 1)
                if c:
                    act.wait_ge(cut_line, 3 * (c - 1) + 1)
                nc.scalar.copy(full, core.ps[0:96, c % 2, :]).then_inc(full_copied, 1)

            def take_abs(c):
                for d in range(ND):
                    act.wait_ge(dt_done, c * ND + d + 1)
                    nc.scalar.activation(soft[d][:, c * CH:(c + 1) * CH], core.ps[:, DT_BANKS[c] + d, :], ACT.Abs,
                                         bias=w["dt_b"][:, d:d + 1]).then_inc(absolute, 1)

            act.wait_ge(padded, ND)
            for c in range(NC_):
                for m in range(2 * ND):
                    act.wait_ge(in_done, c * 2 * ND + m + 1)
                    src = core.ps[:, 4 + m, :]
                    if m < ND:
                        ins = nc.scalar.copy(pre[m][:, PAD + c * CH:PAD + (c + 1) * CH], src)
                    else:
                        ins = nc.scalar.activation(zs[m - ND][:, c * CH:(c + 1) * CH], src, ACT.Silu)
                    ins.then_inc(in_used, 1)
            for c in range(NC_):
                silu_x(c)
                if c:
                    take_abs(c - 1)
                copy_bc(c)
            take_abs(NC_ - 1)
            parts = [soft[d][:, c * CH:(c + 1) * CH] for c in range(NC_) for d in range(ND)]
            for n, part in enumerate(parts):
                act.wait_ge(absolute, n + 1)
                nc.scalar.activation(part, part, ACT.Exp, scale=-1.0).then_inc(exp_done, 1)
            line.after(act, nc.scalar.activation(a_neg[:], w["log_A"][:], ACT.Exp))
            line.after(act, nc.scalar.mul(a_neg[:], a_neg[:], -1.0))
            for n, part in enumerate(parts):
                act.wait_ge(exp_done, n + 1)
                nc.scalar.activation(part, part, ACT.Ln, bias=1.0).then_inc(log_done, 1)

            def copy_b(j, s):
                act.wait_ge(b_spread, j * DS + (s + 1))
                if not (isinstance(j, int) and s < B_RING):
                    act.wait_ge(dbx_done, j * UNITS + max(s - B_RING + 1, 0) * ND)
                nc.scalar.copy(b_rows[s % B_RING][:], core.ps[:, B_BANKS[s % B_RING], :]).then_inc(b_copied, 1)

            def body(j):
                copy_b(j, 0)
                copy_b(j, 1)
                act.wait_ge(chunk_ready, j * 2 * ND + 2 * ND)
                for s in range(DS):
                    for d in range(ND):
                        u = s * ND + d
                        if not (isinstance(j, int) and u < RING):
                            act.wait_ge(scanned, j * UNITS + (u - RING + 1))
                        nc.scalar.activation(da[u % RING][:], delta_c[d][:], ACT.Exp,
                                             scale=a_neg[:, d, s:s + 1]).then_inc(da_done, 1)
                    if s + 2 < DS:
                        copy_b(j, s + 2)

            body(0)
            with act.Fori(1, NC_) as j:
                body(j)

        @block.vector
        def _(dve):
            line = core.dve_line
            ln1.vector(dve)
            dve.wait_ge(ln1.normed, NT)
            ln2.vector(dve)
            core.loaded(dve, "conv_w", "conv_b", "Dp", "dt_b")

            def convolve(c):
                dve.wait_ge(in_used, (c + 1) * 2 * ND)
                cols = slice(c * CH, (c + 1) * CH)
                for d in range(ND):
                    nc.vector.tensor_scalar(delta[d][:, cols], pre[d][:, cols], w["conv_w"][:, d, 0:1],
                                            w["conv_b"][:, d:d + 1], ALU.mult, ALU.add).then_inc(conv_done, 1)
                for k in range(1, DCONV):
                    for d in range(ND):
                        dve.wait_ge(conv_done, (DCONV * c + k - 1) * ND + d + 1)
                        nc.vector.scalar_tensor_tensor(out=delta[d][:, cols], in0=pre[d][:, c * CH + k:c * CH + k + CH],
                                                       scalar=w["conv_w"][:, d, k:k + 1], in1=delta[d][:, cols],
                                                       op0=ALU.mult, op1=ALU.add).then_inc(conv_done, 1)

            def take_positive(c):
                for d in range(ND):
                    dve.wait_ge(absolute, c * ND + d + 1)
                    nc.vector.tensor_scalar(delta[d][:, c * CH:(c + 1) * CH], core.ps[:, DT_BANKS[c] + d, :],
                                            w["dt_b"][:, d:d + 1], 0.0, ALU.add, ALU.max).then_inc(positive, 1)

            for c in range(NC_):
                convolve(c)
                if c >= 2:
                    take_positive(c - 2)
            take_positive(NC_ - 2)
            take_positive(NC_ - 1)
            dve.wait_ge(positive, ND * NC_)

            def add_log(c):
                for d in range(ND):
                    cols = slice(c * CH, (c + 1) * CH)
                    dve.wait_ge(log_done, c * ND + d + 1)
                    nc.vector.tensor_tensor(delta[d][:, cols], delta[d][:, cols], soft[d][:, cols],
                                            ALU.add).then_inc(delta_done, 1)
                dve.wait_ge(delta_done, (c + 1) * ND)

            dve.wait_ge(padded, ND + 1)
            dve.wait_ge(residual, NT)

            def finish(after, cols):
                dve.wait_ge(summed, after * UNITS)
                for d in range(ND):
                    nc.vector.scalar_tensor_tensor(out=yT[d][:], in0=xs[d][:, cols],
                                                   scalar=w["Dp"][:, d:d + 1], in1=core.ps[:, Y_BANK + d, :],
                                                   op0=ALU.mult, op1=ALU.add).then_inc(y_done, 1)
                for d in range(ND):
                    dve.wait_ge(y_done, after * (2 * ND) + (d + 1 - 2 * ND))
                    nc.vector.tensor_tensor(yT[d][:], yT[d][:], zs[d][:, cols], ALU.mult).then_inc(y_done, 1)

            def add_out(after, tiles):
                dve.wait_ge(out_done, after)
                xc = core.x[:, tiles, :].rearrange("p t d -> p (t d)")
                nc.vector.tensor_tensor(xc, xc, core.ps[:, O_BANK, :], ALU.add).then_inc(x_added, 1)
                dve.wait_ge(x_added, after)

            def body(j):
                cols = bass.ds(j * CH, CH)
                if isinstance(j, int):
                    add_log(0)
                for d in range(ND):
                    nc.vector.tensor_copy(delta_c[d][:], delta[d][:, cols]).then_inc(chunk_ready, 1)
                    nc.vector.tensor_tensor(dx_c[d][:], delta[d][:, cols], xs[d][:, cols], ALU.mult).then_inc(chunk_ready, 1)
                if isinstance(j, int):
                    for c in range(1, NC_):
                        add_log(c)
                else:
                    finish(j, bass.ds(j * CH + (-CH), CH))
                for s in range(DS):
                    for d in range(ND):
                        u = s * ND + d
                        dve.wait_ge(da_done, j * UNITS + (u + 1))
                        dve.wait_ge(dbx_done, j * UNITS + (u + 1))
                        if not (isinstance(j, int) and u < 2):
                            dve.wait_ge(hc_done, j * UNITS + (u - 1))
                            dve.wait_ge(saved, j * DS + s)
                        nc.vector.tensor_tensor_scan(out=h[:, d, :], data0=da[u % RING][:], data1=dbx[u % RING][:],
                                                     initial=state[:, s, d:d + 1], op0=ALU.mult,
                                                     op1=ALU.add).then_inc(scanned, 1)
                    dve.wait_ge(c_spread, j * DS + (s + 1))
                    for d in range(ND):
                        u = s * ND + d
                        dve.wait_ge(scanned, j * UNITS + (u + 1))
                        if not (isinstance(j, int) and u < 2):
                            dve.wait_ge(summed, j * UNITS + (u - 1))
                        nc.vector.tensor_tensor(hc[d][:], h[:, d, :], core.ps[:, C_BANK + s % 2, :],
                                                ALU.mult).then_inc(hc_done, 1)
                        if d == 0:
                            dve.wait_ge(scanned, j * UNITS + (s + 1) * ND)
                            nc.vector.tensor_copy(state[:, s, :], h[:, :, CH - 1]).then_inc(saved, 1)
                    if s == 2 and not isinstance(j, int):
                        add_out(j, bass.ds(j * TPC + (-TPC), TPC))

            body(0)
            with dve.Fori(1, NC_) as j:
                body(j)
            finish(NC_, slice(T - CH, T))
            add_out(NC_, slice(NT - TPC, NT))


def linear_attention(core):
    nc, w = core.nc, core.w
    SCALE = float(HD) ** -0.5 / P
    with ExitStack() as ctx:
        def sb(name, shape, dt=F32):
            return ctx.enter_context(nc.sbuf_tensor(f"l_{name}", shape, dt))

        ln = LayerNorm(core, ctx, "ln_l", core.x, core.xn, core.xnT)
        xnT = core.xnT
        keT = sb("keT", [P, T])
        k_tok = sb("k_tok", [P, NT, P])
        v_tok = sb("v_tok", [P, NT, P])
        q_tok = sb("q_tok", [P, NT, P])
        qT = sb("qT", [P, T])
        k_max = sb("k_max", [P, 1])
        k_sum = sb("k_sum", [P, 1])
        q_max = sb("q_max", [P, NT])
        q_sum = sb("q_sum", [P, NT])
        ctxT = sb("ctxT", [P, P])
        mixed = sb("mixed", [P, P])

        k_done = core.sem("l_k")
        kmax_done = core.sem("l_kmax")
        k_exp = core.sem("l_kexp")
        qv_done = core.sem("l_qv")
        v_copied = core.sem("l_v_copied")
        q_shifted = core.sem("l_q_shifted")
        q_exp = core.sem("l_q_exp")
        turned = core.sem("l_turned")
        k_copied = core.sem("l_k_copied")
        q_copied = core.sem("l_q_copied")
        ctx_done = core.sem("l_ctx")
        ctx_copied = core.sem("l_ctx_copied")
        mix_done = core.sem("l_mix")
        mixed_ready = core.sem("l_mixed")
        out_done = core.sem("l_out")
        added = core.sem("l_added")
        bias_added = core.sem("l_bias")
        block = ctx.enter_context(nc.Block())

        @block.gpsimd
        def _(pool):
            core.loaded(pool, "bo")
            pool.wait_ge(ln.normed, NT)
            for t in range(NT):
                nc.gpsimd.tensor_tensor(core.x[:, t, :], core.x[:, t, :], w["bo"][:], ALU.add).then_inc(bias_added, 1)

        @block.tensor
        def _(pe):
            ln.tensor(pe)
            core.loaded(pe, "Wk1", "Wq1", "Wv1", "Wo1")
            for c in range(NC_):
                pe.wait_ge(ln.T_ready, c + 1)
                last = nc.tensor.matmul(core.ps[:, 2 + c, :], w["Wk1"][:], xnT[:, c * CH:(c + 1) * CH],
                                        start=True, stop=True)
            last.then_inc(k_done, 1)
            for g in range(NC_):
                for i, name in enumerate(("Wq1", "Wv1")):
                    if g:
                        pe.wait_ge(q_shifted if i == 0 else v_copied, g)
                    for k in range(TPC):
                        last = nc.tensor.matmul(core.ps[:, 6 + i, k * P:(k + 1) * P], tile_of(xnT, g * TPC + k),
                                                w[name][:], start=True, stop=True)
                    last.then_inc(qv_done, 1)
            for g in range(NC_):
                pe.wait_ge(k_exp, 1)
                if g >= 2:
                    pe.wait_ge(k_copied, g - 1)
                for k in range(TPC):
                    last = nc.tensor.transpose(core.ps[:, g % 2, k * P:(k + 1) * P], tile_of(keT, g * TPC + k),
                                               core.ident[:])
                last.then_inc(turned, 1)
            for g in range(NC_):
                pe.wait_ge(q_exp, g + 1)
                pe.wait_ge(k_copied, min(NC_, g + 3))
                if g >= 2:
                    pe.wait_ge(q_copied, g - 1)
                for k in range(TPC):
                    last = nc.tensor.transpose(core.ps[:, g % 2, k * P:(k + 1) * P], q_tok[:, g * TPC + k, :],
                                               core.ident[:])
                last.then_inc(turned, 1)
            pe.wait_ge(q_shifted, NC_)
            pe.wait_ge(v_copied, NC_)
            pe.wait_ge(k_copied, NC_)
            for t in range(NT):
                last = nc.tensor.matmul(core.ps[:, 2, 0:P], v_tok[:, t, :], k_tok[:, t, :], start=t == 0, stop=t == NT - 1)
            last.then_inc(ctx_done, 1)
            pe.wait_ge(ctx_copied, 1)
            nc.tensor.matmul(core.ps[:, 3, 0:P], ctxT[:], w["Wo1"][:], start=True, stop=True).then_inc(mix_done, 1)
            pe.wait_ge(mixed_ready, 1)
            pe.wait_ge(q_copied, NC_)
            for g in range(NC_):
                for k in range(TPC):
                    last = nc.tensor.matmul(core.ps[:, 4 + g, k * P:(k + 1) * P], tile_of(qT, g * TPC + k), mixed[:],
                                            start=True, stop=True)
                last.then_inc(out_done, 1)

        @block.scalar
        def _(act):
            ln.scalar(act)
            act.wait_ge(kmax_done, 1)
            nc.scalar.activation(keT[:], core.ps[:, 2:6, :].rearrange("p b n -> p (b n)"), ACT.Exp, bias=k_max[:],
                                 accum_out=k_sum[:]).then_inc(k_exp, 1)
            for g in range(NC_):
                act.wait_ge(q_shifted, g + 1)
                qs = q_tok[:, g * TPC:(g + 1) * TPC, :]
                nc.scalar.activation(qs, qs, ACT.Exp).then_inc(q_exp, 1)
                act.wait_ge(qv_done, 2 * g + 2)
                nc.scalar.copy(v_tok[:, g * TPC:(g + 1) * TPC, :],
                               core.ps[:, 7, :].rearrange("p (k d) -> p k d", d=P)).then_inc(v_copied, 1)
            for g in range(NC_):
                act.wait_ge(turned, g + 1)
                nc.scalar.copy(k_tok[:, g * TPC:(g + 1) * TPC, :],
                               core.ps[:, g % 2, :].rearrange("p (k d) -> p k d", d=P)).then_inc(k_copied, 1)
            for g in range(NC_):
                act.wait_ge(turned, NC_ + g + 1)
                nc.scalar.copy(qT[:, g * CH:(g + 1) * CH], core.ps[:, g % 2, :]).then_inc(q_copied, 1)

        @block.vector
        def _(dve):
            line = core.dve_line
            ln.vector(dve)
            dve.wait_ge(k_done, 1)
            nc.vector.tensor_reduce(k_max[:], core.ps[:, 2:6, :], mybir.AxisListType.XY, ALU.max,
                                    negate=True).then_inc(kmax_done, 1)
            for g in range(NC_):
                dve.wait_ge(qv_done, 2 * g + 1)
                src = core.ps[:, 6, :].rearrange("p (k d) -> p k d", d=P)
                cols = slice(g * TPC, (g + 1) * TPC)
                line.after(dve, nc.vector.tensor_reduce(q_max[:, cols], src, AX_X, ALU.max))
                nc.vector.tensor_tensor(q_tok[:, cols, :], src, q_max[:, cols].unsqueeze(2).to_broadcast([P, TPC, P]),
                                        ALU.subtract).then_inc(q_shifted, 1)
            for g in range(NC_):
                dve.wait_ge(q_exp, g + 1)
                cols = slice(g * TPC, (g + 1) * TPC)
                line.mark(nc.vector.tensor_reduce(q_sum[:, cols], q_tok[:, cols, :], AX_X, ALU.add))
            line.wait(dve)
            line.after(dve, nc.vector.reciprocal(q_sum[:], q_sum[:]))
            dve.wait_ge(k_exp, 1)
            line.after(dve, nc.vector.reciprocal(k_max[:], k_sum[:]))
            dve.wait_ge(ctx_done, 1)
            nc.vector.tensor_copy(ctxT[:], core.ps[:, 2, 0:P]).then_inc(ctx_copied, 1)
            dve.wait_ge(mix_done, 1)
            nc.vector.tensor_scalar(mixed[:], core.ps[:, 3, 0:P], k_max[:], SCALE, ALU.mult,
                                    ALU.mult).then_inc(mixed_ready, 1)
            dve.wait_ge(bias_added, NT)
            for t in range(NT):
                if t % TPC == 0:
                    dve.wait_ge(out_done, t // TPC + 1)
                nc.vector.scalar_tensor_tensor(out=core.x[:, t, :],
                                               in0=core.ps[:, 4 + t // TPC, (t % TPC) * P:(t % TPC + 1) * P],
                                               scalar=q_sum[:, t:t + 1], in1=core.x[:, t, :],
                                               op0=ALU.mult, op1=ALU.add).then_inc(added, 1)
            dve.wait_ge(added, NT)


def experts_top4(core, tag):
    nc, w = core.nc, core.w
    PAIRS = E1 // 2
    UNITS = PAIRS + 1
    PG = E1 // GROUPS
    UP, DOWN, S_BANK = 0, 4, 7
    with ExitStack() as ctx:
        def sb(name, shape, dt=F32):
            return ctx.enter_context(nc.sbuf_tensor(f"{tag}_{name}", shape, dt))

        ln = LayerNorm(core, ctx, f"ln_{tag}", core.x, core.xn, core.xnT, banks=(4, 5))
        xnT = core.xnT
        scores = sb("scores", [P, NT, E1])
        choice = sb("choice", [P, NT, E1])
        tmp_scores = sb("tmp_scores", [P, NT, E1])
        top8 = sb("top8", [P, NT, 8])
        keep = sb("keep", [P, NT, E1])
        work = {n: sb(n, [P, NT, E1]) for n in ("gt", "eq", "nth", "sel")}
        work.update({n: sb(n, [P, NT]) for n in ("above", "room")})
        hi = sb("hi", [P, NT * GROUPS, 2])
        lo = sb("lo", [P, NT * GROUPS, 2])
        g_best = sb("g_best", [P, NT * GROUPS])
        g_next = sb("g_next", [P, NT * GROUPS])
        g_low = sb("g_low", [P, NT * GROUPS])
        g_beats = sb("g_beats", [P, NT * GROUPS, GROUPS])
        g_ties = sb("g_ties", [P, NT * GROUPS, GROUPS])
        g_rank = sb("g_rank", [P, NT * GROUPS])
        probs = sb("probs", [P, NT, E1 + 1])
        total = sb("total", [P, NT])
        gate = [sb(f"gate{i}", [P, CH]) for i in range(2)]
        hidden = [sb(f"hidden{i}", [P, CH]) for i in range(2)]

        scored = core.sem(f"{tag}_scored")
        tanh_done = core.sem(f"{tag}_tanh")
        up_done = core.sem(f"{tag}_up")
        gate_done = core.sem(f"{tag}_gate")
        hidden_done = core.sem(f"{tag}_hidden")
        down_done = core.sem(f"{tag}_down")
        added = core.sem(f"{tag}_added")
        block = ctx.enter_context(nc.Block())

        def experts(u):
            return 2 if u < PAIRS else 1
        ADDS = (2 * PAIRS + 1) * TPC

        @block.tensor
        def _(pe):
            core.loaded(pe, "gate1", "w_up1", "w_down1", "sh_up", "sh_down")

            def up(j, u, chunk):
                if not (isinstance(j, int) and u < 2):
                    pe.wait_ge(hidden_done, j * UNITS + (u - 1))
                for k in range(2):
                    weight = w["w_up1"][:, u, k, :] if u < PAIRS else w["sh_up"][:, k, :]
                    nc.tensor.matmul(core.ps[:, UP + 2 * (u % 2) + k, :], weight, chunk,
                                     start=True, stop=True).then_inc(up_done, 1)

            def down(j, u):
                pe.wait_ge(hidden_done, j * UNITS + (u + 1))
                if isinstance(j, int) and u == 1:
                    pe.wait_ge(tanh_done, 1)
                elif not isinstance(j, int) or u > 1:
                    pe.wait_ge(added, j * ADDS + max(u - 1, 0) * 2 * TPC)
                for k in range(TPC):
                    for i in range(experts(u)):
                        part = slice(I1 * i, I1 * (i + 1))
                        weight = w["w_down1"][part, u, :] if u < PAIRS else w["sh_down"][:]
                        last = nc.tensor.matmul(core.ps[:, DOWN + 2 * (u % 2) + i, k * P:(k + 1) * P],
                                                hidden[u % 2][part, k * P:(k + 1) * P], weight, start=True, stop=True)
                last.then_inc(down_done, 1)

            def body(j, chunk):
                for u in range(UNITS):
                    if u >= 2 or not isinstance(j, int):
                        up(j, u, chunk)
                    if u:
                        down(j, u - 1)
                down(j, UNITS - 1)

            def start(c):
                pe.wait_ge(ln.T_ready, c + 1)
                for t in range(c * TPC, (c + 1) * TPC):
                    last = nc.tensor.matmul(core.ps[:, S_BANK, t * E1:(t + 1) * E1], tile_of(xnT, t), w["gate1"][:],
                                            start=True, stop=True)
                if c == 0:
                    for u in range(2):
                        up(0, u, xnT[:, 0:CH])
                if c == NC_ - 1:
                    last.then_inc(scored, 1)

            ln.tensor(pe, start)
            body(0, xnT[:, 0:CH])
            with pe.Fori(1, NC_) as j:
                body(j, xnT[:, bass.ds(j * CH, CH)])

        @block.scalar
        def _(act):
            def silu(j, units):
                for u in units:
                    act.wait_ge(up_done, j * (2 * UNITS) + (2 * u + 1))
                    if not (isinstance(j, int) and u < 2):
                        act.wait_ge(hidden_done, j * UNITS + (u - 1))
                    nc.scalar.activation(gate[u % 2][:], core.ps[:, UP + 2 * (u % 2), :],
                                         ACT.Silu).then_inc(gate_done, 1)

            ln.scalar(act)
            act.wait_ge(scored, 1)
            nc.scalar.activation(scores[:], core.ps[:, S_BANK, 0:NT * E1].rearrange("p (t e) -> p t e", e=E1),
                                 ACT.Tanh, scale=0.5).then_inc(tanh_done, 1)

            silu(0, range(UNITS))
            with act.Fori(1, NC_) as j:
                silu(j, range(UNITS))

        @block.vector
        def _(dve):
            line = core.dve_line

            def multiply(j, u):
                dve.wait_ge(gate_done, j * UNITS + (u + 1))
                dve.wait_ge(up_done, j * (2 * UNITS) + (2 * u + 2))
                if not (isinstance(j, int) and u < 2):
                    dve.wait_ge(down_done, j * UNITS + (u - 1))
                nc.vector.tensor_tensor(hidden[u % 2][:], gate[u % 2][:],
                                        core.ps[:, UP + 2 * (u % 2) + 1, :], ALU.mult).then_inc(hidden_done, 1)

            line.after(dve, nc.vector.memset(keep[:], 1.0))
            line.mark(nc.vector.memset(keep[:, :, 0:1], 0.0))
            line.mark(nc.vector.memset(probs[:, :, E1:E1 + 1], 1.0))
            ln.vector(dve)
            core.loaded(dve, "e_bias", "earlier")
            dve.wait_ge(tanh_done, 1)
            line.after(dve, nc.vector.tensor_scalar(scores[:], scores[:], 0.5, 0.5, ALU.mult, ALU.add))
            line.after(dve, nc.vector.tensor_tensor(choice[:], scores[:],
                                                    w["e_bias"][:].unsqueeze(1).to_broadcast([P, NT, E1]), ALU.add))
            quads = choice[:].rearrange("p t (g i k) -> p (t g) i k", g=GROUPS, k=2)
            line.mark(nc.vector.tensor_tensor(hi[:], quads[:, :, :, 0], quads[:, :, :, 1], ALU.max))
            line.after(dve, nc.vector.tensor_tensor(lo[:], quads[:, :, :, 0], quads[:, :, :, 1], ALU.min))
            line.mark(nc.vector.tensor_tensor(g_best[:], hi[:, :, 0], hi[:, :, 1], ALU.max))
            line.mark(nc.vector.tensor_tensor(g_next[:], hi[:, :, 0], hi[:, :, 1], ALU.min))
            line.after(dve, nc.vector.tensor_tensor(g_low[:], lo[:, :, 0], lo[:, :, 1], ALU.max))
            line.after(dve, nc.vector.tensor_tensor(g_next[:], g_next[:], g_low[:], ALU.max))
            line.after(dve, nc.vector.tensor_tensor(g_best[:], g_best[:], g_next[:], ALU.add))
            mine = g_best[:].unsqueeze(2).to_broadcast([P, NT * GROUPS, GROUPS])
            for g in range(GROUPS):
                of_group = g_best[:].rearrange("p (t g) -> p t g", g=GROUPS)
                mine = of_group[:, :, g:g + 1].to_broadcast([P, NT, GROUPS])
                beats = g_beats[:].rearrange("p (t g) h -> p t g h", g=GROUPS)[:, :, g, :]
                ties = g_ties[:].rearrange("p (t g) h -> p t g h", g=GROUPS)[:, :, g, :]
                line.mark(nc.vector.tensor_tensor(beats, of_group, mine, ALU.is_gt))
                line.mark(nc.vector.tensor_tensor(ties, of_group, mine, ALU.is_equal))
            line.wait(dve)
            earlier = w["earlier"][:].unsqueeze(1).to_broadcast([P, NT, GROUPS * GROUPS])
            ties = g_ties[:].rearrange("p (t g) h -> p t (g h)", g=GROUPS)
            line.after(dve, nc.vector.tensor_tensor(ties, ties, earlier, ALU.mult))
            line.after(dve, nc.vector.tensor_tensor(g_beats[:], g_beats[:], g_ties[:], ALU.add))
            line.after(dve, nc.vector.tensor_reduce(g_rank[:], g_beats[:], AX_X, ALU.add))
            line.after(dve, nc.vector.tensor_scalar(g_rank[:], g_rank[:], float(TOPG), None, ALU.is_lt))
            line.after(dve, nc.vector.tensor_tensor(
                tmp_scores[:].rearrange("p t (g k) -> p (t g) k", g=GROUPS),
                choice[:].rearrange("p t (g k) -> p (t g) k", g=GROUPS),
                g_rank[:].unsqueeze(2).to_broadcast([P, NT * GROUPS, PG]), ALU.mult))
            for u in range(2):
                multiply(0, u)
            for t in range(NT):
                line.mark(nc.vector.max(top8[:, t, :], tmp_scores[:, t, :]))
            line.wait(dve)
            pick_top(core, dve, tmp_scores[:], top8, keep, work, TOP1)
            line.after(dve, nc.vector.tensor_tensor(work["gt"][:], scores[:], work["sel"][:], ALU.mult))
            line.after(dve, nc.vector.tensor_reduce(total[:], work["gt"][:], AX_X, ALU.add))
            line.after(dve, nc.vector.tensor_scalar(total[:], total[:], 1e-20, None, ALU.add))
            line.after(dve, nc.vector.reciprocal(total[:], total[:]))
            line.after(dve, nc.vector.tensor_scalar(total[:], total[:], SCALING, None, ALU.mult))
            line.after(dve, nc.vector.tensor_tensor(probs[:, :, 0:E1], work["gt"][:],
                                                    total[:].unsqueeze(2).to_broadcast([P, NT, E1]), ALU.mult))

            def add(j, u):
                for i in range(experts(u)):
                    e = 2 * u + i
                    if i == 0:
                        dve.wait_ge(down_done, j * UNITS + (u + 1))
                    for k in range(TPC):
                        if e:
                            dve.wait_ge(added, j * ADDS + ((e - 1) * TPC + k + 1))
                        t = j * TPC + k
                        xs = core.x[:, bass.ds(t, 1), :].rearrange("p t d -> p (t d)")
                        nc.vector.scalar_tensor_tensor(out=xs, in0=core.ps[:, DOWN + 2 * (u % 2) + i, k * P:(k + 1) * P],
                                                       scalar=probs[:, bass.ds(t, 1), e], in1=xs,
                                                       op0=ALU.mult, op1=ALU.add).then_inc(added, 1)

            def body(j):
                for u in range(UNITS):
                    if u >= 2 or not isinstance(j, int):
                        multiply(j, u)
                    if u:
                        add(j, u - 1)
                add(j, UNITS - 1)

            body(0)
            with dve.Fori(1, NC_) as j:
                body(j)
            dve.wait_ge(added, NC_ * ADDS)


def gated_linear_attention(core):
    nc, w = core.nc, core.w
    with ExitStack() as ctx:
        def sb(name, shape, dt=F32):
            return ctx.enter_context(nc.sbuf_tensor(f"g_{name}", shape, dt))

        ln = LayerNorm(core, ctx, "ln_g", core.x, core.xn, core.xnT)
        xnT = core.xnT
        qT = sb("qT", [P, T])
        fT = sb("fT", [P, T])
        kT = sb("kT", [P, T])
        suf = sb("suf", [P, T])
        pre = fT
        qd = [sb(f"qd{i}", [P, T]) for i in range(2)]
        kd = [sb(f"kd{i}", [P, T]) for i in range(2)]
        v = sb("v", [P, NT, P])
        gate = sb("gate", [P, NT, P])
        att = sb("att", [P, NT, P])
        g1T = att[:].rearrange("p n t -> p (n t)")
        k_tok = sb("k_tok", [P, NT, P])
        states = sb("states", [P, NT, P])
        o_gated, o_normed, o_T = core.xn, k_tok, kd[0]
        ln_o = LayerNorm(core, ctx, "ln_go", o_gated, o_normed, o_T[:], w["ln_w"][:], None)

        proj = core.sem("g_proj")
        proj_used = core.sem("g_proj_used")
        f_ready = core.sem("g_f")
        k_decayed = core.sem("g_k_decayed")
        q_decayed = core.sem("g_q_decayed")
        suf_widened = core.sem("g_suf_widened")
        pre_widened = core.sem("g_pre_widened")
        level_done = core.sem("g_level_done")
        level_taken = core.sem("g_level_taken")
        turned = core.sem("g_turned")
        k_copied = core.sem("g_k_copied")
        u_done = core.sem("g_u")
        state_done = core.sem("g_state")
        o_done = core.sem("g_o")
        o_taken = core.sem("g_o_taken")
        out_done = core.sem("g_out")
        added = core.sem("g_added")
        block = ctx.enter_context(nc.Block())
        NSTEP = LEVELS + 1

        def halves(a, step):
            return a[:].rearrange("p (n i h) -> p n i h", i=2, h=1 << (step - 1))

        def block_ends(step, side):
            half = 1 << (step - 1)
            return halves(pre, step)[:, :, side, half - 1:half].to_broadcast([P, T // (2 * half), half])

        @block.gpsimd
        def _(pool):
            for step in range(1, NSTEP):
                if step >= 3:
                    pool.wait_ge(level_done, (step - 1) * NC_)
                    pool.wait_ge(pre_widened, step - 1)
                    nc.gpsimd.tensor_tensor(halves(qd[step % 2], step)[:, :, 1, :], halves(qT, step)[:, :, 1, :],
                                            halves(pre, step)[:, :, 1, :], ALU.mult).then_inc(q_decayed, 1)
                pool.wait_ge(q_decayed, step)
                pool.wait_ge(suf_widened, step)
                right = halves(pre, step)[:, :, 1, :]
                nc.gpsimd.tensor_tensor(right, right, block_ends(step, 0), ALU.mult).then_inc(pre_widened, 1)

        @block.tensor
        def _(pe):
            ln.tensor(pe)
            core.loaded(pe, "W_in", "W_g1", "W_g2", "W_out")
            n = 0
            for name in ("lg", "q", "g1", "v", "gate"):
                for c in range(NC_):
                    if n >= 4:
                        pe.wait_ge(proj_used, n - 3)
                    if n < NC_:
                        pe.wait_ge(ln.T_ready, c + 1)
                    if name == "gate":
                        pe.wait_ge(proj_used, 3 * NC_)
                    bank = core.ps[:, 4 + n % 4, :]
                    if name in ("lg", "g1", "q"):
                        weight = {"lg": w["W_in"][:, 2 * P:3 * P], "q": w["W_in"][:, P:2 * P], "g1": w["W_g1"][:]}[name]
                        last = nc.tensor.matmul(bank, weight, xnT[:, c * CH:(c + 1) * CH], start=True, stop=True)
                    else:
                        src, weight = (xnT, w["W_in"][:, 0:P]) if name == "v" else (g1T, w["W_g2"][:])
                        for k in range(TPC):
                            last = nc.tensor.matmul(bank[:, k * P:(k + 1) * P], tile_of(src, c * TPC + k), weight,
                                                    start=True, stop=True)
                    last.then_inc(proj, 1)
                    n += 1
            pe.wait_ge(proj_used, n)
            pe.wait_ge(f_ready, 1)
            for step in range(NSTEP):
                if step:
                    pe.wait_ge(k_decayed, step)
                    pe.wait_ge(q_decayed, step)
                kk, qq = (kT, qT) if step == 0 else (kd[step % 2], qd[step % 2])
                for g in range(NC_):
                    if step >= 2:
                        pe.wait_ge(level_taken, (step - 2) * NC_ + g + 1)
                    for k in range(TPC):
                        t = g * TPC + k
                        last = nc.tensor.matmul(core.ps[:, 4 * (step % 2) + g, k * P:(k + 1) * P], tile_of(kk, t),
                                                tile_of(qq, t), start=True, stop=True)
                    last.then_inc(level_done, 1)
            pe.wait_ge(k_decayed, NSTEP)
            for g in range(NC_):
                pe.wait_ge(level_taken, (NSTEP - 2) * NC_ + g + 1)
                for k in range(TPC):
                    last = nc.tensor.transpose(core.ps[:, g, k * P:(k + 1) * P], tile_of(kd[NSTEP % 2], g * TPC + k),
                                               core.ident[:])
                last.then_inc(turned, 1)
            for g in range(NC_):
                pe.wait_ge(k_copied, g + 1)
                pe.wait_ge(level_taken, (NSTEP - 1) * NC_ + g + 1)
                for k in range(TPC):
                    t = g * TPC + k
                    last = nc.tensor.matmul(core.ps[:, 4 + g, k * P:(k + 1) * P], k_tok[:, t, :], v[:, t, :],
                                            start=True, stop=True)
                last.then_inc(u_done, 1)
            pe.wait_ge(k_copied, NC_)
            for g in range(NC_):
                for k in range(TPC):
                    t = g * TPC + k
                    bank = core.ps[:, g, k * P:(k + 1) * P]
                    last = nc.tensor.matmul(bank, att[:, t, :], v[:, t, :], start=True, stop=t == 0)
                    if t:
                        if t == 1:
                            pe.wait_ge(q_decayed, NSTEP)
                        pe.wait_ge(state_done, t)
                        last = nc.tensor.matmul(bank, tile_of(qd[NSTEP % 2], t), states[:, t, :], start=False, stop=True)
                last.then_inc(o_done, 1)
            pe.wait_ge(o_taken, NC_)
            ln_o.tensor(pe)
            pe.wait_ge(state_done, NT - 1)
            for g in range(NC_):
                pe.wait_ge(ln_o.T_ready, g + 1)
                for k in range(TPC):
                    last = nc.tensor.matmul(core.ps[:, 4 + g, k * P:(k + 1) * P], tile_of(o_T, g * TPC + k),
                                            w["W_out"][:], start=True, stop=True)
                last.then_inc(out_done, 1)

        @block.scalar
        def _(act):
            core.loaded(act, "ln_w")
            ln.scalar(act)
            n = 0
            for name in ("lg", "q", "g1", "v", "gate"):
                for c in range(NC_):
                    act.wait_ge(proj, n + 1)
                    src = core.ps[:, 4 + n % 4, :]
                    cols = slice(c * CH, (c + 1) * CH)
                    by_tile = src.rearrange("p (k d) -> p k d", d=P)
                    if name == "lg":
                        ins = nc.scalar.activation(fT[:, cols], src, ACT.Tanh, scale=0.5)
                    elif name == "g1":
                        ins = nc.scalar.copy(g1T[:, cols], src)
                    elif name == "v":
                        ins = nc.scalar.copy(v[:, c * TPC:(c + 1) * TPC, :], by_tile)
                    elif name == "gate":
                        ins = nc.scalar.activation(gate[:, c * TPC:(c + 1) * TPC, :], by_tile, ACT.Tanh, scale=0.5)
                    else:
                        ins = nc.scalar.activation(qT[:, cols], src, ACT.Silu)
                    ins.then_inc(proj_used, 1)
                    n += 1
            for g in range(NC_):
                act.wait_ge(turned, g + 1)
                nc.scalar.copy(k_tok[:, g * TPC:(g + 1) * TPC, :],
                               core.ps[:, g, :].rearrange("p (k d) -> p k d", d=P)).then_inc(k_copied, 1)
            ln_o.scalar(act)

        @block.vector
        def _(dve):
            line = core.dve_line
            core.loaded(dve, "masks")
            ln.vector(dve)
            dve.wait_ge(proj_used, NC_)
            nc.vector.tensor_scalar(kT[:], fT[:], -0.5, 0.5, ALU.mult, ALU.add).then_inc(f_ready, 1)
            dve.wait_ge(f_ready, 1)
            line.after(dve, nc.vector.tensor_scalar(fT[:], fT[:], 0.5, 0.5, ALU.mult, ALU.add))
            line.after(dve, nc.vector.memset(suf[:], 1.0))
            dve.wait_ge(proj_used, 2 * NC_)

            def take(step):
                for g in range(NC_):
                    dve.wait_ge(level_done, step * NC_ + g + 1)
                    src = core.ps[:, 4 * (step % 2) + g, :].rearrange("p (k d) -> p k d", d=P)
                    dst = att[:, g * TPC:(g + 1) * TPC, :]
                    if step == 0:
                        ins = nc.vector.tensor_tensor(dst, src, core.ident[:].unsqueeze(1).to_broadcast([P, TPC, P]),
                                                      ALU.mult)
                    else:
                        dve.wait_ge(level_taken, (step - 1) * NC_ + g + 1)
                        ins = nc.vector.copy_predicated(
                            dst, w["masks"][:, step - 1, :].unsqueeze(1).to_broadcast([P, TPC, P]), src)
                    ins.then_inc(level_taken, 1)

            for step in range(1, NSTEP):
                k_out = kd[step % 2]
                if step >= 2:
                    dve.wait_ge(suf_widened, step - 1)
                if step <= 2:
                    nc.vector.tensor_tensor(k_out[:], kT[:], suf[:], ALU.mult).then_inc(k_decayed, 1)
                    if step == 2:
                        dve.wait_ge(pre_widened, 1)
                    nc.vector.tensor_tensor(qd[step % 2][:], qT[:], pre[:], ALU.mult).then_inc(q_decayed, 1)
                else:
                    dve.wait_ge(level_done, (step - 1) * NC_)
                    nc.vector.tensor_tensor(halves(k_out, step)[:, :, 0, :], halves(kT, step)[:, :, 0, :],
                                            halves(suf, step)[:, :, 0, :], ALU.mult).then_inc(k_decayed, 1)
                dve.wait_ge(k_decayed, step)
                if step >= 2:
                    dve.wait_ge(pre_widened, step - 1)
                left = halves(suf, step)[:, :, 0, :]
                nc.vector.tensor_tensor(left, left, block_ends(step, 1), ALU.mult).then_inc(suf_widened, 1)
                take(step - 1)
            dve.wait_ge(level_done, (NSTEP - 1) * NC_)
            dve.wait_ge(suf_widened, LEVELS)
            nc.vector.tensor_tensor(kd[NSTEP % 2][:], kT[:], suf[:], ALU.mult).then_inc(k_decayed, 1)
            dve.wait_ge(pre_widened, LEVELS)
            nc.vector.tensor_tensor(qd[NSTEP % 2][:], qT[:], pre[:], ALU.mult).then_inc(q_decayed, 1)
            take(NSTEP - 1)
            dve.wait_ge(proj_used, 5 * NC_)
            line.after(dve, nc.vector.tensor_scalar(gate[:], gate[:], 0.5, 0.5, ALU.mult, ALU.add))
            for t in range(1, NT):
                if (t - 1) % TPC == 0:
                    dve.wait_ge(u_done, (t - 1) // TPC + 1)
                u = core.ps[:, 4 + (t - 1) // TPC, ((t - 1) % TPC) * P:((t - 1) % TPC + 1) * P]
                if t == 1:
                    ins = nc.vector.tensor_copy(states[:, t, :], u)
                else:
                    dve.wait_ge(state_done, t - 1)
                    ins = nc.vector.scalar_tensor_tensor(out=states[:, t, :], in0=states[:, t - 1, :],
                                                         scalar=pre[:, t * P - 1:t * P], in1=u,
                                                         op0=ALU.mult, op1=ALU.add)
                ins.then_inc(state_done, 1)
            for g in range(NC_):
                dve.wait_ge(o_done, g + 1)
                cols = slice(g * TPC, (g + 1) * TPC)
                nc.vector.tensor_tensor(o_gated[:, cols, :], core.ps[:, g, :].rearrange("p (k d) -> p k d", d=P),
                                        gate[:, cols, :], ALU.mult).then_inc(o_taken, 1)
            dve.wait_ge(o_taken, NC_)
            ln_o.vector(dve)
            for g in range(NC_):
                dve.wait_ge(out_done, g + 1)
                xc = core.x[:, g * TPC:(g + 1) * TPC, :]
                nc.vector.tensor_tensor(xc, xc, core.ps[:, 4 + g, :].rearrange("p (k d) -> p k d", d=P),
                                        ALU.add).then_inc(added, 1)
            dve.wait_ge(added, NC_)


WEIGHTS = {
    "Wq0": ("L0_attn_a_Wq", lambda a: a.T),
    "Wk0": ("L0_attn_a_Wk", lambda a: a.T),
    "Wv0": ("L0_attn_a_Wv", lambda a: a.T),
    "Wu0": ("L0_attn_a_Wu", lambda a: a.T),
    "bu": ("L0_attn_a_bu", lambda a: np.broadcast_to(a, (P, P))),
    "gate0": ("L0_ffn_gate_w", lambda a: a.T),
    "w12": ("L0_ffn_w12", lambda a: a.transpose(2, 0, 1)),
    "w3": ("L0_ffn_w3", lambda a: a.reshape(E0, P, H0 // P, P).transpose(3, 0, 2, 1)),
    "norm_g": ("L0_attn_b_norm_g", lambda a: a[:, None]),
    "norm_b": ("L0_attn_b_norm_b", lambda a: a[:, None]),
    "in_proj": ("L0_attn_b_in_proj_w", lambda a: a.T),
    "conv_w": ("L0_attn_b_conv_w", lambda a: a.reshape(ND, P, DCONV).transpose(1, 0, 2)),
    "conv_b": ("L0_attn_b_conv_b", lambda a: a.reshape(ND, P).T),
    "x_bc": ("L0_attn_b_x_proj_w", lambda a: np.tile(a[DTR:].T, (1, 3)).reshape(ND, P, 3 * 2 * DS).transpose(1, 0, 2)),
    "x_dt": ("L0_attn_b_x_proj_w", lambda a: a[:DTR]),
    "dt_proj": ("L0_attn_b_dt_proj_w", lambda a: a.T),
    "dt_b": ("L0_attn_b_dt_proj_b", lambda a: a.reshape(ND, P).T),
    "log_A": ("L0_attn_b_log_A", lambda a: a.reshape(ND, P, DS).transpose(1, 0, 2)),
    "Dp": ("L0_attn_b_Dp", lambda a: a.reshape(ND, P).T),
    "out_proj": ("L0_attn_b_out_proj_w", lambda a: a.T.reshape(ND, P, P).transpose(1, 0, 2)),
    "Wq1": ("L1_attn_a_Wq", lambda a: a),
    "Wk1": ("L1_attn_a_Wk", lambda a: a),
    "Wv1": ("L1_attn_a_Wv", lambda a: a),
    "Wo1": ("L1_attn_a_Wo", lambda a: a),
    "bo": ("L1_attn_a_bo", lambda a: np.broadcast_to(a, (P, P))),
    "gate1": ("L1_ffn_gate_w", lambda a: a.T),
    "e_bias": ("L1_ffn_e_bias", lambda a: np.broadcast_to(a, (P, E1))),
    "w_up1": (("L1_ffn_gate_proj", "L1_ffn_up_proj"),
              lambda g, u: np.stack([a.reshape(E1 // 2, 2 * I1, P) for a in (g, u)], 1).transpose(3, 0, 1, 2)),
    "w_down1": ("L1_ffn_down_proj", lambda a: a.reshape(E1 // 2, 2, P, I1).transpose(1, 3, 0, 2).reshape(2 * I1, E1 // 2, P)),
    "sh_up": (("L1_ffn_shared_gate_w", "L1_ffn_shared_up_w"), lambda g, u: np.pad(np.stack([g, u], 0), ((0, 0), (0, I1), (0, 0))).transpose(2, 0, 1)),
    "sh_down": ("L1_ffn_shared_down_w", lambda a: a.T),
    "W_in": ("L1_attn_b_W_in", lambda a: a.T),
    "W_out": ("L1_attn_b_W_out", lambda a: a.T),
    "W_g1": ("L1_attn_b_W_g1", lambda a: a.T),
    "W_g2": ("L1_attn_b_W_g2", lambda a: a.T),
    "ln_w": ("L1_attn_b_ln_w", lambda a: a[:, None]),
}


def constants():
    pick = np.zeros((96, 2 * DS, P), np.uint16)
    for s in range(2 * DS):
        pick[[s, 2 * DS + s, 4 * DS + s], s, :] = 0x3F80
    i = np.arange(P)
    masks = [(i[:, None] // (2 << n) == i // (2 << n)) & (i[:, None] // (1 << n) % 2 == 0) & (i // (1 << n) % 2 == 1)
             for n in range(LEVELS)]
    earlier = np.tril(np.ones((GROUPS, GROUPS), np.float32), -1)
    return {"pick": pick, "masks": np.stack(masks, 1).astype(np.int32),
            "earlier": np.broadcast_to(earlier.reshape(1, -1), (P, GROUPS * GROUPS))}


def stack(nc, x, out, weights, ident, stages):
    with ExitStack() as ctx:
        core = Core(nc, ctx)
        core.ps = ctx.enter_context(nc.psum_tensor("ps", [P, 8, CH], F32))
        core.x = core.sb("x_res", [P, NT, P])
        core.xn = core.sb("xn", [P, NT, P])
        core.xnT = core.sb("xnT", [P, T])
        core.ident = core.sb("ident", [P, P])
        core.one = core.sb("one", [P, 1])
        core.o_zeroed = core.sem("o_zeroed")
        x_loaded, out_stored = core.sem("x_loaded"), core.sem("out_stored")
        w_loaded = {}
        for name, ap in weights.items():
            core.w[name] = core.sb(f"w_{name}", list(ap.shape), ap.dtype)
            w_loaded[name] = core.sem(f"loaded_{name}")

        def loaded(eng, *names):
            for n in names:
                eng.wait_ge(w_loaded[n], 16)

        def load_weights(eng):
            for name, ap in weights.items():
                eng.dma_start(core.w[name][:], ap).then_inc(w_loaded[name], 16)

        core.loaded = loaded
        core.load_weights = load_weights
        with nc.Block() as block:
            @block.vector
            def _(dve):
                core.dve_line.after(dve, nc.vector.memset(core.one[:], 1.0))

            @block.sync
            def _(sp):
                sp.dma_start(core.ident[:], ident).then_inc(x_loaded, 16)
                sp.dma_start(core.x[:], x[0].rearrange("(t p) d -> p t d", p=P)).then_inc(x_loaded, 16)
                sp.wait_ge(x_loaded, 32)
        core.stage_sems = []
        for i, (build, *args) in enumerate(stages):
            if i == len(STAGES) // 2:
                core.clear_sems()
            build(core, *args)
        with nc.Block() as block:
            @block.sync
            def _(sp):
                sp.dma_start(out[0].rearrange("(t p) d -> p t d", p=P), core.x[:]).then_inc(out_stored, 16)
                sp.wait_ge(out_stored, 16)
                for name in weights:
                    sp.wait_ge(w_loaded[name], 16)


STAGES = ((softmax_attention,), (experts_top2, "e1"), (selective_scan,), (experts_top2, "e2"),
          (linear_attention,), (experts_top4, "m1"), (gated_linear_attention,), (experts_top4, "m2"))


def kernel(**inputs):
    import concourse.bacc as bacc
    from concourse.bass_utils import run_bass_kernel_spmd

    nc = bacc.Bacc("TRN2", target_bir_lowering=False, num_devices=1)
    arrays, aps = {}, {}

    def given(name, a):
        a = np.ascontiguousarray(a)
        arrays[name] = a
        return nc.dram_tensor(name, a.shape, mybir.dt.from_np(a.dtype), kind="ExternalInput").ap()

    x = given("x_dram", inputs["L0_attn_a_x"])
    ident = given("ident_dram", np.eye(P, dtype=np.float32))
    for name, (source, layout) in WEIGHTS.items():
        sources = (source,) if isinstance(source, str) else source
        aps[name] = given(f"{name}_dram", layout(*(np.asarray(inputs[n]) for n in sources)))
    for name, a in constants().items():
        aps[name] = given(f"{name}_dram", a)
    out = nc.dram_tensor("out_dram", (1, T, P), F32, kind="ExternalOutput").ap()
    stack(nc, x, out, aps, ident, STAGES)
    r = run_bass_kernel_spmd(nc, [arrays], core_ids=[0])
    return r.results[0]["out_dram"]
```
